# Optimizing a Trainium2 kernel written in Bass

```python
import numpy as np
import jax
import jax.numpy as jnp

def _softmax(x, axis=-1):
    return jax.nn.softmax(x, axis=axis)

def _gelu(x):
    return jax.nn.gelu(x, approximate=True)

def _silu(x):
    return jax.nn.silu(x)

def _sigmoid(x):
    return jax.nn.sigmoid(x)

def _layernorm(x, axis=-1, eps=1e-05):
    m = jnp.mean(x, axis=axis, keepdims=True)
    v = jnp.var(x, axis=axis, keepdims=True)
    return (x - m) / jnp.sqrt(v + eps)

def _scatter_add(tgt, idx, src, axis=0):
    return tgt.at[idx].add(src)

def _segment_sum(src, seg, n):
    return jax.ops.segment_sum(src, seg, n)
kernel_name = 'mk_xattn_ffn_d2_seqx_r8_f84955'

def setup_inputs(seed: int=0):
    np.random.seed(seed)
    _w = jnp.asarray

    def _rec_inputs():
        import jax
        import jax.numpy as jnp
        _rk = jax.random.key(seed)
        x = -0.0003929 + 0.9999 * jax.random.normal(jax.random.fold_in(_rk, 1), (8, 128, 128), jnp.float32)
        _lenS = 128 - jax.random.randint(jax.random.fold_in(_rk, 7), (8,), 0, max(1, 128 // 4) + 1, jnp.int32)
        _lenS2 = 128 - jax.random.randint(jax.random.fold_in(_rk, 8), (8,), 0, max(1, 128 // 4) + 1, jnp.int32)
        _ctx_768P = jax.random.normal(jax.random.fold_in(_rk, 11), (8, 16, 96), jnp.float32)
        _ctx_768c = jax.random.dirichlet(jax.random.fold_in(_rk, 511), 0.3 * jnp.ones((16,), jnp.float32), (8, 128))
        _ctx_768t = jnp.einsum('bsk,bkd->bsd', _ctx_768c, _ctx_768P)
        _ctx_768t = _ctx_768t * jax.lax.rsqrt(jnp.mean(jnp.square(_ctx_768t)) + 1e-12) * 0.953939
        ctx_768 = -7.36909e-05 + 0.999899 * (_ctx_768t + 0.3 * jax.random.normal(jax.random.fold_in(_rk, 611), (8, 128, 96), jnp.float32))
        return (x, ctx_768)
    x, ctx_768 = _rec_inputs()

    def _L0_xattn_setup():
        import jax, jax.numpy as jnp
        import numpy as np
        EPS = 1e-08
        key = jax.random.key(seed)
        kv, kt, k1, k2, k3, k4 = jax.random.split(key, 6)
        B, S = (16, 128)
        VD, TD, H = (128, 96, 64)
        visual_features = jax.random.normal(kv, (B, S, VD), dtype=jnp.float32)
        text_features = jax.random.normal(kt, (B, S, TD), dtype=jnp.float32)
        Wv = jax.random.normal(k1, (H, VD), dtype=jnp.float32) * (1.0 / np.sqrt(VD))
        bv = jax.random.normal(k2, (H,), dtype=jnp.float32) * 0.01
        Wt = jax.random.normal(k3, (H, TD), dtype=jnp.float32) * (1.0 / np.sqrt(TD))
        bt = jax.random.normal(k4, (H,), dtype=jnp.float32) * 0.01
        return {'visual_features': visual_features, 'text_features': text_features, 'Wv': Wv, 'bv': bv, 'Wt': Wt, 'bt': bt}
    _L0_xattn_all = _L0_xattn_setup()
    _L0_xattn_in = {k: v for k, v in _L0_xattn_all.items() if k in ('Wv', 'bv', 'Wt', 'bt')}
    del _L0_xattn_all

    def _L0_ffn_setup():
        import jax, jax.numpy as jnp
        import numpy as np
        BLOCK = 32
        W_BITS = 4
        ACT_BITS = 16

        def act_qdq(x):
            qmax = 2.0 ** (ACT_BITS - 1) - 1.0
            scale = jnp.maximum(jnp.max(jnp.abs(x)) / qmax, 1e-12)
            return jnp.clip(jnp.round(x / scale), -qmax - 1.0, qmax) * scale

        def fixed_qdq_u16(x):
            scale = 1.0 / 65536.0
            return jnp.clip(jnp.round(x / scale), 0.0, 65535.0) * scale

        def lpbq_dequant(w):
            O, I = w.shape
            qmax = 2.0 ** (W_BITS - 1) - 1.0
            wb = w.reshape(O, I // BLOCK, BLOCK)
            s = jnp.maximum(jnp.max(jnp.abs(wb), axis=-1, keepdims=True) / qmax, 1e-12)
            wq = jnp.clip(jnp.round(wb / s), -qmax - 1.0, qmax) * s
            return wq.reshape(O, I)
        key = jax.random.key(seed)
        k1, k2, k3, k4 = jax.random.split(key, 4)
        B, S, H, I = (2, 512, 128, 384)
        x = jax.random.normal(k1, (B, S, H), jnp.float32)
        w_gate = jax.random.normal(k2, (I, H), jnp.float32) * 0.02
        w_up = jax.random.normal(k3, (I, H), jnp.float32) * 0.02
        w_down = jax.random.normal(k4, (H, I), jnp.float32) * 0.02
        return {'x': x, 'w_gate': w_gate, 'w_up': w_up, 'w_down': w_down}
    _L0_ffn_all = _L0_ffn_setup()
    _L0_ffn_in = {k: v for k, v in _L0_ffn_all.items() if k in ('w_gate', 'w_up', 'w_down')}
    del _L0_ffn_all

    def _L1_xattn_setup():
        import jax, jax.numpy as jnp
        import numpy as np
        HEADS = 8
        DIM_HEAD = 128
        ATTN_MATRIX_SCALE = 1.5
        SCALE = DIM_HEAD ** (-0.5)

        def _split_heads(t):
            b, n, _ = t.shape
            t = t.reshape(b, n, HEADS, DIM_HEAD)
            return t.transpose(2, 0, 1, 3).reshape(HEADS, b * n, DIM_HEAD)
        key = jax.random.key(seed)
        ks = jax.random.split(key, 7)
        b, n, m = (2, 256, 256)
        qd, cd, inner = (128, 96, HEADS * DIM_HEAD)
        x = jax.random.normal(ks[0], (b, n, qd), dtype=jnp.float32)
        context = jax.random.normal(ks[1], (b, m, cd), dtype=jnp.float32)
        Wq = jax.random.normal(ks[2], (qd, inner), dtype=jnp.float32) * qd ** (-0.5)
        Wk = jax.random.normal(ks[3], (cd, inner), dtype=jnp.float32) * cd ** (-0.5)
        Wv = jax.random.normal(ks[4], (cd, inner), dtype=jnp.float32) * cd ** (-0.5)
        Wout = jax.random.normal(ks[5], (inner, qd), dtype=jnp.float32) * inner ** (-0.5)
        bout = jnp.zeros((qd,), dtype=jnp.float32)
        return {'x': x, 'context': context, 'Wq': Wq, 'Wk': Wk, 'Wv': Wv, 'Wout': Wout, 'bout': bout}
    _L1_xattn_all = _L1_xattn_setup()
    _L1_xattn_in = {k: v for k, v in _L1_xattn_all.items() if k in ('Wq', 'Wk', 'Wv', 'Wout', 'bout')}
    del _L1_xattn_all

    def _L1_ffn_setup():
        import jax, jax.numpy as jnp
        import numpy as np
        D_MODEL = 128
        FFN = 512
        N_EXPERTS = 8
        TOPK = 2
        B, L = (4, 256)

        def _moe(x, gate_w, gate_b, w1, b1, w2, b2):
            bs, l, d = x.shape
            T = bs * l
            xf = x.reshape(T, d)
            logits = xf @ gate_w + gate_b
            top_vals, top_idx = jax.lax.top_k(logits, TOPK)
            rows = jnp.arange(T)[:, None]
            sparse = jnp.full_like(logits, -jnp.inf).at[rows, top_idx].set(top_vals)
            gates = jax.nn.softmax(sparse, axis=-1)
            out = jnp.zeros_like(xf)
            for e in range(N_EXPERTS):
                h = jax.nn.gelu(xf @ w1[e] + b1[e], approximate=False)
                y = h @ w2[e] + b2[e]
                out = out + gates[:, e:e + 1] * y
            return out.reshape(bs, l, d)
        key = jax.random.key(seed)
        ks = jax.random.split(key, 8)
        s_in = 1.0 / np.sqrt(D_MODEL)
        s_ffn = 1.0 / np.sqrt(FFN)
        x = jax.random.normal(ks[0], (B, L, D_MODEL), dtype=jnp.float32)
        gate_w = jax.random.uniform(ks[1], (D_MODEL, N_EXPERTS), jnp.float32, -s_in, s_in)
        gate_b = jax.random.uniform(ks[2], (N_EXPERTS,), jnp.float32, -s_in, s_in)
        w1 = jax.random.uniform(ks[3], (N_EXPERTS, D_MODEL, FFN), jnp.float32, -s_in, s_in)
        b1 = jax.random.uniform(ks[4], (N_EXPERTS, FFN), jnp.float32, -s_in, s_in)
        w2 = jax.random.uniform(ks[5], (N_EXPERTS, FFN, D_MODEL), jnp.float32, -s_ffn, s_ffn)
        b2 = jax.random.uniform(ks[6], (N_EXPERTS, D_MODEL), jnp.float32, -s_ffn, s_ffn)
        return {'x': x, 'gate_w': gate_w, 'gate_b': gate_b, 'w1': w1, 'b1': b1, 'w2': w2, 'b2': b2}
    _L1_ffn_all = _L1_ffn_setup()
    _L1_ffn_in = {k: v for k, v in _L1_ffn_all.items() if k in ('gate_w', 'gate_b', 'w1', 'b1', 'w2', 'b2')}
    del _L1_ffn_all
    return {'x': x, 'ctx_768': ctx_768, 'L0_xattn_Wv': _L0_xattn_in['Wv'], 'L0_xattn_bv': _L0_xattn_in['bv'], 'L0_xattn_Wt': _L0_xattn_in['Wt'], 'L0_xattn_bt': _L0_xattn_in['bt'], 'L0_ffn_w_gate': _L0_ffn_in['w_gate'], 'L0_ffn_w_up': _L0_ffn_in['w_up'], 'L0_ffn_w_down': _L0_ffn_in['w_down'], 'L1_xattn_Wq': _L1_xattn_in['Wq'], 'L1_xattn_Wk': _L1_xattn_in['Wk'], 'L1_xattn_Wv': _L1_xattn_in['Wv'], 'L1_xattn_Wout': _L1_xattn_in['Wout'], 'L1_xattn_bout': _L1_xattn_in['bout'], 'L1_ffn_gate_w': _L1_ffn_in['gate_w'], 'L1_ffn_gate_b': _L1_ffn_in['gate_b'], 'L1_ffn_w1': _L1_ffn_in['w1'], 'L1_ffn_b1': _L1_ffn_in['b1'], 'L1_ffn_w2': _L1_ffn_in['w2'], 'L1_ffn_b2': _L1_ffn_in['b2']}

def reference(x, ctx_768, L0_xattn_Wv, L0_xattn_bv, L0_xattn_Wt, L0_xattn_bt, L0_ffn_w_gate, L0_ffn_w_up, L0_ffn_w_down, L1_xattn_Wq, L1_xattn_Wk, L1_xattn_Wv, L1_xattn_Wout, L1_xattn_bout, L1_ffn_gate_w, L1_ffn_gate_b, L1_ffn_w1, L1_ffn_b1, L1_ffn_w2, L1_ffn_b2):
    import jax
    import jax.numpy as jnp

    def _L0_xattn_ref(visual_features, text_features, Wv, bv, Wt, bt):
        import jax, jax.numpy as jnp
        import numpy as np
        EPS = 1e-08
        v = jnp.einsum('bsd,hd->bsh', visual_features, Wv) + bv
        t = jnp.einsum('bsd,hd->bsh', text_features, Wt) + bt
        dots = jnp.einsum('bih,bjh->bij', v, t)
        vn = jnp.linalg.norm(v, axis=-1)
        tn = jnp.linalg.norm(t, axis=-1)
        denom = jnp.maximum(vn[:, :, None] * tn[:, None, :], EPS)
        return dots / denom

    def _L0_ffn_ref(x, w_gate, w_up, w_down):
        import jax, jax.numpy as jnp
        import numpy as np
        BLOCK = 32
        W_BITS = 4
        ACT_BITS = 16

        def act_qdq(x):
            qmax = 2.0 ** (ACT_BITS - 1) - 1.0
            scale = jnp.maximum(jnp.max(jnp.abs(x)) / qmax, 1e-12)
            return jnp.clip(jnp.round(x / scale), -qmax - 1.0, qmax) * scale

        def fixed_qdq_u16(x):
            scale = 1.0 / 65536.0
            return jnp.clip(jnp.round(x / scale), 0.0, 65535.0) * scale

        def lpbq_dequant(w):
            O, I = w.shape
            qmax = 2.0 ** (W_BITS - 1) - 1.0
            wb = w.reshape(O, I // BLOCK, BLOCK)
            s = jnp.maximum(jnp.max(jnp.abs(wb), axis=-1, keepdims=True) / qmax, 1e-12)
            wq = jnp.clip(jnp.round(wb / s), -qmax - 1.0, qmax) * s
            return wq.reshape(O, I)
        x = act_qdq(x)
        up = act_qdq(x @ lpbq_dequant(w_up).T)
        gate = act_qdq(x @ lpbq_dequant(w_gate).T)
        sig = fixed_qdq_u16(jax.nn.sigmoid(gate))
        gate = act_qdq(gate * sig)
        o = act_qdq(gate * up)
        return o @ lpbq_dequant(w_down).T

    def _L1_xattn_ref(x, context, Wq, Wk, Wv, Wout, bout):
        import jax, jax.numpy as jnp
        import numpy as np
        HEADS = 8
        DIM_HEAD = 128
        ATTN_MATRIX_SCALE = 1.5
        SCALE = DIM_HEAD ** (-0.5)

        def _split_heads(t):
            b, n, _ = t.shape
            t = t.reshape(b, n, HEADS, DIM_HEAD)
            return t.transpose(2, 0, 1, 3).reshape(HEADS, b * n, DIM_HEAD)
        b, n, _ = x.shape
        qh = _split_heads(jnp.einsum('bnq,qi->bni', x, Wq))
        kh = _split_heads(jnp.einsum('bmc,ci->bmi', context, Wk))
        vh = _split_heads(jnp.einsum('bmc,ci->bmi', context, Wv))
        sim = jnp.einsum('hid,hjd->hij', qh, kh) * SCALE
        mean = jnp.mean(sim, axis=-1, keepdims=True)
        sim = (sim - mean) * ATTN_MATRIX_SCALE + mean
        attn = jax.nn.softmax(sim, axis=-1)
        out = jnp.einsum('hij,hjd->hid', attn, vh)
        out = out.reshape(HEADS, b, n, DIM_HEAD).transpose(1, 2, 0, 3)
        out = out.reshape(b, n, HEADS * DIM_HEAD)
        return jnp.einsum('bni,iq->bnq', out, Wout) + bout

    def _L1_ffn_ref(x, gate_w, gate_b, w1, b1, w2, b2):
        import jax, jax.numpy as jnp
        import numpy as np
        D_MODEL = 128
        FFN = 512
        N_EXPERTS = 8
        TOPK = 2
        B, L = (4, 256)

        def _moe(x, gate_w, gate_b, w1, b1, w2, b2):
            bs, l, d = x.shape
            T = bs * l
            xf = x.reshape(T, d)
            logits = xf @ gate_w + gate_b
            top_vals, top_idx = jax.lax.top_k(logits, TOPK)
            rows = jnp.arange(T)[:, None]
            sparse = jnp.full_like(logits, -jnp.inf).at[rows, top_idx].set(top_vals)
            gates = jax.nn.softmax(sparse, axis=-1)
            out = jnp.zeros_like(xf)
            for e in range(N_EXPERTS):
                h = jax.nn.gelu(xf @ w1[e] + b1[e], approximate=False)
                y = h @ w2[e] + b2[e]
                out = out + gates[:, e:e + 1] * y
            return out.reshape(bs, l, d)
        return _moe(x, gate_w, gate_b, w1, b1, w2, b2)
    x = x + _L0_xattn_ref(_layernorm(x, axis=-1), ctx_768, L0_xattn_Wv, L0_xattn_bv, L0_xattn_Wt, L0_xattn_bt)
    x = x + _L0_ffn_ref(_layernorm(x, axis=-1), L0_ffn_w_gate, L0_ffn_w_up, L0_ffn_w_down)
    x = x + _L1_xattn_ref(_layernorm(x, axis=-1), ctx_768, L1_xattn_Wq, L1_xattn_Wk, L1_xattn_Wv, L1_xattn_Wout, L1_xattn_bout)
    x = x + _L1_ffn_ref(_layernorm(x, axis=-1), L1_ffn_gate_w, L1_ffn_gate_b, L1_ffn_w1, L1_ffn_b1, L1_ffn_w2, L1_ffn_b2)
    return x

_drawn_inputs = setup_inputs


def setup_inputs(seed=0):
    import zlib

    import numpy as np

    out = dict(_drawn_inputs(seed))
    spreads = {'L1_xattn_bout': (0.0, 0.1)}
    factors = {'L0_xattn_bv': 24.789,
     'L0_xattn_bt': 37.882,
     'L0_ffn_w_gate': 3.573,
     'L0_ffn_w_up': 3.461,
     'L0_ffn_w_down': 3.194,
     'L1_ffn_b1': 4.455,
     'L1_ffn_b2': 3.221}
    for name, (base, spread) in spreads.items():
        noise = np.random.default_rng([zlib.crc32(name.encode()), seed]).standard_normal(out[name].shape)
        drawn = base * np.exp(spread * noise) if base else spread * noise
        out[name] = jnp.asarray(drawn.astype(out[name].dtype))
    for name, factor in factors.items():
        out[name] = (out[name] * factor).astype(out[name].dtype)
    return out
```

```python
import concourse.bass as bass
from concourse import mybir
from contextlib import ExitStack


def xattn_ffn_two_layers(nc, x, ctx_768, L0_xattn_Wv, L0_xattn_bv, L0_xattn_Wt, L0_xattn_bt, L0_ffn_w_gate,
                         L0_ffn_w_up, L0_ffn_w_down, L1_xattn_Wq, L1_xattn_Wk, L1_xattn_Wv, L1_xattn_Wout,
                         L1_xattn_bout, L1_ffn_gate_w, L1_ffn_gate_b, L1_ffn_w1, L1_ffn_b1, L1_ffn_w2,
                         L1_ffn_b2, out):
    fp32, fp32r, u32 = mybir.dt.float32, mybir.dt.float32r, mybir.dt.uint32
    ALU, ACT, AX = mybir.AluOpType, mybir.ActivationFunctionType, mybir.AxisListType

    P = 128
    NB, S, D = x.shape
    C = ctx_768.shape[2]
    T = NB * S
    HALF = T // 2
    CH = NB // 2
    HD = L0_xattn_Wv.shape[0]
    FC0 = L0_ffn_w_gate.shape[0] // P
    BLK = 32
    NBLK = D // BLK
    NH = L1_xattn_Wq.shape[1] // P
    DH = P
    NE, _, F1 = L1_ffn_w1.shape
    FC1 = F1 // P
    assert S == P and D == P and T == 1024 and NH % 2 == 0 and NE % 2 == 0

    LN_EPS = 1e-5
    COS_EPS = 1e-8
    RNORM_MAX = 1e30
    QMAX = 32767.0
    SCALE_MIN = 1e-12
    WMAX = 7.0
    MAGIC = 1.5 * 2.0 ** 23
    MAGIC16 = MAGIC * 2.0 ** -16
    SIG_TOP = 65535.0 / 65536.0
    SM_SCALE = 1.5 * DH ** -0.5
    E1 = 2.718281828459045

    es = ExitStack()
    with es:
        def sb(name, shape, dt=fp32):
            return es.enter_context(nc.sbuf_tensor(name, shape, dt))

        def sem(name):
            return es.enter_context(nc.semaphore(name))

        ident = sb("ident", [P, P])
        ones = sb("ones", [P, P])
        minus_half = sb("minus_half", [P, 2 * NB])
        base_e = sb("base_e", [P, NB])
        xs = sb("xs", [P, NB, D])
        xn = sb("xn", [P, NB, D])
        xnT = sb("xnT", [P, T])
        xnT_hi = sb("xnT_hi", [P, T], fp32r)
        xnT_lo = sb("xnT_lo", [P, T], fp32r)
        bstat = sb("bstat", [P, NB, 6])
        mv = sb("mv", [P, NB, 2])
        var_eps = sb("var_eps", [P, NB])
        rstd = sb("rstd", [P, NB])
        ctx_aug = sb("ctx_aug", [P, NB, C + 1])
        ctxT = sb("ctxT", [C, T])
        ctxT_hi = sb("ctxT_hi", [C + 1, T], fp32r)
        ctxT_lo = sb("ctxT_lo", [C, T], fp32r)
        wv0 = sb("wv0", [HD, D])
        wt0 = sb("wt0", [HD, C])
        bv0 = sb("bv0", [HD, 1])
        bt0 = sb("bt0", [HD, 1])
        wT0 = sb("wT0", [P, 2, HD])
        nsq = sb("nsq", [P, 2, NB])
        rn = sb("rn", [P, 2, NB])
        wf = sb("wf", [P, 3, FC0 * NBLK, BLK])
        wf_q = sb("wf_q", [P, 3, FC0 * NBLK, BLK])
        wf_s = sb("wf_s", [P, 3 * FC0 * NBLK])
        wf_rs = sb("wf_rs", [P, 3 * FC0 * NBLK])
        wfT = sb("wfT", [P, 3 * FC0, P])
        amax = sb("amax", [P, 8, 4])
        qs = sb("qs", [P, 8, 8])
        wq = sb("wq", [D, NH * DH])
        wout = sb("wout", [DH, NH, D])
        bout = sb("bout", [1, D])
        hT = sb("hT", [P, 2, D + 2 * C])
        A32 = sb("A32", [D, NH, C])
        A_hi = sb("A_hi", [D, NH, C], fp32r)
        A_lo = sb("A_lo", [D, NH, C], fp32r)
        Bh = sb("Bh", [C, NH, D])
        Acur_hi = sb("Acur_hi", [D, 2, C], fp32r)
        Acur_lo = sb("Acur_lo", [D, 2, C], fp32r)
        qT_hi = sb("qT_hi", [C + 1, 2, T], fp32r)
        qT_lo = sb("qT_lo", [C, 2, T], fp32r)
        tmax = sb("tmax", [P, 2 * NB])
        Z = sb("Z", [P, C + NB])
        rsum = sb("rsum", [P, 2, CH])
        On = sb("On", [P, NB, C])
        OT = sb("OT", [C, NH, T])
        wk, wv = OT[:, 0, :], OT[:, 1, :]
        PT = sb("PT", [P, 2, NB, T])
        gw = sb("gw", [D, NE])
        gb = sb("gb", [1, NE])
        b1n = sb("b1n", [NE * FC1, P])
        b1T = sb("b1T", [P, NE * FC1])
        b1cur = sb("b1cur", [P, 2, FC1])
        b2 = sb("b2", [NE, D])
        w1 = wq[:, :].rearrange("p (a f) -> p a f", a=2)
        w1_hi = sb("w1_hi", [D, 2, F1], fp32r)
        w1_lo = sb("w1_lo", [D, 2, F1], fp32r)
        w2 = wout[:, :, :].rearrange("p (a c) d -> p a c d", a=2)
        logit = sb("logit", [P, NB, NE])
        top = sb("top", [P, NB, 8])
        topi = sb("topi", [P, NB, 8], u32)
        topf = sb("topf", [P, NB, 8])
        iota_i = sb("iota_i", [P, NE], mybir.dt.int32)
        iota_f = sb("iota_f", [P, NE])
        dtop = sb("dtop", [P, NB])
        etop = sb("etop", [P, NB])
        g01 = sb("g01", [P, 2, NB])
        gate_a = sb("gate_a", [P, NB, NE])
        gate_b = sb("gate_b", [P, NB, NE])
        gates = sb("gates", [P, NB, NE])
        gatesT = ctxT[0:NE, :]

        flat = PT[:, :, :, :].rearrange("p a b t -> p (a b t)")
        W3 = FC0 * T

        def big(i):
            return flat[:, i * W3:(i + 1) * W3].rearrange("p (c t) -> p c t", c=FC0)
        g_raw, u_raw, sig, gsv = big(0), big(1), big(2), big(3)
        cosr = flat[:, 4 * W3:4 * W3 + T].rearrange("p (b d) -> p b d", b=NB)
        vT, vsq, tT, tsq = (flat[0:HD, i * T:(i + 1) * T] for i in range(4))
        hidT = flat[:, 0:2 * FC1 * HALF].rearrange("p (a c t) -> p a c t", a=2, c=FC1)

        ps = es.enter_context(nc.psum_tensor("ps", [P, 8, HALF], fp32))

        def chunks(bank, n=CH):
            return ps[:, bank, 0:n * P].rearrange("p (b d) -> p b d", b=n)

        ld = {n: sem("ld_" + n) for n in ("x0", "x1", "ctx", "w0", "wf", "watt", "wout", "small")}
        w1_loaded = [sem(f"w1_loaded{i}") for i in range(2)]
        w2_loaded = [sem(f"w2_loaded{i}") for i in range(2)]
        const_step, const_ready = sem("const_step"), sem("const_ready")
        dve_done, act_done, pool_done = sem("dve_done"), sem("act_done"), sem("pool_done")
        var_ready, rstd_ready, xn_ready = sem("var_ready"), sem("rstd_ready"), sem("xn_ready")
        xT_ps, xT_ready, xT_hi_ready, xT_lo_ready = sem("xT_ps"), sem("xT_ready"), sem("xT_hi_ready"), sem("xT_lo_ready")
        ctxT_ps, ctxT_ready, ctxT_lo_ready = sem("ctxT_ps"), sem("ctxT_ready"), sem("ctxT_lo_ready")
        wT0_ps, wT0_ready = sem("wT0_ps"), sem("wT0_ready")
        t_ps, t_ready, v_ps, v_ready = sem("t_ps"), sem("t_ready"), sem("v_ps"), sem("v_ready")
        nsq_ps, nsq_ready, rn_pow, rn_ready = sem("nsq_ps"), sem("nsq_ready"), sem("rn_pow"), sem("rn_ready")
        rt_ps, dots_ps, cos_used = sem("rt_ps"), sem("dots_ps"), sem("cos_used")
        hT_ps, hT_ready, AB_ps, AB_ready, A_lo_ready = (sem("hT_ps"), sem("hT_ready"), sem("AB_ps"), sem("AB_ready"),
                                                        sem("A_lo_ready"))
        wq_ready, wfT_ps, wfT_ready = sem("wq_ready"), sem("wfT_ps"), sem("wfT_ready")
        am_ready, amT_ps, gmax_read = sem("am_ready"), sem("amT_ps"), sem("gmax_read")
        raw_ps, raw_ready = sem("raw_ps"), sem("raw_ready")
        ng_ready, sig_ready, no_ready, down_ps, x_added = (sem("ng_ready"), sem("sig_ready"), sem("no_ready"),
                                                           sem("down_ps"), sem("x_added"))
        Acur_ready, q_ps, q_hi_ready, q_lo_ready = sem("Acur_ready"), sem("q_ps"), sem("q_hi_ready"), sem("q_lo_ready")
        max_ps, max_read, z_ready, z_ps, mrow_ready = (sem("max_ps"), sem("max_read"), sem("z_ready"), sem("z_ps"),
                                                       sem("mrow_ready"))
        st_ps, exp_ready, pv_ps, on_ready, ot_ps, ot_ready = (sem("st_ps"), sem("exp_ready"), sem("pv_ps"),
                                                              sem("on_ready"), sem("ot_ps"), sem("ot_ready"))
        y_ps, rs_ready = sem("y_ps"), sem("rs_ready")
        b1T_ps, b1T_ready, logit_ps, logit_read = sem("b1T_ps"), sem("b1T_ready"), sem("logit_ps"), sem("logit_read")
        dtop_ready, etop_ready, gates_ready, gT_ps, gT_ready, b2_ps = (
            sem("dtop_ready"), sem("etop_ready"), sem("gates_ready"), sem("gT_ps"), sem("gT_ready"), sem("b2_ps"))
        w1_split, hid_ps, hid_ready, ey_ps, ey_added = (sem("w1_split"), sem("hid_ps"), sem("hid_ready"), sem("ey_ps"),
                                                        sem("ey_added"))
        out_stored = sem("out_stored")

        block = es.enter_context(nc.Block())

        MAX_AT = [0, 1, 1, 1, 1, 2, 1, 1, 2, 1, 1, 2, 1, 1, 0, 0]
        PV_N = [5] * 12 + [4] + [0] * 3
        assert sum(MAX_AT) == 2 * NB and sum(PV_N) == NB * NB
        OT_AT = 9
        Z_AT = 14

        @block.sync
        def _(sp):
            def load(dst, src, s):
                sp.dma_start(dst, src).then_inc(s, 16)
            for h in range(2):
                load(xs[:, h * CH:(h + 1) * CH, :], x[h * CH:(h + 1) * CH].rearrange("b s d -> s b d"), ld[f"x{h}"])
            load(wt0[:, :], L0_xattn_Wt, ld["w0"])
            load(wv0[:, :], L0_xattn_Wv, ld["w0"])
            load(bt0[:, :], L0_xattn_bt.rearrange("(h o) -> h o", o=1), ld["w0"])
            load(bv0[:, :], L0_xattn_bv.rearrange("(h o) -> h o", o=1), ld["w0"])
            for i, w in enumerate((L0_ffn_w_gate, L0_ffn_w_up)):
                load(wf[:, i, :, :].rearrange("p (c n) k -> p c (n k)", c=FC0),
                     w.rearrange("(c p) d -> p c d", p=P), ld["wf"])
            load(wf[:, 2, :, :].rearrange("p n k -> p (n k)"), L0_ffn_w_down, ld["wf"])
            load(wout[:, :, :], L1_xattn_Wout.rearrange("(h j) d -> j h d", j=DH), ld["wout"])
            load(bout[:, :], L1_xattn_bout.rearrange("(o d) -> o d", o=1), ld["small"])
            load(gw[:, :], L1_ffn_gate_w, ld["small"])
            load(gb[:, :], L1_ffn_gate_b.rearrange("(o d) -> o d", o=1), ld["small"])
            load(b1n[:, :], L1_ffn_b1.rearrange("e (c p) -> (e c) p", p=P), ld["small"])
            load(b2[:, :], L1_ffn_b2, ld["small"])

            def load_expert(e, buf):
                sp.dma_start(w1[:, buf, :], L1_ffn_w1[e]
                             ).then_inc(w1_loaded[buf], 16)
                sp.dma_start(w2[:, buf, :, :], L1_ffn_w2[e].rearrange("(c p) d -> p c d", p=P)
                             ).then_inc(w2_loaded[buf], 16)
            sp.wait_ge(AB_ready, NH)
            load_expert(0, 0)
            load_expert(1, 1)
            for e in range(NE - 2):
                sp.wait_ge(w1_split, e + 1)
                sp.wait_ge(ey_ps, 2 * e + 2)
                load_expert(e + 2, e % 2)
            for h in range(2):
                sp.wait_ge(ey_added, 2 * (NE - 1) + h + 2)
                sp.dma_start(out[h * CH:(h + 1) * CH].rearrange("b s d -> s b d"), xs[:, h * CH:(h + 1) * CH, :]
                             ).then_inc(out_stored, 16)
            sp.wait_ge(out_stored, 32)

        @block.gpsimd
        def _(pool):
            nc.gpsimd.memset(ident[:, :], 0.0)
            nc.gpsimd.memset(ones[:, :], 1.0)
            nc.gpsimd.memset(minus_half[:, :], -0.5)
            nc.gpsimd.memset(base_e[:, :], E1)
            nc.gpsimd.memset(ctx_aug[:, :, C:C + 1], 1.0)
            nc.gpsimd.memset(Z[:, :], 0.0)
            nc.gpsimd.iota(iota_i[:, :], [[1, NE]], base=0, channel_multiplier=0).then_inc(const_step, 1)
            pool.wait_ge(const_step, 1)
            nc.gpsimd.affine_select(out=ident[:, :], in_=ident[:, :], compare_op=ALU.not_equal, fill=1.0, base=0,
                                    pattern=[[-1, P]], channel_multiplier=1).then_inc(const_ready, 1)

            def rstd_pow(k):
                pool.wait_ge(var_ready, k + 1)
                nc.gpsimd.tensor_tensor(out=rstd[:, :], in0=var_eps[:, :], in1=minus_half[:, 0:NB],
                                        op=ALU.pow).then_inc(rstd_ready, 1)

            def norm_pow(i):
                pool.wait_ge(nsq_ready, i + 1)
                nc.gpsimd.tensor_tensor(out=rn[:, i, :], in0=nsq[:, i, :], in1=minus_half[:, 0:NB],
                                        op=ALU.pow).then_inc(rn_pow, 1)

            rstd_pow(0)
            norm_pow(0)
            norm_pow(1)
            pool.wait_ge(AB_ready, NH)
            nc.gpsimd.tensor_tensor(out=A_lo[:, :, :], in0=A32[:, :, :], in1=A_hi[:, :, :].bitcast(fp32),
                                    op=ALU.subtract).then_inc(A_lo_ready, 1)
            rstd_pow(1)
            rstd_pow(2)

            def stage_A(h, buf):
                nc.gpsimd.tensor_copy(Acur_hi[:, buf, :], A_hi[:, h, :].bitcast(fp32))
                nc.gpsimd.tensor_copy(Acur_lo[:, buf, :], A_lo[:, h, :].bitcast(fp32)).then_inc(Acur_ready, 1)
            pool.wait_ge(A_lo_ready, 1)
            stage_A(0, 0)
            stage_A(1, 1)
            for h in range(NH - 2):
                pool.wait_ge(q_ps, 2 * h + 2)
                stage_A(h + 2, h % 2)

            rstd_pow(3)
            pool.wait_ge(dtop_ready, 1)
            nc.gpsimd.tensor_tensor(out=etop[:, :], in0=base_e[:, :], in1=dtop[:, :], op=ALU.pow
                                    ).then_inc(etop_ready, 1)

            def split_w1(e, buf, k):
                pool.wait_ge(w1_loaded[buf], 16 * k)
                nc.gpsimd.tensor_copy(w1_hi[:, buf, :], w1[:, buf, :]).then_inc(pool_done, 1)
                nc.gpsimd.tensor_copy(b1cur[:, buf, :], b1T[:, e * FC1:(e + 1) * FC1])
                pool.wait_ge(pool_done, e + 1)
                nc.gpsimd.tensor_tensor(out=w1_lo[:, buf, :], in0=w1[:, buf, :], in1=w1_hi[:, buf, :].bitcast(fp32),
                                        op=ALU.subtract).then_inc(w1_split, 1)
            pool.wait_ge(b1T_ready, 1)
            split_w1(0, 0, 1)
            split_w1(1, 1, 1)
            for e in range(NE - 2):
                pool.wait_ge(hid_ready, 2 * FC1 * (e + 1))
                split_w1(e + 2, e % 2, e // 2 + 2)

        @block.tensor
        def _(pe):
            mm, tr = nc.tensor.matmul, nc.tensor.transpose

            def transpose_stream(k, src, ready, count):
                for b in range(NB):
                    if b % (NB // count) == 0:
                        pe.wait_ge(ready, k + b // (NB // count) + 1)
                    i = tr(ps[:, b // CH, (b % CH) * P:(b % CH + 1) * P], src[:, b, :], ident[:, :])
                    if b % CH == CH - 1:
                        i.then_inc(xT_ps, 1)

            pe.wait_ge(const_ready, 1)
            pe.wait_ge(ld["ctx"], 16)
            for b in range(NB):
                i = tr(ps[0:C, b // CH, (b % CH) * P:(b % CH + 1) * P], ctx_aug[:, b, 0:C], ident[:, :])
                if b % CH == CH - 1:
                    i.then_inc(ctxT_ps, 1)
            pe.wait_ge(ld["w0"], 64)
            tr(ps[0:C, 2, 0:HD], wt0[:, :], ident[0:HD, 0:HD])
            tr(ps[0:D, 2, HD:2 * HD], wv0[:, :], ident[0:HD, 0:HD]).then_inc(wT0_ps, 1)
            pe.wait_ge(wT0_ready, 1)
            for h in range(2):
                pe.wait_ge(ctxT_ready, h + 1)
                mm(ps[0:HD, 3 + h, :], wT0[0:C, 0, :], ctxT[:, h * HALF:(h + 1) * HALF], start=True, stop=True
                   ).then_inc(t_ps, 1)

            def squared_norms(i, sq, bank):
                for b in range(NB):
                    j = mm(ps[:, bank, b:b + 1], sq[:, b * P:(b + 1) * P], ones[0:HD, 0:1],
                           start=True, stop=True)
                j.then_inc(nsq_ps, 1)
            pe.wait_ge(t_ready, 2)
            squared_norms(0, tsq, 2)
            pe.wait_ge(rn_ready, 1)
            for b in range(NB):
                i = mm(ps[:, 5 + b // CH, (b % CH) * P:(b % CH + 1) * P], rn[:, 0, b:b + 1].to_broadcast([P, P]),
                       ident[:, :], start=True, stop=True)
                if b % CH == CH - 1:
                    i.then_inc(rt_ps, 1)
            pe.wait_ge(ctxT_lo_ready, 2)
            transpose_stream(0, xn, xn_ready, NB)
            for h in range(2):
                pe.wait_ge(xT_ready, h + 1)
                mm(ps[0:HD, 3 + h, :], wT0[:, 1, :], xnT[:, h * HALF:(h + 1) * HALF], start=True, stop=True
                   ).then_inc(v_ps, 1)
            pe.wait_ge(v_ready, 2)
            squared_norms(1, vsq, 7)
            for b in range(NB):
                i = mm(ps[:, b // CH, (b % CH) * P:(b % CH + 1) * P], vT[:, b * P:(b + 1) * P],
                       tT[:, b * P:(b + 1) * P], start=True, stop=True)
                if b % CH == CH - 1:
                    i.then_inc(dots_ps, 1)

            pe.wait_ge(ld["watt"], 48)
            pe.wait_ge(ld["wout"], 16)

            def head_transposes(h):
                if h >= 2:
                    pe.wait_ge(hT_ready, h - 1)
                bank = 3 + h % 2
                cols = slice(h * DH, (h + 1) * DH)
                tr(ps[:, bank, 0:D], wq[:, cols], ident[:, :])
                tr(ps[:, bank, D:D + C], wk[:, cols], ident[0:C, 0:C])
                tr(ps[:, bank, D + C:D + 2 * C], wv[:, cols], ident[0:C, 0:C]).then_inc(hT_ps, 1)

            def head_products(h):
                pe.wait_ge(hT_ready, h + 1)
                if h == 0:
                    pe.wait_ge(nsq_ready, 2)
                if h < 2:
                    pe.wait_ge(cos_used, 2)
                if h >= 2:
                    pe.wait_ge(AB_ready, h - 1)
                bank, w = 6 + h % 2, hT[:, h % 2, :]
                mm(ps[:, bank, 0:C], w[:, 0:D], w[:, D:D + C], start=True, stop=True)
                mm(ps[0:C, bank, P:P + D], w[:, D + C:D + 2 * C], wout[:, h, :], start=True, stop=True
                   ).then_inc(AB_ps, 1)
            head_transposes(0)
            for h in range(NH):
                if h + 1 < NH:
                    head_transposes(h + 1)
                head_products(h)

            pe.wait_ge(wq_ready, 1)
            pe.wait_ge(AB_ready, NH)
            for j in range(3 * FC0):
                w, c = j // FC0, j % FC0
                i = tr(ps[:, (2, 5, 6)[w], c * P:(c + 1) * P],
                       wf_q[:, w, c * NBLK:(c + 1) * NBLK, :].rearrange("p n k -> p (n k)"), ident[:, :])
                if c == FC0 - 1:
                    i.then_inc(wfT_ps, 1)

            def spread_max(k):
                pe.wait_ge(am_ready, k + 1)
                mm(ps[:, 7, 0:P], amax[:, k, 3:4].to_broadcast([P, P]), ident[:, :], start=True, stop=True
                   ).then_inc(amT_ps, 1)
            spread_max(0)
            pe.wait_ge(x_added, 1)
            transpose_stream(0, xn, no_ready, 1)
            pe.wait_ge(wfT_ready, 2)
            for j in range(4 * FC0):
                w, c, h = j // (2 * FC0), j // 2 % FC0, j % 2
                if j < 2:
                    pe.wait_ge(xT_ready, 2 + h + 1)
                if j >= 6:
                    pe.wait_ge(raw_ready, j - 5)
                mm(ps[:, j % 6, :], wfT[:, w * FC0 + c, :], xnT[:, h * HALF:(h + 1) * HALF], start=True, stop=True
                   ).then_inc(raw_ps, 1)
                if j == 8:
                    spread_max(1)
            for k in (2, 3, 4):
                spread_max(k)
            for b in range(NB):
                if b == 0:
                    pe.wait_ge(raw_ready, 4 * FC0)
                    pe.wait_ge(wfT_ready, 3)
                for c in range(FC0):
                    if b == 0:
                        pe.wait_ge(no_ready, 2 + c)
                    i = mm(ps[:, b // CH, (b % CH) * P:(b % CH + 1) * P], gsv[:, c, b * P:(b + 1) * P],
                           wfT[:, 2 * FC0 + c, :], start=(c == 0), stop=(c == FC0 - 1))
                if b % CH == CH - 1:
                    i.then_inc(down_ps, 1)

            pe.wait_ge(x_added, 2)
            for b in range(NB):
                pe.wait_ge(xn_ready, 2 * NB + b + 1)
                i = tr(ps[:, b // CH, (b % CH) * P:(b % CH + 1) * P], xn[:, b, :], ident[:, :])
                if b % CH == CH - 1:
                    i.then_inc(xT_ps, 1)

            def project(h, buf, halves):
                for hf in halves:
                    if hf == 0:
                        pe.wait_ge(Acur_ready, h + 1)
                    cols = slice(hf * HALF, (hf + 1) * HALF)
                    o = ps[0:C, 7 - hf, :]
                    mm(o, Acur_hi[:, buf, :], xnT_hi[:, cols], start=True, stop=False)
                    mm(o, Acur_hi[:, buf, :], xnT_lo[:, cols], start=False, stop=False)
                    mm(o, Acur_lo[:, buf, :], xnT_hi[:, cols], start=False, stop=True).then_inc(q_ps, 1)

            def max_tile(h, buf, t, first=False):
                qc, hf = t // 2, t % 2
                if t == 0 or t == NB:
                    pe.wait_ge(q_hi_ready, 2 * h + t // NB + 1)
                if not (first and t < 2):
                    pe.wait_ge(max_read, 2 * NB * h + t - 1)
                mm(ps[:, 2 + t % 2, :], qT_hi[0:C, buf, qc * P:(qc + 1) * P], ctxT_hi[0:C, hf * HALF:(hf + 1) * HALF],
                   start=True, stop=True).then_inc(max_ps, 1)

            def max_rows(h):
                pe.wait_ge(z_ready, h + 1)
                for qc in range(NB):
                    i = tr(ps[0:C + 1, 6 + qc // CH, (qc % CH) * P:(qc % CH + 1) * P], Z[:, qc:qc + C + 1], ident[:, :])
                    if qc % CH == CH - 1:
                        i.then_inc(z_ps, 1)

            def score_tile(h, buf, t, first=False):
                kc, hf = t // 2, t % 2
                if t < 2:
                    pe.wait_ge(mrow_ready, 2 * h + t + 1)
                    pe.wait_ge(q_lo_ready, 2 * h + t + 1)
                if not (first and t < 2):
                    pe.wait_ge(exp_ready, 2 * NB * h + t - 1)
                k, q, o = slice(kc * P, (kc + 1) * P), slice(hf * HALF, (hf + 1) * HALF), ps[:, t % 2, :]
                mm(o, ctxT_hi[:, k], qT_hi[:, buf, q], start=True, stop=False)
                mm(o, ctxT_hi[0:C, k], qT_lo[:, buf, q], start=False, stop=False)
                mm(o, ctxT_lo[:, k], qT_hi[0:C, buf, q], start=False, stop=True).then_inc(st_ps, 1)

            def pv_part(h, buf, n0, n1):
                for n in range(n0, n1):
                    qc, kc = n // NB, n % NB
                    if n == 0:
                        pe.wait_ge(exp_ready, 2 * NB * (h + 1))
                    c0 = (qc % CH) * (C + 1)
                    i = mm(ps[:, 4 + qc // CH, c0:c0 + C + 1], PT[:, buf, kc, qc * P:(qc + 1) * P], ctx_aug[:, kc, :],
                           start=(kc == 0), stop=(kc == NB - 1))
                    if kc == NB - 1 and qc % CH == CH - 1:
                        i.then_inc(pv_ps, 1)

            def out_transposes(h, hf):
                pe.wait_ge(on_ready, 2 * h + hf + 1)
                for j in range(CH):
                    i = tr(ps[0:C, 6, j * P:(j + 1) * P], On[:, hf * CH + j, :], ident[:, :])
                i.then_inc(ot_ps, 1)

            def head(h, buf, first=False, last=False):
                t_max, n_pv = 0, 0
                if not last:
                    pe.wait_ge(mrow_ready, 2 * h + 2)
                    project(h + 1, 1 - buf, (0,))
                for t in range(2 * NB):
                    score_tile(h, buf, t, first)
                    if t == 1 and not last:
                        pe.wait_ge(q_hi_ready, 2 * (h + 1) + 1)
                        project(h + 1, 1 - buf, (1,))
                    if not first:
                        pv_part(h - 1, 1 - buf, n_pv, n_pv + PV_N[t])
                        n_pv += PV_N[t]
                    if not last:
                        for _ in range(MAX_AT[t]):
                            max_tile(h + 1, 1 - buf, t_max)
                            t_max += 1
                    if t == OT_AT and not first:
                        if last:
                            pe.wait_ge(ot_ready, 2 * (h - 1))
                        else:
                            pe.wait_ge(q_lo_ready, 2 * (h + 1) + 2)
                        out_transposes(h - 1, 0)
                    if t == Z_AT and not last:
                        if first:
                            pe.wait_ge(q_lo_ready, 2 * (h + 1) + 2)
                        else:
                            pe.wait_ge(ot_ready, 2 * (h - 1) + 1)
                        max_rows(h + 1)
                if not first:
                    if not last:
                        pe.wait_ge(mrow_ready, 2 * (h + 1) + 1)
                    else:
                        pe.wait_ge(ot_ready, 2 * (h - 1) + 1)
                    out_transposes(h - 1, 1)

            pe.wait_ge(xT_lo_ready, 2)
            pe.wait_ge(ctxT_lo_ready, 2)
            project(0, 0, (0, 1))
            for t in range(2 * NB):
                max_tile(0, 0, t, first=True)
            pe.wait_ge(q_lo_ready, 2)
            max_rows(0)
            pe.wait_ge(mrow_ready, 2)
            head(0, 0, first=True)
            with pe.Fori(0, NH // 2 - 1) as i:
                head(2 * i + 1, 1)
                head(2 * i + 2, 0)
            head(NH - 1, 1, last=True)
            pv_part(NH - 1, 1, 0, NB * NB)
            pe.wait_ge(ot_ready, 2 * (NH - 1))
            out_transposes(NH - 1, 0)
            pe.wait_ge(ot_ready, 2 * (NH - 1) + 1)
            out_transposes(NH - 1, 1)
            pe.wait_ge(ld["small"], 80)
            pe.wait_ge(exp_ready, 2 * NB * NH)
            for b in range(NB):
                if b % CH == 0:
                    pe.wait_ge(ot_ready, 2 * (NH - 1) + b // CH + 1)
                o = ps[:, b // CH, (b % CH) * P:(b % CH + 1) * P]
                for h in range(NH):
                    mm(o, OT[:, h, b * P:(b + 1) * P], Bh[:, h, :], start=(h == 0), stop=False)
                i = mm(o, ones[0:1, :], bout[:, :], start=False, stop=True)
                if b % CH == CH - 1:
                    i.then_inc(y_ps, 1)

            tr(ps[:, 3, 0:NE * FC1], b1n[:, :], ident[0:NE * FC1, 0:NE * FC1]).then_inc(b1T_ps, 1)
            for b in range(NB):
                pe.wait_ge(xn_ready, 3 * NB + b + 1)
                i = tr(ps[:, 4 + b // CH, (b % CH) * P:(b % CH + 1) * P], xn[:, b, :], ident[:, :])
                if b % CH == CH - 1:
                    i.then_inc(xT_ps, 1)
            pe.wait_ge(xT_ready, 6)
            for b in range(NB):
                o = ps[:, 6, b * NE:(b + 1) * NE]
                mm(o, xnT[:, b * P:(b + 1) * P], gw[:, :], start=True, stop=False)
                i = mm(o, ones[0:1, :], gb[:, :], start=False, stop=True)
            i.then_inc(logit_ps, 1)

            def gate_bias():
                pe.wait_ge(gates_ready, 1)
                for b in range(NB):
                    i = tr(ps[0:NE, 6 + b // CH, (b % CH) * P:(b % CH + 1) * P], gates[:, b, :], ident[:, :])
                i.then_inc(gT_ps, 1)
                pe.wait_ge(gT_ready, 1)
                for b in range(NB):
                    i = mm(ps[:, 6 + b // CH, (b % CH) * P:(b % CH + 1) * P], gatesT[:, b * P:(b + 1) * P], b2[:, :],
                           start=True, stop=True)
                i.then_inc(b2_ps, 1)

            def hidden_tile(e, buf, s, first=False):
                hf, c = s // FC1, s % FC1
                if s == 0:
                    pe.wait_ge(w1_split, e + 1)
                if not (first and s < 3):
                    pe.wait_ge(hid_ready, 2 * FC1 * e + s - 2)
                f, t = slice(c * P, (c + 1) * P), slice(hf * HALF, (hf + 1) * HALF)
                o = ps[:, s % 4, :]
                mm(o, w1_hi[:, buf, f], xnT_hi[:, t], start=True, stop=False)
                mm(o, w1_hi[:, buf, f], xnT_lo[:, t], start=False, stop=False)
                mm(o, w1_lo[:, buf, f], xnT_hi[:, t], start=False, stop=True).then_inc(hid_ps, 1)

            def expert_out(e, buf, hf, j, k, first=False):
                if j == 0:
                    pe.wait_ge(hid_ready, 2 * FC1 * e + FC1 * (hf + 1))
                    pe.wait_ge(w2_loaded[buf], 16 * k)
                    if not first:
                        pe.wait_ge(ey_added, 2 * e + hf)
                for c in range(FC1):
                    i = mm(ps[:, 4 + hf, j * P:(j + 1) * P], hidT[:, hf, c, j * P:(j + 1) * P], w2[:, buf, c, :],
                           start=(c == 0), stop=(c == FC1 - 1))
                if j == CH - 1:
                    i.then_inc(ey_ps, 1)

            def expert(e, buf, k, k_prev, first=False):
                for s in range(2 * FC1):
                    hidden_tile(e, buf, s, first)
                    if s < FC1:
                        if not first:
                            expert_out(e - 1, 1 - buf, 1, s, k_prev)
                    else:
                        expert_out(e, buf, 0, s - FC1, k, first)
                    if first and s == FC1 - 1:
                        gate_bias()
            pe.wait_ge(xT_lo_ready, 4)
            pe.wait_ge(b1T_ready, 1)
            expert(0, 0, 1, 0, first=True)
            with pe.Fori(0, NE // 2 - 1) as i:
                expert(2 * i + 1, 1, i + 1, i + 1)
                expert(2 * i + 2, 0, i + 2, i + 1)
            expert(NE - 1, 1, NE // 2, NE // 2)
            for j in range(CH):
                expert_out(NE - 1, 1, 1, j, NE // 2)

        @block.scalar
        def _(act):
            af, count = nc.scalar.activation, [0]

            def link(ins):
                count[0] += 1
                ins.then_inc(act_done, 1)
                act.wait_ge(act_done, count[0])

            act.dma_start(ctx_aug[:, :, 0:C], ctx_768.rearrange("b s c -> s b c")).then_inc(ld["ctx"], 16)
            act.dma_start(wq[:, :], L1_xattn_Wq).then_inc(ld["watt"], 16)
            act.dma_start(wk, L1_xattn_Wk).then_inc(ld["watt"], 16)
            act.dma_start(wv, L1_xattn_Wv).then_inc(ld["watt"], 16)

            def cols(h):
                return slice(h * HALF, (h + 1) * HALF)
            for h in range(2):
                act.wait_ge(ctxT_ps, h + 1)
                af(ctxT[:, cols(h)], ps[0:C, h, :], ACT.Copy)
                af(ctxT_hi[0:C, cols(h)], ps[0:C, h, :], ACT.Copy).then_inc(ctxT_ready, 1)
            act.wait_ge(wT0_ps, 1)
            af(wT0[0:C, 0, :], ps[0:C, 2, 0:HD], ACT.Copy)
            af(wT0[:, 1, :], ps[:, 2, HD:2 * HD], ACT.Copy).then_inc(wT0_ready, 1)

            def with_bias(src_ps, bias, dst, dst_sq, ready):
                for h in range(2):
                    act.wait_ge(src_ps, h + 1)
                    af(dst[:, cols(h)], ps[0:HD, 3 + h, :], ACT.Identity, bias=bias[:, 0:1])
                    af(dst_sq[:, cols(h)], ps[0:HD, 3 + h, :], ACT.Square, bias=bias[:, 0:1]).then_inc(ready, 1)

            def evacuate_xT(k, bank, plain=True):
                for h in range(2):
                    act.wait_ge(xT_ps, 2 * k + h + 1)
                    af(xnT[:, cols(h)], ps[:, bank + h, :], ACT.Copy).then_inc(xT_ready, 1)
            with_bias(t_ps, bt0, tT, tsq, t_ready)
            evacuate_xT(0, 0)
            with_bias(v_ps, bv0, vT, vsq, v_ready)
            for h in range(NH):
                act.wait_ge(hT_ps, h + 1)
                if h >= 2:
                    act.wait_ge(AB_ps, h - 1)
                af(hT[:, h % 2, :], ps[:, 3 + h % 2, 0:D + 2 * C], ACT.Copy).then_inc(hT_ready, 1)
                if h >= 1:
                    act.wait_ge(AB_ps, h)
                    g, bank = h - 1, 6 + (h - 1) % 2
                    af(A32[:, g, :], ps[:, bank, 0:C], ACT.Copy)
                    af(A_hi[:, g, :], ps[:, bank, 0:C], ACT.Copy)
                    af(Bh[:, g, :], ps[0:C, bank, P:P + D], ACT.Copy).then_inc(AB_ready, 1)
            act.wait_ge(AB_ps, NH)
            g, bank = NH - 1, 6 + (NH - 1) % 2
            af(A32[:, g, :], ps[:, bank, 0:C], ACT.Copy)
            af(A_hi[:, g, :], ps[:, bank, 0:C], ACT.Copy)
            af(Bh[:, g, :], ps[0:C, bank, P:P + D], ACT.Copy).then_inc(AB_ready, 1)
            for w in range(3):
                act.wait_ge(wfT_ps, w + 1)
                af(wfT[:, w * FC0:(w + 1) * FC0, :], chunks((2, 5, 6)[w], FC0), ACT.Copy).then_inc(wfT_ready, 1)
            evacuate_xT(1, 0)
            for j in range(4 * FC0):
                act.wait_ge(raw_ps, j + 1)
                dst = (g_raw, u_raw)[j // (2 * FC0)]
                af(dst[:, j // 2 % FC0, cols(j % 2)], ps[:, j % 6, :], ACT.Copy).then_inc(raw_ready, 1)
            for c in range(FC0):
                act.wait_ge(ng_ready, c + 1)
                af(sig[:, c, :], g_raw[:, c, :], ACT.Sigmoid, scale=qs[:, 1, 0:1]).then_inc(sig_ready, 1)

            def split_xT(k, bank):
                for h in range(2):
                    act.wait_ge(xT_ps, 2 * k + h + 1)
                    af(xnT_hi[:, cols(h)], ps[:, bank + h, :], ACT.Copy).then_inc(xT_hi_ready, 1)
                    if k == 3:
                        af(xnT[:, cols(h)], ps[:, bank + h, :], ACT.Copy).then_inc(xT_ready, 1)
            split_xT(2, 0)

            def queries_hi(h, buf, hf):
                act.wait_ge(q_ps, 2 * h + hf + 1)
                af(qT_hi[0:C, buf, cols(hf)], ps[0:C, 7 - hf, :], ACT.Copy).then_inc(q_hi_ready, 1)

            def max_row(h, buf, hf):
                act.wait_ge(z_ps, 2 * h + hf + 1)
                af(qT_hi[C:C + 1, buf, cols(hf)], ps[C:C + 1, 6 + hf, :], ACT.Copy).then_inc(mrow_ready, 1)

            def out_T(h, hf):
                act.wait_ge(ot_ps, 2 * h + hf + 1)
                dst = OT[:, bass.ds(h, 1), cols(hf)].rearrange("p o t -> p (o t)")
                af(dst, ps[0:C, 6, :], ACT.Copy).then_inc(ot_ready, 1)

            def head(h, buf, first=False, last=False):
                if not last:
                    queries_hi(h + 1, 1 - buf, 0)
                for t in range(2 * NB):
                    kc, hf = t // 2, t % 2
                    act.wait_ge(st_ps, 2 * NB * h + t + 1)
                    af(PT[:, buf, kc, cols(hf)], ps[:, t % 2, :], ACT.Exp, scale=SM_SCALE).then_inc(exp_ready, 1)
                    if t == 1 and not last:
                        queries_hi(h + 1, 1 - buf, 1)
                    if t == OT_AT and not first:
                        out_T(h - 1, 0)
                    if t == Z_AT and not last:
                        max_row(h + 1, 1 - buf, 0)
                        max_row(h + 1, 1 - buf, 1)
                if not first:
                    out_T(h - 1, 1)
            queries_hi(0, 0, 0)
            queries_hi(0, 0, 1)
            max_row(0, 0, 0)
            max_row(0, 0, 1)
            head(0, 0, first=True)
            with act.Fori(0, NH // 2 - 1) as i:
                head(2 * i + 1, 1)
                head(2 * i + 2, 0)
            head(NH - 1, 1, last=True)
            out_T(NH - 1, 0)
            out_T(NH - 1, 1)

            act.wait_ge(b1T_ps, 1)
            af(b1T[:, :], ps[:, 3, 0:NE * FC1], ACT.Copy).then_inc(b1T_ready, 1)
            split_xT(3, 4)

            def hidden(e, buf, s, first=False):
                hf, c = s // FC1, s % FC1
                act.wait_ge(hid_ps, 2 * FC1 * e + s + 1)
                if c == 0 and not first:
                    act.wait_ge(ey_ps, 2 * (e - 1) + hf + 1)
                af(hidT[:, hf, c, :], ps[:, s % 4, :], ACT.Gelu, bias=b1cur[:, buf, c:c + 1]).then_inc(hid_ready, 1)
            for s in range(2 * FC1):
                hidden(0, 0, s, first=True)
                if s == 2:
                    act.wait_ge(gT_ps, 1)
                    for h in range(2):
                        j = af(gatesT[:, cols(h)], ps[0:NE, 6 + h, :], ACT.Copy)
                    j.then_inc(gT_ready, 1)
            with act.Fori(0, NE // 2 - 1) as i:
                for u in (1, 2):
                    for s in range(2 * FC1):
                        hidden(2 * i + u, u % 2, s)
            for s in range(2 * FC1):
                hidden(NE - 1, 1, s)

        @block.vector
        def _(dve):
            v, count = nc.vector, [0]

            def link(ins):
                count[0] += 1
                ins.then_inc(dve_done, 1)
                dve.wait_ge(dve_done, count[0])

            def cols(h):
                return slice(h * HALF, (h + 1) * HALF)

            def layer_norm_stats(k):
                for b in range(NB):
                    if k == 0 and b % CH == 0:
                        dve.wait_ge(ld[f"x{b // CH}"], 16)
                    i = v.bn_stats(bstat[:, b, :], xs[:, b, :])
                link(i)
                for b in range(NB):
                    i = v.bn_aggr(mv[:, b, :], bstat[:, b, :])
                link(i)
                v.tensor_scalar(var_eps[:, :], mv[:, :, 1], LN_EPS, None, ALU.add).then_inc(var_ready, 1)

            def layer_norm(k):
                dve.wait_ge(rstd_ready, k + 1)
                for b in range(NB):
                    i = v.tensor_scalar(xn[:, b, :], xs[:, b, :], mv[:, b, 0:1], rstd[:, b:b + 1], ALU.subtract,
                                        ALU.mult)
                    i.then_inc(xn_ready, 1)

            v.memset(ctxT_hi[C:C + 1, :].bitcast(fp32), 1.0)
            layer_norm_stats(0)
            layer_norm(0)
            for h in range(2):
                dve.wait_ge(ctxT_ready, h + 1)
                v.tensor_tensor(ctxT_lo[:, cols(h)], ps[0:C, h, :], ctxT_hi[0:C, cols(h)].bitcast(fp32),
                                ALU.subtract).then_inc(ctxT_lo_ready, 1)

            def norms(i, bank):
                dve.wait_ge(nsq_ps, i + 1)
                v.tensor_copy(nsq[:, i, :], ps[:, bank, 0:NB]).then_inc(nsq_ready, 1)

            def clamp_norms(i):
                dve.wait_ge(rn_pow, i + 1)
                v.tensor_scalar(rn[:, i, :], rn[:, i, :], RNORM_MAX, None, ALU.min).then_inc(rn_ready, 1)
            norms(0, 2)
            clamp_norms(0)

            dve.wait_ge(ld["wf"], 48)
            w3 = wf[:, :, :, :].rearrange("p a n k -> p (a n) k")
            q3 = wf_q[:, :, :, :].rearrange("p a n k -> p (a n) k")
            link(v.tensor_reduce(wf_s[:, :], w3, AX.X, ALU.max, apply_absolute_value=True))
            link(v.tensor_scalar(wf_s[:, :], wf_s[:, :], 1.0 / WMAX, SCALE_MIN, ALU.mult, ALU.max))
            link(v.reciprocal(wf_rs[:, :], wf_s[:, :]))
            nblk = 3 * FC0 * NBLK

            def per_block(t):
                return t[:, :].rearrange("p (n o) -> p n o", o=1).to_broadcast([P, nblk, BLK])
            link(v.tensor_tensor(q3, w3, per_block(wf_rs), ALU.mult))
            link(v.tensor_scalar(q3, q3, WMAX, -WMAX - 1.0, ALU.min, ALU.max))
            link(v.tensor_scalar(q3, q3, MAGIC, MAGIC, ALU.add, ALU.subtract))
            v.tensor_tensor(q3, q3, per_block(wf_s), ALU.mult).then_inc(wq_ready, 1)

            norms(1, 7)
            clamp_norms(1)
            dve.wait_ge(rn_ready, 2)
            for h in range(2):
                dve.wait_ge(rt_ps, h + 1)
                for j in range(CH):
                    b = h * CH + j
                    i = v.tensor_scalar(cosr[:, b, :], chunks(5 + h)[:, j, :], rn[:, 1, b:b + 1], 1.0 / COS_EPS,
                                        ALU.mult, ALU.min)
                i.then_inc(cos_used, 1)
            dve.wait_ge(cos_used, 2)
            for h in range(2):
                dve.wait_ge(dots_ps, h + 1)
                i = v.tensor_tensor(cosr[:, h * CH:(h + 1) * CH, :], chunks(h), cosr[:, h * CH:(h + 1) * CH, :], ALU.mult)
            i.then_inc(x_added, 1)
            dve.wait_ge(x_added, 1)
            link(v.tensor_tensor(xs[:, :, :], xs[:, :, :], cosr, ALU.add))

            def global_max(k):
                dve.wait_ge(amT_ps, k + 1)
                link(v.tensor_reduce(qs[:, k, 7:8], ps[:, 7, 0:P], AX.X, ALU.max))

            def quant_scale(k, unit):
                if unit is None:
                    link(v.tensor_scalar(qs[:, k, 0:1], qs[:, k, 7:8], 1.0 / QMAX, SCALE_MIN, ALU.mult, ALU.max))
                    link(v.reciprocal(qs[:, k, 1:2], qs[:, k, 0:1]))
                    return
                link(v.tensor_scalar(qs[:, k, 2:3], qs[:, k, 7:8], unit, 1.0 / QMAX, ALU.mult, ALU.mult))
                link(v.tensor_scalar(qs[:, k, 0:1], qs[:, k, 2:3], SCALE_MIN, None, ALU.max))
                link(v.reciprocal(qs[:, k, 3:4], qs[:, k, 0:1]))
                link(v.tensor_scalar(qs[:, k, 1:2], qs[:, k, 3:4], unit, None, ALU.mult))

            def quantise(dst, src, k):
                link(v.tensor_scalar(dst, src, qs[:, k, 1:2], MAGIC, ALU.mult, ALU.add))
                return v.tensor_scalar(dst, dst, MAGIC, None, ALU.subtract)

            def part_max(k, c, src):
                return v.tensor_reduce(amax[:, k, c:c + 1], src, AX.X, ALU.max, apply_absolute_value=True)

            def join_max(k):
                v.tensor_reduce(amax[:, k, 3:4], amax[:, k, 0:3], AX.X, ALU.max).then_inc(am_ready, 1)

            layer_norm_stats(1)
            layer_norm(1)
            dve.wait_ge(xn_ready, 2 * NB)
            v.tensor_reduce(amax[:, 0, 3:4], xn[:, :, :], AX.XY, ALU.max, apply_absolute_value=True
                            ).then_inc(am_ready, 1)
            global_max(0)
            quant_scale(0, None)
            quantise(xn[:, :, :], xn[:, :, :], 0).then_inc(no_ready, 1)
            sx = qs[:, 0, 0:1]
            for c in range(FC0):
                dve.wait_ge(raw_ready, 2 * (c + 1))
                i = part_max(1, c, g_raw[:, c, :])
            link(i)
            join_max(1)
            global_max(1)
            quant_scale(1, sx)
            for c in range(FC0):
                quantise(g_raw[:, c, :], g_raw[:, c, :], 1).then_inc(ng_ready, 1)
            for c in range(FC0):
                dve.wait_ge(raw_ready, 2 * (FC0 + c + 1))
                i = part_max(2, c, u_raw[:, c, :])
            link(i)
            join_max(2)
            global_max(2)
            quant_scale(2, sx)
            for c in range(FC0):
                i = quantise(u_raw[:, c, :], u_raw[:, c, :], 2)
            link(i)
            for c in range(FC0):
                dve.wait_ge(sig_ready, c + 1)
                link(v.tensor_scalar(sig[:, c, :], sig[:, c, :], SIG_TOP, MAGIC16, ALU.min, ALU.add))
                link(v.tensor_scalar(sig[:, c, :], sig[:, c, :], MAGIC16, MAGIC16, ALU.max, ALU.subtract))
                link(v.tensor_tensor(gsv[:, c, :], sig[:, c, :], g_raw[:, c, :], ALU.mult))
                i = part_max(3, c, gsv[:, c, :])
            link(i)
            join_max(3)
            global_max(3)
            quant_scale(3, qs[:, 1, 0:1])
            for c in range(FC0):
                link(quantise(gsv[:, c, :], gsv[:, c, :], 3))
                link(v.tensor_tensor(gsv[:, c, :], gsv[:, c, :], u_raw[:, c, :], ALU.mult))
                i = part_max(4, c, gsv[:, c, :])
            link(i)
            join_max(4)
            global_max(4)
            link(v.tensor_scalar(qs[:, 5, 0:1], qs[:, 3, 0:1], qs[:, 2, 0:1], None, ALU.mult))
            quant_scale(4, qs[:, 5, 0:1])
            for c in range(FC0):
                quantise(gsv[:, c, :], gsv[:, c, :], 4).then_inc(no_ready, 1)
            for h in range(2):
                dve.wait_ge(down_ps, h + 1)
                i = v.scalar_tensor_tensor(out=xs[:, h * CH:(h + 1) * CH, :], in0=chunks(h), scalar=qs[:, 4, 0:1],
                                           in1=xs[:, h * CH:(h + 1) * CH, :], op0=ALU.mult, op1=ALU.add)
            i.then_inc(x_added, 1)
            dve.wait_ge(x_added, 2)

            layer_norm_stats(2)
            layer_norm(2)

            def split_xT(k, bank):
                for h in range(2):
                    dve.wait_ge(xT_hi_ready, 2 * (k - 2) + h + 1)
                    if k == 3:
                        dve.wait_ge(xT_ready, 4 + h + 1)
                    v.tensor_tensor(xnT_lo[:, cols(h)], ps[:, bank + h, :], xnT_hi[:, cols(h)].bitcast(fp32),
                                    ALU.subtract).then_inc(xT_lo_ready, 1)
            split_xT(2, 0)

            def queries_lo(h, buf, hf):
                dve.wait_ge(q_hi_ready, 2 * h + hf + 1)
                v.tensor_tensor(qT_lo[:, buf, cols(hf)], ps[0:C, 7 - hf, :], qT_hi[0:C, buf, cols(hf)].bitcast(fp32),
                                ALU.subtract).then_inc(q_lo_ready, 1)

            def tile_max(h, t):
                dve.wait_ge(max_ps, 2 * NB * h + t + 1)
                v.tensor_reduce(tmax[:, t:t + 1], ps[:, 2 + t % 2, :], AX.X, ALU.max).then_inc(max_read, 1)

            def join_tiles(h, first=False):
                dve.wait_ge(max_read, 2 * NB * (h + 1))
                if not first:
                    dve.wait_ge(z_ps, 2 * h)
                v.tensor_reduce(Z[:, C:C + NB], tmax[:, :].rearrange("p (q a) -> p q a", a=2), AX.X, ALU.max,
                                negate=True).then_inc(z_ready, 1)

            def normalise(h, hf):
                dve.wait_ge(pv_ps, 2 * h + hf + 1)
                o = ps[:, 4 + hf, 0:CH * (C + 1)].rearrange("p (q c) -> p q c", c=C + 1)
                v.reciprocal(rsum[:, hf, :].rearrange("p (q o) -> p q o", o=1), o[:, :, C:C + 1]).then_inc(rs_ready, 1)
                dve.wait_ge(rs_ready, 2 * h + hf + 1)
                v.tensor_tensor(On[:, hf * CH:(hf + 1) * CH, :], o[:, :, 0:C],
                                rsum[:, hf, :].rearrange("p (q o) -> p q o", o=1).to_broadcast([P, CH, C]),
                                ALU.mult).then_inc(on_ready, 1)

            def head(h, buf, first=False, last=False):
                t_max, n_pv = 0, 0
                if not last:
                    queries_lo(h + 1, 1 - buf, 0)
                for t in range(2 * NB):
                    if t == 1 and not last:
                        queries_lo(h + 1, 1 - buf, 1)
                    if not last:
                        for _ in range(MAX_AT[t]):
                            tile_max(h + 1, t_max)
                            t_max += 1
                    before, n_pv = n_pv, n_pv + PV_N[t]
                    if not first:
                        if before < NB * CH <= n_pv:
                            normalise(h - 1, 0)
                        if before < NB * NB <= n_pv:
                            normalise(h - 1, 1)
                    if t_max == 2 * NB and not last and MAX_AT[t]:
                        join_tiles(h + 1)
            queries_lo(0, 0, 0)
            queries_lo(0, 0, 1)
            for t in range(2 * NB):
                tile_max(0, t)
            join_tiles(0, first=True)
            head(0, 0, first=True)
            with dve.Fori(0, NH // 2 - 1) as i:
                head(2 * i + 1, 1)
                head(2 * i + 2, 0)
            head(NH - 1, 1, last=True)
            normalise(NH - 1, 0)
            normalise(NH - 1, 1)
            for h in range(2):
                dve.wait_ge(y_ps, h + 1)
                i = v.tensor_tensor(xs[:, h * CH:(h + 1) * CH, :], chunks(h), xs[:, h * CH:(h + 1) * CH, :], ALU.add)
            link(i)

            layer_norm_stats(3)
            layer_norm(3)
            split_xT(3, 4)
            dve.wait_ge(logit_ps, 1)
            link(v.tensor_copy(logit[:, :, :].rearrange("p b e -> p (b e)"), ps[:, 6, 0:NB * NE]))
            for b in range(NB):
                i = v.max(top[:, b, :], logit[:, b, :])
            link(i)
            for b in range(NB):
                i = v.max_index(topi[:, b, :], top[:, b, :], logit[:, b, :])
            v.tensor_tensor(dtop[:, :], top[:, :, 1], top[:, :, 0], ALU.subtract).then_inc(dtop_ready, 1)
            link(v.tensor_copy(iota_f[:, :], iota_i[:, :]))
            link(v.tensor_copy(topf[:, :, :], topi[:, :, :]))
            dve.wait_ge(etop_ready, 1)
            link(v.tensor_scalar(g01[:, 1, :], etop[:, :], 1.0, None, ALU.add))
            link(v.reciprocal(g01[:, 0, :], g01[:, 1, :]))
            link(v.tensor_tensor(g01[:, 1, :], etop[:, :], g01[:, 0, :], ALU.mult))

            def along_e(a):
                return a.rearrange("p (b o) -> p b o", o=1).to_broadcast([P, NB, NE])
            iota_b = iota_f[:, :].rearrange("p (o e) -> p o e", o=1).to_broadcast([P, NB, NE])
            for j, g in ((0, gate_a), (1, gate_b)):
                link(v.tensor_tensor(g[:, :, :], iota_b, topf[:, :, j:j + 1].to_broadcast([P, NB, NE]), ALU.is_equal))
                link(v.tensor_tensor(g[:, :, :], g[:, :, :], along_e(g01[:, j, :]), ALU.mult))
            v.tensor_tensor(gates[:, :, :], gate_a[:, :, :], gate_b[:, :, :], ALU.add).then_inc(gates_ready, 1)
            dve.wait_ge(gates_ready, 1)
            dve.wait_ge(b2_ps, 1)
            for h in range(2):
                i = v.tensor_tensor(xs[:, h * CH:(h + 1) * CH, :], chunks(6 + h), xs[:, h * CH:(h + 1) * CH, :], ALU.add)
            i.then_inc(ey_added, 1)

            def add_expert(e, hf, first=False):
                dve.wait_ge(ey_ps, 2 * e + hf + 1)
                dve.wait_ge(ey_added, 1 if first else 2 * e + hf)
                for j in range(CH):
                    b = hf * CH + j
                    g = gates[:, b, bass.ds(e, 1)]
                    i = v.scalar_tensor_tensor(out=xs[:, b, :], in0=chunks(4 + hf)[:, j, :], scalar=g,
                                               in1=xs[:, b, :], op0=ALU.mult, op1=ALU.add)
                i.then_inc(ey_added, 1)
            add_expert(0, 0, first=True)
            add_expert(0, 1, first=True)
            with dve.Fori(1, NE) as e:
                add_expert(e, 0)
                add_expert(e, 1)


_INS = ['x', 'ctx_768', 'L0_xattn_Wv', 'L0_xattn_bv', 'L0_xattn_Wt', 'L0_xattn_bt', 'L0_ffn_w_gate', 'L0_ffn_w_up',
        'L0_ffn_w_down', 'L1_xattn_Wq', 'L1_xattn_Wk', 'L1_xattn_Wv', 'L1_xattn_Wout', 'L1_xattn_bout',
        'L1_ffn_gate_w', 'L1_ffn_gate_b', 'L1_ffn_w1', 'L1_ffn_b1', 'L1_ffn_w2', 'L1_ffn_b2']
_OUTS = [((8, 128, 128), 'float32')]


def kernel(**inputs):
    import numpy as _np
    import concourse.bacc as _bacc
    from concourse import mybir as _mybir
    from concourse.bass_utils import run_bass_kernel_spmd as _run

    nc = _bacc.Bacc("TRN2", target_bir_lowering=False, num_devices=1)
    arrays, args = {}, []
    for name in _INS:
        a = _np.ascontiguousarray(inputs[name])
        arrays[f"in_{name}_dram"] = a
        args.append(nc.dram_tensor(f"in_{name}_dram", a.shape, _mybir.dt.from_np(a.dtype), kind="ExternalInput").ap())
    for i, (shape, dtype) in enumerate(_OUTS):
        dt = _mybir.dt.from_np(_np.dtype(dtype))
        args.append(nc.dram_tensor(f"out_{i}_dram", shape, dt, kind="ExternalOutput").ap())
    xattn_ffn_two_layers(nc, *args)
    r = _run(nc, [arrays], core_ids=[0])
    got = tuple(r.results[0][f"out_{i}_dram"] for i in range(len(_OUTS)))
    return got[0]
```

```python
import concourse.bass as bass
from concourse import mybir
from contextlib import ExitStack


def xattn_ffn_two_layers(nc, x, ctx_768, L0_xattn_Wv, L0_xattn_bv, L0_xattn_Wt, L0_xattn_bt, L0_ffn_w_gate,
                         L0_ffn_w_up, L0_ffn_w_down, L1_xattn_Wq, L1_xattn_Wk, L1_xattn_Wv, L1_xattn_Wout,
                         L1_xattn_bout, L1_ffn_gate_w, L1_ffn_gate_b, L1_ffn_w1, L1_ffn_b1, L1_ffn_w2,
                         L1_ffn_b2, out):
    fp32, fp32r, u32 = mybir.dt.float32, mybir.dt.float32r, mybir.dt.uint32
    ALU, ACT, AX = mybir.AluOpType, mybir.ActivationFunctionType, mybir.AxisListType

    P = 128
    NB, S, D = x.shape
    C = ctx_768.shape[2]
    T = NB * S
    HALF = T // 2
    CH = NB // 2
    HD = L0_xattn_Wv.shape[0]
    FC0 = L0_ffn_w_gate.shape[0] // P
    BLK = 32
    NBLK = D // BLK
    NH = L1_xattn_Wq.shape[1] // P
    DH = P
    NE, _, F1 = L1_ffn_w1.shape
    FC1 = F1 // P
    assert S == P and D == P and T == 1024 and NH % 2 == 0 and NE % 2 == 0

    LN_EPS = 1e-5
    COS_EPS = 1e-8
    RNORM_MAX = 1e30
    QMAX = 32767.0
    SCALE_MIN = 1e-12
    WMAX = 7.0
    MAGIC = 1.5 * 2.0 ** 23
    MAGIC16 = MAGIC * 2.0 ** -16
    SIG_TOP = 65535.0 / 65536.0
    SM_SCALE = 1.5 * DH ** -0.5
    E1 = 2.718281828459045

    es = ExitStack()
    with es:
        def sb(name, shape, dt=fp32):
            return es.enter_context(nc.sbuf_tensor(name, shape, dt))

        def sem(name):
            return es.enter_context(nc.semaphore(name))

        ident = sb("ident", [P, P])
        ident_r = sb("ident_r", [P, P], fp32r)
        ones = sb("ones", [P, P])
        magic = sb("magic", [P, 1])
        minus_half = sb("minus_half", [P, NB])
        base_e = sb("base_e", [P, NB])
        xs = sb("xs", [P, NB, D])
        xn = sb("xn", [P, NB, D])
        xnT = sb("xnT", [P, T])
        xnT_hi = sb("xnT_hi", [P, T], fp32r)
        xnT_lo = sb("xnT_lo", [P, T], fp32r)
        bstat = sb("bstat", [P, NB, 6])
        mv = sb("mv", [P, NB, 2])
        var_eps = sb("var_eps", [P, NB])
        rstd = sb("rstd", [P, NB])
        ctx = sb("ctx", [P, NB, C])
        CW = C + 1
        ctx_hi = sb("ctx_hi", [P, NB, CW], fp32r)
        ctx_lo = sb("ctx_lo", [P, NB, CW], fp32r)
        ctxT = sb("ctxT", [C, T])
        ctxT_hi = sb("ctxT_hi", [C + 1, T], fp32r)
        ctxT_lo = sb("ctxT_lo", [C, T], fp32r)
        wv0 = sb("wv0", [HD, D])
        wt0 = sb("wt0", [HD, C])
        bv0 = sb("bv0", [HD, 1])
        bt0 = sb("bt0", [HD, 1])
        wT0 = sb("wT0", [P, 2, HD])
        nsq = sb("nsq", [P, 2, NB])
        rn = sb("rn", [P, 2, NB])
        NWB = 3 * FC0 * NBLK
        wf = sb("wf", [P, 3, FC0 * NBLK, BLK])
        wf_s = sb("wf_s", [P, NWB])
        wf_rs = sb("wf_rs", [P, NWB])
        wfT = sb("wfT", [P, 3 * FC0, P])
        amax = sb("amax", [P, 8, 4])
        qs = sb("qs", [P, 8, 8])
        wq = sb("wq", [D, NH * DH])
        wout = sb("wout", [DH, NH, D])
        bout = sb("bout", [1, D])
        A_hi = sb("A_hi", [D, NH + 1, C], fp32r)
        A_lo = sb("A_lo", [D, NH + 1, C], fp32r)
        BW = D + 1
        Bh = sb("Bh", [C + 1, NH, BW])
        Acur_hi = sb("Acur_hi", [D, 2, C], fp32r)
        Acur_lo = sb("Acur_lo", [D, 2, C], fp32r)
        qT_hi = sb("qT_hi", [C + 1, 2, T], fp32r)
        qT_lo = sb("qT_lo", [C, 2, T], fp32r)
        tmax = sb("tmax", [P, NB])
        Z = sb("Z", [P, C + CH], fp32r)
        rsum = sb("rsum", [P, 2, CH])
        O = sb("O", [C + 1, 2, HALF])
        P_hi = sb("P_hi", [P, NB, HALF], fp32r)
        P_lo = sb("P_lo", [P, NB, HALF], fp32r)
        R = sb("R", [P, 9 * T])
        gw = sb("gw", [D, NE])
        gb = sb("gb", [1, NE])
        b1n = sb("b1n", [NE * FC1, P])
        b1T = sb("b1T", [P, NE * FC1])
        b1cur = sb("b1cur", [P, 2, FC1])
        w1 = sb("w1", [D, NE, F1])
        w2 = sb("w2", [P, NE, FC1, D])
        w1_hi = sb("w1_hi", [D, 2, F1], fp32r)
        w1_lo = sb("w1_lo", [D, 2, F1], fp32r)
        b2 = sb("b2", [NE, D])
        logit = sb("logit", [P, NB, NE])
        top = sb("top", [P, NB, 8])
        topi = sb("topi", [P, NB, 8], u32)
        topf = sb("topf", [P, NB, 8])
        iota_i = sb("iota_i", [P, NE], mybir.dt.int32)
        iota_f = sb("iota_f", [P, NE])
        dtop = sb("dtop", [P, NB])
        etop = sb("etop", [P, NB])
        g01 = sb("g01", [P, 2, NB])
        gate_a = sb("gate_a", [P, NB, NE])
        gate_b = sb("gate_b", [P, NB, NE])
        gates = sb("gates", [P, NB, NE])

        E = R[:, 0:NB * HALF].rearrange("p (n t) -> p n t", n=NB)
        hid = E
        wk, wv = R[0:C, 0:NH * DH], R[0:C, NH * DH:2 * NH * DH]
        vT, vsq, tT, tsq = (R[0:HD, (2 + i) * T:(3 + i) * T] for i in range(4))
        cosr = R[:, 6 * T:7 * T].rearrange("p (b d) -> p b d", b=NB)
        A32 = R[:, 7 * T:7 * T + NH * C].rearrange("p (h c) -> p h c", h=NH)
        hT = R[:, 8 * T:8 * T + 2 * (D + 2 * C)].rearrange("p (a c) -> p a c", a=2)
        g_raw, u_raw, sig = (R[:, i * FC0 * T:(i + 1) * FC0 * T].rearrange("p (c t) -> p c t", c=FC0)
                             for i in range(3))
        gatesT = ctxT[0:NE, :]
        ps = es.enter_context(nc.psum_tensor("ps", [P, 8, HALF], fp32))

        def chunks(bank, n=CH):
            return ps[:, bank, 0:n * P].rearrange("p (b d) -> p b d", b=n)

        ld = {n: sem("ld_" + n) for n in ("x0", "x1", "ctx", "w0", "wf", "watt", "wout", "small", "w1", "w2")}
        const_step, const_ready = sem("const_step"), sem("const_ready")
        dve_done, act_done, pool_done = sem("dve_done"), sem("act_done"), sem("pool_done")
        var_ready, rstd_ready, xn_ready = sem("var_ready"), sem("rstd_ready"), sem("xn_ready")
        xT_ps, xT_ready, xT_hi_ready, xT_lo_ready = sem("xT_ps"), sem("xT_ready"), sem("xT_hi_ready"), sem("xT_lo_ready")
        ctxT_ps, ctxT_ready, ctxT_lo_ready = sem("ctxT_ps"), sem("ctxT_ready"), sem("ctxT_lo_ready")
        wT0_ps, wT0_ready = sem("wT0_ps"), sem("wT0_ready")
        t_ps, t_ready, v_ps, v_ready = sem("t_ps"), sem("t_ready"), sem("v_ps"), sem("v_ready")
        nsq_ps, nsq_ready, rn_pow, rn_ready = sem("nsq_ps"), sem("nsq_ready"), sem("rn_pow"), sem("rn_ready")
        rt_ps, dots_ps, cos_used = sem("rt_ps"), sem("dots_ps"), sem("cos_used")
        hT_ps, hT_ready, AB_ps, AB_ready, A_lo_ready = (sem("hT_ps"), sem("hT_ready"), sem("AB_ps"), sem("AB_ready"),
                                                        sem("A_lo_ready"))
        wq_ready, wfT_ps, wfT_ready = sem("wq_ready"), sem("wfT_ps"), sem("wfT_ready")
        am_ready, amT_ps, gmax_read = sem("am_ready"), sem("amT_ps"), sem("gmax_read")
        raw_ps, raw_ready, xq_ready = sem("raw_ps"), sem("raw_ready"), sem("xq_ready")
        ng_ready, sig_ready, no_ready, down_ps, x_added = (sem("ng_ready"), sem("sig_ready"), sem("no_ready"),
                                                           sem("down_ps"), sem("x_added"))
        Acur_ready, q_ps, q_hi_ready, q_lo_ready = sem("Acur_ready"), sem("q_ps"), sem("q_hi_ready"), sem("q_lo_ready")
        max_ps, max_read, z_ready, z_ps, mrow_ready = (sem("max_ps"), sem("max_read"), sem("z_ready"), sem("z_ps"),
                                                       sem("mrow_ready"))
        st_ps, exp_ready, pv_ps, o_ready = sem("st_ps"), sem("exp_ready"), sem("pv_ps"), sem("o_ready")
        y_ps, rs_ready, y_added = sem("y_ps"), sem("rs_ready"), sem("y_added")
        bout_ps, bout_added = sem("bout_ps"), sem("bout_added")
        b1T_ps, b1T_ready, logit_ps, logit_read = sem("b1T_ps"), sem("b1T_ready"), sem("logit_ps"), sem("logit_read")
        dtop_ready, etop_ready, gates_ready, gT_ps, gT_ready, b2_ps = (
            sem("dtop_ready"), sem("etop_ready"), sem("gates_ready"), sem("gT_ps"), sem("gT_ready"), sem("b2_ps"))
        p_hi_dve, p_lo_dve, p_lo_pool = sem("p_hi_dve"), sem("p_lo_dve"), sem("p_lo_pool")
        ctx_split, ident_r_ready, inv_ready, vq_ready, stats_in = (sem("ctx_split"), sem("ident_r_ready"),
                                                                   sem("inv_ready"), sem("vq_ready"), sem("stats_in"))
        w_split, hid_ps, hid_ready, ey_ps, ey_added = (sem("w_split"), sem("hid_ps"), sem("hid_ready"), sem("ey_ps"),
                                                        sem("ey_added"))
        out_stored = sem("out_stored")

        block = es.enter_context(nc.Block())

        LAG = 3
        MAX_AT = [1, 1, 2, 1, 2, 1, 0, 0]
        FIRST_MAX_BANKS = (2, 3, 5, 7)
        Z_AT = 6
        O_AT = 3
        Y_AT = 5
        assert sum(MAX_AT) == 2 * CH and len(MAX_AT) == NB and LAG <= O_AT < Y_AT
        HI_DVE = (0, 2, 4, 6)
        LO_DVE = (3, 7)
        HI_ACT = tuple(t for t in range(NB) if t not in HI_DVE)
        LO_POOL = tuple(t for t in range(NB) if t not in LO_DVE)

        @block.sync
        def _(sp):
            def load(dst, src, s):
                sp.dma_start(dst, src).then_inc(s, 16)
            for h in range(2):
                load(xs[:, h * CH:(h + 1) * CH, :], x[h * CH:(h + 1) * CH].rearrange("b s d -> s b d"), ld[f"x{h}"])
            load(wt0[:, :], L0_xattn_Wt, ld["w0"])
            load(wv0[:, :], L0_xattn_Wv, ld["w0"])
            load(bt0[:, :], L0_xattn_bt.rearrange("(h o) -> h o", o=1), ld["w0"])
            load(bv0[:, :], L0_xattn_bv.rearrange("(h o) -> h o", o=1), ld["w0"])
            for i, w in enumerate((L0_ffn_w_gate, L0_ffn_w_up)):
                load(wf[:, i, :, :].rearrange("p (c n) k -> p c (n k)", c=FC0),
                     w.rearrange("(c p) d -> p c d", p=P), ld["wf"])
            load(wf[:, 2, :, :].rearrange("p n k -> p (n k)"), L0_ffn_w_down, ld["wf"])
            load(wout[:, :, :], L1_xattn_Wout.rearrange("(h j) d -> j h d", j=DH), ld["wout"])
            load(bout[:, :], L1_xattn_bout.rearrange("(o d) -> o d", o=1), ld["small"])
            load(gw[:, :], L1_ffn_gate_w, ld["small"])
            load(gb[:, :], L1_ffn_gate_b.rearrange("(o d) -> o d", o=1), ld["small"])
            load(b1n[:, :], L1_ffn_b1.rearrange("e (c p) -> (e c) p", p=P), ld["small"])
            load(b2[:, :], L1_ffn_b2, ld["small"])

            load(w1[:, :, :], L1_ffn_w1.rearrange("e d f -> d e f"), ld["w1"])
            for e in range(NE):
                load(w2[:, e, :, :], L1_ffn_w2[e].rearrange("(c p) d -> p c d", p=P), ld["w2"])
            for h in range(2):
                sp.wait_ge(ey_added, 2 * (NE - 1) + h + 2)
                sp.dma_start(out[h * CH:(h + 1) * CH].rearrange("b s d -> s b d"), xs[:, h * CH:(h + 1) * CH, :]
                             ).then_inc(out_stored, 16)
            sp.wait_ge(out_stored, 32)

        @block.gpsimd
        def _(pool):
            nc.gpsimd.memset(ident[:, :], 0.0)
            nc.gpsimd.memset(ones[:, :], 1.0)
            nc.gpsimd.memset(magic[:, :], MAGIC)
            nc.gpsimd.memset(minus_half[:, :], -0.5)
            nc.gpsimd.memset(base_e[:, :], E1)
            nc.gpsimd.memset(ctx_hi[:, :, C:C + 1].bitcast(fp32), 1.0)
            nc.gpsimd.memset(ctx_lo[:, :, C:CW].bitcast(fp32), 0.0)
            nc.gpsimd.memset(Z[:, :].bitcast(fp32), 0.0)
            nc.gpsimd.memset(A_hi[:, NH, :].bitcast(fp32), 0.0)
            nc.gpsimd.memset(A_lo[:, NH, :].bitcast(fp32), 0.0)
            nc.gpsimd.iota(iota_i[:, :], [[1, NE]], base=0, channel_multiplier=0).then_inc(const_step, 1)
            pool.wait_ge(const_step, 1)
            nc.gpsimd.affine_select(out=ident[:, :], in_=ident[:, :], compare_op=ALU.not_equal, fill=1.0, base=0,
                                    pattern=[[-1, P]], channel_multiplier=1).then_inc(const_ready, 1)

            def rstd_pow(k):
                b = slice(0, NB) if k < 2 else slice((k % 2) * CH, (k % 2 + 1) * CH)
                pool.wait_ge(var_ready, k + 1)
                nc.gpsimd.tensor_tensor(out=rstd[:, b], in0=var_eps[:, b], in1=minus_half[:, b],
                                        op=ALU.pow).then_inc(rstd_ready, 1)

            def norm_pow(i):
                pool.wait_ge(nsq_ready, i + 1)
                nc.gpsimd.tensor_tensor(out=rn[:, i, :], in0=nsq[:, i, :], in1=minus_half[:, 0:NB],
                                        op=ALU.pow).then_inc(rn_pow, 1)

            rstd_pow(0)
            norm_pow(0)
            norm_pow(1)
            pool.wait_ge(ld["ctx"], 16)
            nc.gpsimd.tensor_copy(ctx_hi[:, :, 0:C], ctx[:, :, :]).then_inc(ctx_split, 1)
            pool.wait_ge(ctx_split, 1)
            nc.gpsimd.tensor_tensor(out=ctx_lo[:, :, 0:C], in0=ctx[:, :, :], in1=ctx_hi[:, :, 0:C].bitcast(fp32),
                                    op=ALU.subtract).then_inc(ctx_split, 1)
            rstd_pow(1)
            pool.wait_ge(AB_ready, NH)
            nc.gpsimd.tensor_tensor(out=A_lo[:, 0:NH, :], in0=A32, in1=A_hi[:, 0:NH, :].bitcast(fp32),
                                    op=ALU.subtract).then_inc(A_lo_ready, 1)

            def stage_A(h, buf):
                src_hi = A_hi[:, bass.ds(h, 1), :].rearrange("p o c -> p (o c)").bitcast(fp32)
                src_lo = A_lo[:, bass.ds(h, 1), :].rearrange("p o c -> p (o c)").bitcast(fp32)
                nc.gpsimd.tensor_copy(Acur_hi[:, buf, :], src_hi)
                nc.gpsimd.tensor_copy(Acur_lo[:, buf, :], src_lo).then_inc(Acur_ready, 1)
            pool.wait_ge(A_lo_ready, 1)
            stage_A(0, 0)
            stage_A(1, 1)
            pool.wait_ge(b1T_ready, 1)
            nc.gpsimd.tensor_copy(b1cur[:, :, :].rearrange("p a c -> p (a c)"), b1T[:, 0:2 * FC1])
            pool.wait_ge(ld["w1"], 16)
            nc.gpsimd.tensor_copy(w1_hi[:, :, :], w1[:, 0:2, :]).then_inc(w_split, 1)
            pool.wait_ge(w_split, 1)
            nc.gpsimd.tensor_tensor(out=w1_lo[:, :, :], in0=w1[:, 0:2, :], in1=w1_hi[:, :, :].bitcast(fp32),
                                    op=ALU.subtract).then_inc(w_split, 1)
            rstd_pow(2)
            rstd_pow(3)

            def exp_lo(u, t):
                n = NB * u + t
                if t in HI_DVE:
                    pool.wait_ge(p_hi_dve, len(HI_DVE) * u + HI_DVE.index(t) + 1)
                else:
                    pool.wait_ge(exp_ready, n + 1)
                nc.gpsimd.tensor_tensor(out=P_lo[:, t, :], in0=E[:, t, :], in1=P_hi[:, t, :].bitcast(fp32),
                                        op=ALU.subtract).then_inc(p_lo_pool, 1)

            def head(h, buf, stage=True):
                for f in range(2):
                    for t in LO_POOL:
                        if f == 0 and t == LO_POOL[2] and stage:
                            pool.wait_ge(q_ps, 2 * h + 2)
                        exp_lo(2 * h + f, t)
                        if f == 0 and t == LO_POOL[2] and stage:
                            stage_A(h + 2, buf)
            head(0, 0)
            with pool.Fori(0, NH // 2 - 1) as i:
                head(2 * i + 1, 1)
                head(2 * i + 2, 0)
            head(NH - 1, 1, stage=False)

            rstd_pow(4)
            rstd_pow(5)
            pool.wait_ge(dtop_ready, 1)
            nc.gpsimd.tensor_tensor(out=etop[:, :], in0=base_e[:, :], in1=dtop[:, :], op=ALU.pow
                                    ).then_inc(etop_ready, 1)

        @block.tensor
        def _(pe):
            mm, tr = nc.tensor.matmul, nc.tensor.transpose

            def transpose_half(k, h, bank):
                for j in range(CH):
                    pe.wait_ge(xn_ready, NB * k + CH * h + j + 1)
                    i = tr(ps[:, bank, j * P:(j + 1) * P], xn[:, CH * h + j, :], ident[:, :])
                i.then_inc(xT_ps, 1)

            pe.wait_ge(const_ready, 1)
            pe.wait_ge(ld["ctx"], 16)
            for b in range(NB):
                i = tr(ps[0:C, b // CH, (b % CH) * P:(b % CH + 1) * P], ctx[:, b, :], ident[:, :])
                if b % CH == CH - 1:
                    i.then_inc(ctxT_ps, 1)
            pe.wait_ge(ld["w0"], 64)
            tr(ps[0:C, 2, 0:HD], wt0[:, :], ident[0:HD, 0:HD])
            tr(ps[0:D, 2, HD:2 * HD], wv0[:, :], ident[0:HD, 0:HD]).then_inc(wT0_ps, 1)
            pe.wait_ge(wT0_ready, 1)
            for h in range(2):
                pe.wait_ge(ctxT_ready, h + 1)
                mm(ps[0:HD, 3 + h, :], wT0[0:C, 0, :], ctxT[:, h * HALF:(h + 1) * HALF], start=True, stop=True
                   ).then_inc(t_ps, 1)
            for h in range(2):
                transpose_half(0, h, 5 + h)

            def squared_norms(i, sq, bank):
                for b in range(NB):
                    j = mm(ps[:, bank, b:b + 1], sq[:, b * P:(b + 1) * P], ones[0:HD, 0:1],
                           start=True, stop=True)
                j.then_inc(nsq_ps, 1)
            pe.wait_ge(t_ready, 2)
            for h in range(2):
                pe.wait_ge(xT_ready, h + 1)
                mm(ps[0:HD, 3 + h, :], wT0[:, 1, :], xnT[:, h * HALF:(h + 1) * HALF], start=True, stop=True
                   ).then_inc(v_ps, 1)
            squared_norms(0, tsq, 2)
            pe.wait_ge(v_ready, 2)
            squared_norms(1, vsq, 7)
            for b in range(NB):
                i = mm(ps[:, 5 + b // CH, (b % CH) * P:(b % CH + 1) * P], vT[:, b * P:(b + 1) * P],
                       tT[:, b * P:(b + 1) * P], start=True, stop=True)
                if b % CH == CH - 1:
                    i.then_inc(dots_ps, 1)
            pe.wait_ge(rn_ready, 1)
            pe.wait_ge(ctxT_lo_ready, 2)
            for b in range(NB):
                i = mm(ps[:, b // CH, (b % CH) * P:(b % CH + 1) * P], rn[:, 0, b:b + 1].to_broadcast([P, P]),
                       ident[:, :], start=True, stop=True)
                if b % CH == CH - 1:
                    i.then_inc(rt_ps, 1)

            pe.wait_ge(ld["watt"], 48)
            pe.wait_ge(ld["wout"], 16)

            def head_transposes(h):
                if h >= 2:
                    pe.wait_ge(hT_ready, h - 1)
                bank = 3 + h % 2
                cols = slice(h * DH, (h + 1) * DH)
                tr(ps[:, bank, 0:D], wq[:, cols], ident[:, :])
                tr(ps[:, bank, D:D + C], wk[:, cols], ident[0:C, 0:C])
                tr(ps[:, bank, D + C:D + 2 * C], wv[:, cols], ident[0:C, 0:C]).then_inc(hT_ps, 1)

            def head_products(h):
                pe.wait_ge(hT_ready, h + 1)
                if h < 2:
                    pe.wait_ge(nsq_ready, h + 1)
                else:
                    pe.wait_ge(AB_ready, h - 1)
                bank, w = (2, 7)[h % 2], hT[:, h % 2, :]
                mm(ps[:, bank, 0:C], w[:, 0:D], w[:, D:D + C], start=True, stop=True)
                mm(ps[0:C, bank, P:P + D], w[:, D + C:D + 2 * C], wout[:, h, :], start=True, stop=True
                   ).then_inc(AB_ps, 1)
            head_transposes(0)
            for h in range(NH):
                if h + 1 < NH:
                    head_transposes(h + 1)
                head_products(h)

            pe.wait_ge(wq_ready, 1)
            pe.wait_ge(AB_ready, NH)
            for j in range(3 * FC0):
                w, c = j // FC0, j % FC0
                i = tr(ps[:, (3, 4, 2)[w], c * P:(c + 1) * P],
                       wf[:, w, c * NBLK:(c + 1) * NBLK, :].rearrange("p n k -> p (n k)"), ident[:, :])
                if c == FC0 - 1:
                    i.then_inc(wfT_ps, 1)
            pe.wait_ge(ld["small"], 80)
            tr(ps[:, 7, 0:NE * FC1], b1n[:, :], ident[0:NE * FC1, 0:NE * FC1]).then_inc(b1T_ps, 1)
            pe.wait_ge(b1T_ready, 1)

            def spread_max(k):
                pe.wait_ge(am_ready, k + 1)
                mm(ps[:, 7, 0:P], amax[:, k, 3:4].to_broadcast([P, P]), ident[:, :], start=True, stop=True
                   ).then_inc(amT_ps, 1)
            spread_max(0)
            pe.wait_ge(x_added, 1)
            for b in range(NB):
                if b % CH == 0:
                    pe.wait_ge(xq_ready, b // CH + 1)
                i = tr(ps[:, 5 + b // CH, (b % CH) * P:(b % CH + 1) * P], xn[:, b, :], ident[:, :])
                if b % CH == CH - 1:
                    i.then_inc(xT_ps, 1)
            for j in range(4 * FC0):
                w, c, h = j // (2 * FC0), j // 2 % FC0, j % 2
                if j < 2:
                    pe.wait_ge(xT_ready, 2 + h + 1)
                    pe.wait_ge(wfT_ready, j + 1)
                if j == 2:
                    pe.wait_ge(wfT_ready, 3)
                if j >= 5:
                    pe.wait_ge(raw_ready, j - 4)
                mm(ps[:, j % 5, :], wfT[:, w * FC0 + c, :], xnT[:, h * HALF:(h + 1) * HALF], start=True, stop=True
                   ).then_inc(raw_ps, 1)
                if j == 8:
                    spread_max(1)
            for k in (2, 3, 4):
                spread_max(k)
            for b in range(NB):
                if b % CH == 0:
                    pe.wait_ge(no_ready, b // CH + 1)
                for c in range(FC0):
                    i = mm(ps[:, 5 + b // CH, (b % CH) * P:(b % CH + 1) * P], sig[:, c, b * P:(b + 1) * P],
                           wfT[:, 2 * FC0 + c, :], start=(c == 0), stop=(c == FC0 - 1))
                if b % CH == CH - 1:
                    i.then_inc(down_ps, 1)

            pe.wait_ge(raw_ready, 4 * FC0)
            mm(ps[:, 4, 0:D], ones[0:1, :], bout[:, :], start=True, stop=True).then_inc(bout_ps, 1)

            def project(head, f, hb):
                if f == 0:
                    pe.wait_ge(Acur_ready, head + 1)
                cols = slice(f * HALF, (f + 1) * HALF)
                o = ps[0:C, 6, :]
                mm(o, Acur_hi[:, hb, :], xnT_hi[:, cols], start=True, stop=False)
                mm(o, Acur_hi[:, hb, :], xnT_lo[:, cols], start=False, stop=False)
                mm(o, Acur_lo[:, hb, :], xnT_hi[:, cols], start=False, stop=True).then_inc(q_ps, 1)

            def max_tile(u, f, hb, n, first=False):
                qc, kh = n // 2, n % 2
                if n == 0:
                    pe.wait_ge(q_hi_ready, u + 1)
                if first and n >= len(FIRST_MAX_BANKS):
                    pe.wait_ge(max_read, n - len(FIRST_MAX_BANKS) + 1)
                if not first:
                    pe.wait_ge(max_read, 2 * CH * u + n - 1)
                q0 = f * HALF + qc * P
                mm(ps[:, FIRST_MAX_BANKS[n % 4] if first else 2 + n % 2, :], qT_hi[0:C, hb, q0:q0 + P], ctxT_hi[0:C, kh * HALF:(kh + 1) * HALF],
                   start=True, stop=True).then_inc(max_ps, 1)

            def max_row(u):
                pe.wait_ge(z_ready, u + 1)
                for qc in range(CH):
                    i = mm(ps[0:C + 1, 7, qc * P:(qc + 1) * P], Z[:, qc:qc + C + 1], ident_r[:, :], start=True,
                           stop=True)
                i.then_inc(z_ps, 1)

            def score_tile(u, f, hb, t, first=False):
                if t == 0:
                    pe.wait_ge(mrow_ready, u + 1)
                    pe.wait_ge(q_lo_ready, u + 1)
                if not (first and t < 2):
                    pe.wait_ge(exp_ready, NB * u + t - 1)
                k, q, o = slice(t * P, (t + 1) * P), slice(f * HALF, (f + 1) * HALF), ps[:, t % 2, :]
                mm(o, ctxT_hi[:, k], qT_hi[:, hb, q], start=True, stop=False)
                mm(o, ctxT_hi[0:C, k], qT_lo[:, hb, q], start=False, stop=False)
                mm(o, ctxT_lo[:, k], qT_hi[0:C, hb, q], start=False, stop=True).then_inc(st_ps, 1)

            def output_chunk(u, f, t):
                if t in LO_DVE:
                    pe.wait_ge(p_lo_dve, len(LO_DVE) * u + LO_DVE.index(t) + 1)
                else:
                    pe.wait_ge(p_lo_pool, len(LO_POOL) * u + LO_POOL.index(t) + 1)
                o = ps[0:CW, 4 + f, :]
                mm(o, ctx_hi[:, t, :], P_hi[:, t, :], start=(t == 0), stop=False)
                mm(o, ctx_lo[:, t, :], P_hi[:, t, :], start=False, stop=False)
                mm(o, ctx_hi[:, t, :], P_lo[:, t, :], start=False, stop=(t == NB - 1)).then_inc(pv_ps, 1)

            def y_place(f, j):
                return ps[:, 4 + f, j * BW:(j + 1) * BW] if j < CH - 1 else ps[:, 6, 0:BW]

            def project_out(u, head, f):
                pe.wait_ge(o_ready, u + 1)
                for j in range(CH):
                    i = mm(y_place(f, j), O[:, f, j * P:(j + 1) * P], Bh[:, bass.ds(head, 1), :].rearrange("p o d -> p (o d)"),
                           start=True, stop=True)
                i.then_inc(y_ps, 1)

            def unit(u, head, f, hb, first=False, second=False, n_next=2):
                n_max = 0
                for t in range(NB):
                    score_tile(u, f, hb, t, first)
                    if t == 0 and n_next == 2:
                        pe.wait_ge(q_lo_ready, u + 2)
                        if not (first or second):
                            pe.wait_ge(y_added, u - 1)
                        project(head + 1, f, 1 - hb)
                    if t == LAG and first:
                        pe.wait_ge(bout_added, 1)
                    if t == LAG and not (first or second):
                        pe.wait_ge(y_added, u - 1)
                    for k in range(2):
                        if n_next >= 1 and k < MAX_AT[t]:
                            max_tile(u + 1, 1 - f, hb if f == 0 else 1 - hb, n_max)
                            n_max += 1
                        if k == 0 and t >= LAG:
                            output_chunk(u, f, t - LAG)
                        elif k == 0 and not first:
                            output_chunk(u - 1, 1 - f, t - LAG + NB)
                    if n_next >= 1 and t == Z_AT:
                        max_row(u + 1)
                    if t == Y_AT and not first:
                        if n_next == 2:
                            pe.wait_ge(q_lo_ready, u + 3)
                        project_out(u - 1, head if f == 1 else head - 1, 1 - f)

            transpose_half(2, 0, 0)
            pe.wait_ge(ctx_split, 2)
            pe.wait_ge(xT_lo_ready, 1)
            pe.wait_ge(x_added, 3)
            project(0, 0, 0)
            transpose_half(2, 1, 1)
            for n in range(2 * CH):
                max_tile(0, 0, 0, n, first=True)
            pe.wait_ge(xT_lo_ready, 2)
            pe.wait_ge(q_lo_ready, 1)
            project(0, 1, 0)
            pe.wait_ge(ident_r_ready, 1)
            max_row(0)
            unit(0, 0, 0, 0, first=True)
            unit(1, 0, 1, 0, second=True)
            with pe.Fori(0, NH // 2 - 1) as i:
                for k in range(4):
                    unit(4 * i + 2 + k, 2 * i + 1 + k // 2, k % 2, (k // 2 + 1) % 2)
            unit(2 * NH - 2, NH - 1, 0, 1, n_next=1)
            unit(2 * NH - 1, NH - 1, 1, 1, n_next=0)
            for t in range(NB - LAG, NB):
                output_chunk(2 * NH - 1, 1, t)
            transpose_half(3, 0, 7)
            project_out(2 * NH - 1, NH - 1, 1)

            def router():
                pe.wait_ge(xT_ready, 6)
                pe.wait_ge(xT_lo_ready, 3)
                for b in range(NB):
                    o = ps[:, 7, b * NE:(b + 1) * NE]
                    mm(o, xnT[:, b * P:(b + 1) * P], gw[:, :], start=True, stop=False)
                    i = mm(o, ones[0:1, :], gb[:, :], start=False, stop=True)
                i.then_inc(logit_ps, 1)

            def transpose_gates():
                pe.wait_ge(gates_ready, 1)
                for b in range(NB):
                    i = tr(ps[0:NE, 6 + b // CH, (b % CH) * P:(b % CH + 1) * P], gates[:, b, :], ident[:, :])
                i.then_inc(gT_ps, 1)

            def gate_bias():
                pe.wait_ge(gT_ready, 1)
                for b in range(NB):
                    i = mm(ps[:, 6 + b // CH, (b % CH) * P:(b % CH + 1) * P], gatesT[:, b * P:(b + 1) * P], b2[:, :],
                           start=True, stop=True)
                i.then_inc(b2_ps, 1)

            def hidden_tile(e, buf, s, first=False):
                hf, c = s // FC1, s % FC1
                if s == 0:
                    pe.wait_ge(w_split, 2 if first else 2 * e)
                if not (first and s < 4):
                    pe.wait_ge(hid_ready, 2 * FC1 * e + s - 3)
                f, t = slice(c * P, (c + 1) * P), slice(hf * HALF, (hf + 1) * HALF)
                o = ps[:, s % 4, :]
                mm(o, w1_hi[:, buf, f], xnT_hi[:, t], start=True, stop=False)
                mm(o, w1_hi[:, buf, f], xnT_lo[:, t], start=False, stop=False)
                mm(o, w1_lo[:, buf, f], xnT_hi[:, t], start=False, stop=True).then_inc(hid_ps, 1)

            def expert_out(e, hf, j, bank_read=None):
                if j == 0:
                    pe.wait_ge(hid_ready, 2 * FC1 * e + FC1 * (hf + 1))
                    if bank_read is not None:
                        pe.wait_ge(ey_added, bank_read)
                for c in range(FC1):
                    i = mm(ps[:, 4 + hf, j * P:(j + 1) * P], hid[:, hf * FC1 + c, j * P:(j + 1) * P],
                           w2[:, bass.ds(e, 1), c, :].rearrange("p o d -> p (o d)"), start=(c == 0), stop=(c == FC1 - 1))
                if j == CH - 1:
                    i.then_inc(ey_ps, 1)

            def expert(e, buf, reads=None):
                for s in range(2 * FC1):
                    hidden_tile(e, buf, s)
                    if s < FC1:
                        expert_out(e - 1, 1, s, 2 * (e - 1) + 1 if reads is None else reads[0])
                    else:
                        expert_out(e, 0, s - FC1, 2 * e if reads is None else reads[1])
                    if reads is not None and s == FC1 - 1:
                        transpose_gates()
                    if reads is not None and s == FC1 + 1:
                        gate_bias()
            pe.wait_ge(ld["w2"], 16 * NE)
            pe.wait_ge(xT_lo_ready, 3)
            pe.wait_ge(exp_ready, 2 * NH * NB)
            pe.wait_ge(max_read, 2 * NH * 2 * CH)
            for s in range(FC1):
                hidden_tile(0, 0, s, first=True)
            transpose_half(3, 1, 6)
            for j in range(CH):
                expert_out(0, 0, j)
            router()
            pe.wait_ge(xT_lo_ready, 4)
            for s in range(FC1, 2 * FC1):
                hidden_tile(0, 0, s)
            expert(1, 1, reads=(None, 1))
            with pe.Fori(0, NE // 2 - 1) as i:
                expert(2 * i + 2, 0)
                expert(2 * i + 3, 1)
            for j in range(CH):
                expert_out(NE - 1, 1, j, 2 * (NE - 1) + 1)

        @block.scalar
        def _(act):
            af, count = nc.scalar.activation, [0]

            def link(ins):
                count[0] += 1
                ins.then_inc(act_done, 1)
                act.wait_ge(act_done, count[0])

            act.dma_start(ctx[:, :, :], ctx_768.rearrange("b s c -> s b c")).then_inc(ld["ctx"], 16)
            act.dma_start(wq[:, :], L1_xattn_Wq).then_inc(ld["watt"], 16)
            act.dma_start(wk, L1_xattn_Wk).then_inc(ld["watt"], 16)
            act.dma_start(wv, L1_xattn_Wv).then_inc(ld["watt"], 16)

            def cols(h):
                return slice(h * HALF, (h + 1) * HALF)
            act.wait_ge(const_ready, 1)
            af(ident_r[:, :], ident[:, :], ACT.Copy).then_inc(ident_r_ready, 1)
            for h in range(2):
                act.wait_ge(ctxT_ps, h + 1)
                af(ctxT[:, cols(h)], ps[0:C, h, :], ACT.Copy)
                af(ctxT_hi[0:C, cols(h)], ps[0:C, h, :], ACT.Copy).then_inc(ctxT_ready, 1)
            act.wait_ge(wT0_ps, 1)
            af(wT0[0:C, 0, :], ps[0:C, 2, 0:HD], ACT.Copy)
            af(wT0[:, 1, :], ps[:, 2, HD:2 * HD], ACT.Copy).then_inc(wT0_ready, 1)

            def with_bias(src_ps, bias, dst, dst_sq, ready):
                for h in range(2):
                    act.wait_ge(src_ps, h + 1)
                    af(dst[:, cols(h)], ps[0:HD, 3 + h, :], ACT.Identity, bias=bias[:, 0:1])
                    af(dst_sq[:, cols(h)], ps[0:HD, 3 + h, :], ACT.Square, bias=bias[:, 0:1]).then_inc(ready, 1)

            def evacuate_xT(k, bank, plain=True):
                for h in range(2):
                    act.wait_ge(xT_ps, 2 * k + h + 1)
                    af(xnT[:, cols(h)], ps[:, bank + h, :], ACT.Copy).then_inc(xT_ready, 1)
            with_bias(t_ps, bt0, tT, tsq, t_ready)
            evacuate_xT(0, 5)
            with_bias(v_ps, bv0, vT, vsq, v_ready)

            def keep_products(h):
                act.wait_ge(AB_ps, h + 1)
                bank = (2, 7)[h % 2]
                af(A32[:, h, :], ps[:, bank, 0:C], ACT.Copy)
                af(A_hi[:, h, :], ps[:, bank, 0:C], ACT.Copy)
                af(Bh[0:C, h, 0:D], ps[0:C, bank, P:P + D], ACT.Copy).then_inc(AB_ready, 1)
            for h in range(NH):
                act.wait_ge(hT_ps, h + 1)
                if h >= 2:
                    act.wait_ge(AB_ps, h - 1)
                af(hT[:, h % 2, :], ps[:, 3 + h % 2, 0:D + 2 * C], ACT.Copy).then_inc(hT_ready, 1)
                if h >= 1:
                    keep_products(h - 1)
            keep_products(NH - 1)
            for w in range(3):
                act.wait_ge(wfT_ps, w + 1)
                af(wfT[:, w * FC0:(w + 1) * FC0, :], chunks((3, 4, 2)[w], FC0), ACT.Copy).then_inc(wfT_ready, 1)
            act.wait_ge(b1T_ps, 1)
            af(b1T[:, :], ps[:, 7, 0:NE * FC1], ACT.Copy).then_inc(b1T_ready, 1)
            evacuate_xT(1, 5)
            for j in range(4 * FC0):
                act.wait_ge(raw_ps, j + 1)
                dst = (g_raw, u_raw)[j // (2 * FC0)]
                af(dst[:, j // 2 % FC0, cols(j % 2)], ps[:, j % 5, :], ACT.Copy).then_inc(raw_ready, 1)

            def first_quant_step(k, t):
                af(t, t, ACT.Identity, bias=magic[:, 0:1], scale=qs[:, k, 1:2]).then_inc(vq_ready, 1)
            act.wait_ge(A_lo_ready, 1)
            for c in range(FC0):
                act.wait_ge(ng_ready, c + 1)
                af(sig[:, c, :], g_raw[:, c, :], ACT.Sigmoid, scale=qs[:, 1, 0:1]).then_inc(sig_ready, 1)
            act.wait_ge(inv_ready, 1)
            for c in range(FC0):
                first_quant_step(2, u_raw[:, c, :])
            act.wait_ge(inv_ready, 2)
            for c in range(1, FC0):
                first_quant_step(3, sig[:, c, :])
            act.wait_ge(inv_ready, 3)
            first_quant_step(4, sig[:, :, cols(1)])

            def split_xT(k, h, bank):
                act.wait_ge(xT_ps, 2 * k + h + 1)
                af(xnT_hi[:, cols(h)], ps[:, bank, :], ACT.Copy).then_inc(xT_hi_ready, 1)
                if k == 3:
                    af(xnT[:, cols(h)], ps[:, bank, :], ACT.Copy).then_inc(xT_ready, 1)
            nc.scalar.preload_act_table(ACT.Exp)
            split_xT(2, 0, 0)

            def queries_hi(u, f, hb):
                act.wait_ge(q_ps, u + 1)
                af(qT_hi[0:C, hb, cols(f)], ps[0:C, 6, :], ACT.Copy).then_inc(q_hi_ready, 1)

            def max_row(u, f, hb):
                act.wait_ge(z_ps, u + 1)
                af(qT_hi[C:C + 1, hb, cols(f)], ps[C:C + 1, 7, :], ACT.Copy).then_inc(mrow_ready, 1)

            def take_output(u, f):
                act.wait_ge(pv_ps, NB * (u + 1))
                af(O[:, f, :], ps[0:CW, 4 + f, :], ACT.Copy).then_inc(o_ready, 1)

            def unit(u, f, hb, first=False, n_next=2):
                for t in range(NB):
                    act.wait_ge(st_ps, NB * u + t + 1)
                    if not first:
                        act.wait_ge(pv_ps, NB * (u - 1) + t + 1)
                    i = af(E[:, t, :], ps[:, t % 2, :], ACT.Exp, scale=SM_SCALE)
                    if t in HI_ACT:
                        i = af(P_hi[:, t, :], ps[:, t % 2, :], ACT.Exp, scale=SM_SCALE)
                    i.then_inc(exp_ready, 1)
                    if t == 1 and n_next == 2:
                        queries_hi(u + 2, f, 1 - hb)
                    if t == O_AT and not first:
                        take_output(u - 1, 1 - f)
                    if t == Z_AT and n_next >= 1:
                        max_row(u + 1, 1 - f, hb if f == 0 else 1 - hb)
            queries_hi(0, 0, 0)
            split_xT(2, 1, 1)
            queries_hi(1, 1, 0)
            max_row(0, 0, 0)
            unit(0, 0, 0, first=True)
            unit(1, 1, 0)
            with act.Fori(0, NH // 2 - 1) as i:
                for k in range(4):
                    unit(4 * i + 2 + k, k % 2, (k // 2 + 1) % 2)
            unit(2 * NH - 2, 0, 1, n_next=1)
            unit(2 * NH - 1, 1, 1, n_next=0)
            nc.scalar.preload_act_table(ACT.Gelu)
            take_output(2 * NH - 1, 1)

            split_xT(3, 0, 7)

            def hidden(e, buf, s, first=False):
                hf, c = s // FC1, s % FC1
                act.wait_ge(hid_ps, 2 * FC1 * e + s + 1)
                if c == 0 and not first:
                    act.wait_ge(ey_ps, 2 * (e - 1) + hf + 1)
                af(hid[:, s, :], ps[:, s % 4, :], ACT.Gelu, bias=b1cur[:, buf, c:c + 1]
                   ).then_inc(hid_ready, 1)
            for s in range(FC1):
                hidden(0, 0, s, first=True)
            split_xT(3, 1, 6)
            for s in range(FC1, 2 * FC1):
                hidden(0, 0, s, first=True)
            for s in range(FC1):
                hidden(1, 1, s)
            act.wait_ge(gT_ps, 1)
            for h in range(2):
                j = af(gatesT[:, cols(h)], ps[0:NE, 6 + h, :], ACT.Copy)
            j.then_inc(gT_ready, 1)
            for s in range(FC1, 2 * FC1):
                hidden(1, 1, s)
            with act.Fori(0, NE // 2 - 1) as i:
                for buf in range(2):
                    for s in range(2 * FC1):
                        hidden(2 * i + 2 + buf, buf, s)

        @block.vector
        def _(dve):
            v, count = nc.vector, [0]

            def link(ins):
                count[0] += 1
                ins.then_inc(dve_done, 1)
                dve.wait_ge(dve_done, count[0])

            def cols(h):
                return slice(h * HALF, (h + 1) * HALF)

            def chunk_stats(h):
                for b in range(h * CH, (h + 1) * CH):
                    i = v.bn_stats(bstat[:, b, :], xs[:, b, :])
                return i

            def layer_norm_stats(h=None):
                b0, b1 = (0, NB) if h is None else (h * CH, (h + 1) * CH)
                for b in range(b0, b1):
                    i = v.bn_aggr(mv[:, b, :], bstat[:, b, :])
                link(i)
                v.tensor_scalar(var_eps[:, b0:b1], mv[:, b0:b1, 1], LN_EPS, None, ALU.add).then_inc(var_ready, 1)

            def half(t, h):
                return t[:, h * CH:(h + 1) * CH, :]

            def layer_norm(k, h=None):
                dve.wait_ge(rstd_ready, k + 1 if h is None else 2 * k + h - 1)
                for b in range(NB) if h is None else range(h * CH, (h + 1) * CH):
                    i = v.tensor_scalar(xn[:, b, :], xs[:, b, :], mv[:, b, 0:1], rstd[:, b:b + 1], ALU.subtract,
                                        ALU.mult)
                    i.then_inc(xn_ready, 1)

            v.memset(ctxT_hi[C:C + 1, :].bitcast(fp32), 1.0)
            v.memset(Bh[0:C, :, D:BW], 0.0)
            v.memset(Bh[C:C + 1, :, 0:D], 0.0)
            v.memset(Bh[C:C + 1, :, D:BW], 1.0)
            for h in range(2):
                dve.wait_ge(ld[f"x{h}"], 16)
                i = chunk_stats(h)
            link(i)
            layer_norm_stats()
            layer_norm(0)
            for h in range(2):
                dve.wait_ge(ctxT_ready, h + 1)
                v.tensor_tensor(ctxT_lo[:, cols(h)], ps[0:C, h, :], ctxT_hi[0:C, cols(h)].bitcast(fp32),
                                ALU.subtract).then_inc(ctxT_lo_ready, 1)

            dve.wait_ge(ld["wf"], 48)
            w3 = wf[:, :, :, :].rearrange("p a n k -> p (a n) k")
            link(v.tensor_reduce(wf_s[:, :], w3, AX.X, ALU.max, apply_absolute_value=True))
            link(v.tensor_scalar(wf_s[:, :], wf_s[:, :], 1.0 / WMAX, SCALE_MIN, ALU.mult, ALU.max))
            link(v.reciprocal(wf_rs[:, :], wf_s[:, :]))

            def per_block(t):
                return t[:, :].rearrange("p (n o) -> p n o", o=1).to_broadcast([P, NWB, BLK])
            link(v.tensor_tensor(w3, w3, per_block(wf_rs), ALU.mult))
            link(v.tensor_scalar(w3, w3, WMAX, -WMAX - 1.0, ALU.min, ALU.max))
            link(v.tensor_scalar(w3, w3, MAGIC, MAGIC, ALU.add, ALU.subtract))
            v.tensor_tensor(w3, w3, per_block(wf_s), ALU.mult).then_inc(wq_ready, 1)

            def norms(i, bank):
                dve.wait_ge(nsq_ps, i + 1)
                v.tensor_copy(nsq[:, i, :], ps[:, bank, 0:NB]).then_inc(nsq_ready, 1)

            def clamp_norms(i):
                dve.wait_ge(rn_pow, i + 1)
                v.tensor_scalar(rn[:, i, :], rn[:, i, :], RNORM_MAX, None, ALU.min).then_inc(rn_ready, 1)
            norms(0, 2)
            norms(1, 7)
            clamp_norms(0)
            clamp_norms(1)
            dve.wait_ge(rn_ready, 2)
            for h in range(2):
                dve.wait_ge(rt_ps, h + 1)
                for j in range(CH):
                    b = h * CH + j
                    i = v.tensor_scalar(cosr[:, b, :], chunks(h)[:, j, :], rn[:, 1, b:b + 1], 1.0 / COS_EPS,
                                        ALU.mult, ALU.min)
            link(i)
            for h in range(2):
                dve.wait_ge(dots_ps, h + 1)
                i = v.tensor_tensor(half(cosr, h), chunks(5 + h), half(cosr, h), ALU.mult)
            i.then_inc(x_added, 1)
            dve.wait_ge(x_added, 1)
            for h in range(2):
                link(v.tensor_tensor(half(xs, h), half(xs, h), half(cosr, h), ALU.add))
                i = chunk_stats(h)
            link(i)

            def global_max(k):
                dve.wait_ge(amT_ps, k + 1)
                link(v.tensor_reduce(qs[:, k, 7:8], ps[:, 7, 0:P], AX.X, ALU.max))

            def quant_scale(k, unit):
                s_q = 1.0 / QMAX if unit is None else qs[:, k, 2:3]
                link(v.tensor_scalar(qs[:, k, 0:1], qs[:, k, 7:8], s_q, SCALE_MIN, ALU.mult, ALU.max))
                if unit is None:
                    return v.reciprocal(qs[:, k, 1:2], qs[:, k, 0:1])
                link(v.reciprocal(qs[:, k, 3:4], qs[:, k, 0:1]))
                return v.tensor_scalar(qs[:, k, 1:2], qs[:, k, 3:4], unit, None, ALU.mult)

            def unit_over_qmax(k, unit):
                return v.tensor_scalar(qs[:, k, 2:3], unit, 1.0 / QMAX, None, ALU.mult)

            def first_quant_step(k, t):
                return v.tensor_scalar(t, t, qs[:, k, 1:2], MAGIC, ALU.mult, ALU.add)

            def second_quant_step(t):
                return v.tensor_scalar(t, t, MAGIC, None, ALU.subtract)

            def part_max(k, c, src):
                return v.tensor_reduce(amax[:, k, c:c + 1], src, AX.X, ALU.max, apply_absolute_value=True)

            def join_max(k):
                v.tensor_reduce(amax[:, k, 3:4], amax[:, k, 0:3], AX.X, ALU.max).then_inc(am_ready, 1)

            layer_norm_stats()
            layer_norm(1)
            dve.wait_ge(xn_ready, 2 * NB)
            v.tensor_reduce(amax[:, 0, 3:4], xn[:, :, :], AX.XY, ALU.max, apply_absolute_value=True
                            ).then_inc(am_ready, 1)
            global_max(0)
            link(quant_scale(0, None))
            for h in range(2):
                link(first_quant_step(0, half(xn, h)))
                second_quant_step(half(xn, h)).then_inc(xq_ready, 1)
            sx = qs[:, 0, 0:1]
            unit_over_qmax(1, sx)
            unit_over_qmax(2, sx)
            for c in range(FC0):
                dve.wait_ge(raw_ready, 2 * (c + 1))
                i = part_max(1, c, g_raw[:, c, :])
            link(i)
            join_max(1)
            global_max(1)
            link(quant_scale(1, sx))
            for c in range(FC0):
                link(first_quant_step(1, g_raw[:, c, :]))
                second_quant_step(g_raw[:, c, :]).then_inc(ng_ready, 1)
            sg = qs[:, 1, 0:1]
            unit_over_qmax(3, sg)
            for c in range(FC0):
                dve.wait_ge(raw_ready, 2 * (FC0 + c + 1))
                i = part_max(2, c, u_raw[:, c, :])
            link(i)
            join_max(2)

            def times_sigmoid(c):
                dve.wait_ge(sig_ready, c + 1)
                link(v.tensor_scalar(sig[:, c, :], sig[:, c, :], SIG_TOP, MAGIC16, ALU.min, ALU.add))
                link(v.scalar_tensor_tensor(out=sig[:, c, :], in0=sig[:, c, :], scalar=MAGIC16, in1=g_raw[:, c, :],
                                            op0=ALU.subtract, op1=ALU.mult))
                return part_max(3, c, sig[:, c, :])
            times_sigmoid(0)
            global_max(2)
            quant_scale(2, sx).then_inc(inv_ready, 1)
            su = qs[:, 2, 0:1]
            for c in range(1, FC0):
                i = times_sigmoid(c)
            link(i)
            join_max(3)
            for c in range(FC0):
                dve.wait_ge(vq_ready, c + 1)
                i = second_quant_step(u_raw[:, c, :])
            global_max(3)
            quant_scale(3, sg).then_inc(inv_ready, 1)
            dve.wait_ge(inv_ready, 2)
            link(first_quant_step(3, sig[:, 0, :]))
            for c in range(FC0):
                if c >= 1:
                    dve.wait_ge(vq_ready, FC0 + c)
                link(v.scalar_tensor_tensor(out=sig[:, c, :], in0=sig[:, c, :], scalar=MAGIC, in1=u_raw[:, c, :],
                                            op0=ALU.subtract, op1=ALU.mult))
                i = part_max(4, c, sig[:, c, :])
            link(i)
            join_max(4)
            so_unit = qs[:, 5, 0:1]
            link(v.tensor_scalar(so_unit, qs[:, 3, 0:1], su, None, ALU.mult))
            unit_over_qmax(4, so_unit)
            global_max(4)
            quant_scale(4, so_unit).then_inc(inv_ready, 1)
            dve.wait_ge(inv_ready, 3)
            link(first_quant_step(4, sig[:, :, cols(0)]))
            second_quant_step(sig[:, :, cols(0)]).then_inc(no_ready, 1)
            dve.wait_ge(vq_ready, 2 * FC0)
            second_quant_step(sig[:, :, cols(1)]).then_inc(no_ready, 1)
            def add_down(h):
                dve.wait_ge(down_ps, h + 1)
                return v.scalar_tensor_tensor(out=half(xs, h), in0=chunks(5 + h), scalar=qs[:, 4, 0:1],
                                              in1=half(xs, h), op0=ALU.mult, op1=ALU.add)

            def split_xT(k, h, bank):
                dve.wait_ge(xT_hi_ready, 2 * (k - 2) + h + 1)
                if k == 3:
                    dve.wait_ge(xT_ready, 4 + h + 1)
                v.tensor_tensor(xnT_lo[:, cols(h)], ps[:, bank, :], xnT_hi[:, cols(h)].bitcast(fp32),
                                ALU.subtract).then_inc(xT_lo_ready, 1)
            link(add_down(0))
            link(chunk_stats(0))
            layer_norm_stats(0)
            add_down(1).then_inc(x_added, 2)
            layer_norm(2, 0)
            dve.wait_ge(x_added, 3)
            link(chunk_stats(1))
            layer_norm_stats(1)
            split_xT(2, 0, 0)
            layer_norm(2, 1)

            def queries_lo(u, f, hb):
                dve.wait_ge(q_hi_ready, u + 1)
                v.tensor_tensor(qT_lo[:, hb, cols(f)], ps[0:C, 6, :], qT_hi[0:C, hb, cols(f)].bitcast(fp32),
                                ALU.subtract).then_inc(q_lo_ready, 1)

            def tile_max(u, n, first=False):
                dve.wait_ge(max_ps, 2 * CH * u + n + 1)
                v.tensor_reduce(tmax[:, n:n + 1], ps[:, FIRST_MAX_BANKS[n % 4] if first else 2 + n % 2, :], AX.X, ALU.max).then_inc(max_read, 1)

            def join_tiles(u, first=False):
                dve.wait_ge(max_read, 2 * CH * (u + 1))
                if not first:
                    dve.wait_ge(z_ps, u)
                v.tensor_reduce(Z[:, C:C + CH], tmax[:, :].rearrange("p (q a) -> p q a", a=2), AX.X, ALU.max,
                                negate=True).then_inc(z_ready, 1)

            def split_exp(u, t):
                if t not in HI_DVE and t not in LO_DVE:
                    return
                dve.wait_ge(exp_ready, NB * u + t + 1)
                if t in HI_DVE:
                    v.tensor_copy(P_hi[:, t, :], E[:, t, :]).then_inc(p_hi_dve, 1)
                if t in LO_DVE:
                    v.tensor_tensor(P_lo[:, t, :], E[:, t, :], P_hi[:, t, :].bitcast(fp32),
                                    ALU.subtract).then_inc(p_lo_dve, 1)

            def add_head(u, f):
                dve.wait_ge(y_ps, u + 1)
                y = ps[:, 4 + f, 0:(CH - 1) * BW].rearrange("p (j d) -> p j d", d=BW)
                y_last = ps[:, 6, 0:BW]
                v.reciprocal(rsum[:, f, 0:CH - 1], y[:, :, D])
                v.reciprocal(rsum[:, f, CH - 1:CH], y_last[:, D:BW]).then_inc(rs_ready, 1)
                dve.wait_ge(rs_ready, u + 1)
                for j in range(CH):
                    b = f * CH + j
                    i = v.scalar_tensor_tensor(out=xs[:, b, :], in0=y[:, j, 0:D] if j < CH - 1 else y_last[:, 0:D],
                                               scalar=rsum[:, f, j:j + 1], in1=xs[:, b, :], op0=ALU.mult, op1=ALU.add)
                i.then_inc(y_added, 1)

            def unit(u, f, hb, first=False, n_next=2):
                n_max = 0
                for t in range(NB):
                    for k in range(2):
                        if n_next >= 1 and k < MAX_AT[t]:
                            tile_max(u + 1, n_max)
                            n_max += 1
                            if n_max == 2 * CH:
                                join_tiles(u + 1)
                        if k == 0:
                            split_exp(u, t)
                    if t == 1 and n_next == 2:
                        queries_lo(u + 2, f, 1 - hb)
                    if t == Y_AT + 1 and not first:
                        add_head(u - 1, 1 - f)
                        if n_next == 0:
                            dve.wait_ge(y_added, u)
                            link(chunk_stats(0))
                            layer_norm_stats(0)
            queries_lo(0, 0, 0)
            split_xT(2, 1, 1)
            for n in range(2 * CH):
                tile_max(0, n, first=True)
            join_tiles(0, first=True)
            queries_lo(1, 1, 0)
            dve.wait_ge(bout_ps, 1)
            v.tensor_tensor(xs[:, :, :], xs[:, :, :],
                            ps[:, 4, 0:D].rearrange("p (o d) -> p o d", o=1).to_broadcast([P, NB, D]), ALU.add
                            ).then_inc(bout_added, 1)
            unit(0, 0, 0, first=True)
            dve.wait_ge(bout_added, 1)
            unit(1, 1, 0)
            with dve.Fori(0, NH // 2 - 1) as i:
                for k in range(4):
                    unit(4 * i + 2 + k, k % 2, (k // 2 + 1) % 2)
            unit(2 * NH - 2, 0, 1, n_next=1)
            unit(2 * NH - 1, 1, 1, n_next=0)
            layer_norm(3, 0)
            add_head(2 * NH - 1, 1)
            dve.wait_ge(y_added, 2 * NH)
            link(chunk_stats(1))
            layer_norm_stats(1)
            split_xT(3, 0, 7)
            layer_norm(3, 1)

            split_xT(3, 1, 6)
            dve.wait_ge(logit_ps, 1)
            link(v.tensor_copy(logit[:, :, :].rearrange("p b e -> p (b e)"), ps[:, 7, 0:NB * NE]))
            for b in range(NB):
                i = v.max(top[:, b, :], logit[:, b, :])
            link(i)
            for b in range(NB):
                i = v.max_index(topi[:, b, :], top[:, b, :], logit[:, b, :])
            v.tensor_tensor(dtop[:, :], top[:, :, 1], top[:, :, 0], ALU.subtract).then_inc(dtop_ready, 1)
            link(v.tensor_copy(iota_f[:, :], iota_i[:, :]))
            link(v.tensor_copy(topf[:, :, :], topi[:, :, :]))
            dve.wait_ge(etop_ready, 1)
            link(v.tensor_scalar(g01[:, 1, :], etop[:, :], 1.0, None, ALU.add))
            link(v.reciprocal(g01[:, 0, :], g01[:, 1, :]))
            link(v.tensor_tensor(g01[:, 1, :], etop[:, :], g01[:, 0, :], ALU.mult))

            def along_e(a):
                return a.rearrange("p (b o) -> p b o", o=1).to_broadcast([P, NB, NE])
            iota_b = iota_f[:, :].rearrange("p (o e) -> p o e", o=1).to_broadcast([P, NB, NE])
            for j, g in ((0, gate_a), (1, gate_b)):
                link(v.tensor_tensor(g[:, :, :], iota_b, topf[:, :, j:j + 1].to_broadcast([P, NB, NE]), ALU.is_equal))
                link(v.tensor_tensor(g[:, :, :], g[:, :, :], along_e(g01[:, j, :]), ALU.mult))
            v.tensor_tensor(gates[:, :, :], gate_a[:, :, :], gate_b[:, :, :], ALU.add).then_inc(gates_ready, 1)

            def add_expert(e, hf, before=None):
                dve.wait_ge(ey_ps, 2 * e + hf + 1)
                dve.wait_ge(ey_added, 2 * e + hf) if before is None else before and dve.wait_ge(ey_added, before)
                for j in range(CH):
                    b = hf * CH + j
                    i = v.scalar_tensor_tensor(out=xs[:, b, :], in0=chunks(4 + hf)[:, j, :],
                                               scalar=gates[:, b, bass.ds(e, 1)], in1=xs[:, b, :], op0=ALU.mult,
                                               op1=ALU.add)
                i.then_inc(ey_added, 1)

            def split_w1(e, buf):
                dve.wait_ge(hid_ready, 2 * FC1 * (e - 1))
                v.tensor_copy(b1cur[:, buf, :], b1T[:, bass.ds(FC1 * e, FC1)])
                src = w1[:, bass.ds(e, 1), :].rearrange("p o f -> p (o f)")
                v.tensor_copy(w1_hi[:, buf, :], src).then_inc(w_split, 1)
                dve.wait_ge(w_split, 2 * e - 1)
                v.tensor_tensor(w1_lo[:, buf, :], src, w1_hi[:, buf, :].bitcast(fp32), ALU.subtract
                                ).then_inc(w_split, 1)
            dve.wait_ge(ld["w1"], 16)
            dve.wait_ge(gates_ready, 1)
            split_w1(2, 0)
            add_expert(0, 0, before=0)
            add_expert(0, 1, before=0)
            dve.wait_ge(ey_added, 2)
            dve.wait_ge(b2_ps, 1)
            for h in range(2):
                i = v.tensor_tensor(half(xs, h), chunks(6 + h), half(xs, h), ALU.add)
            i.then_inc(ey_added, 1)
            add_expert(1, 0, before=3)
            split_w1(3, 1)
            with dve.Fori(0, NE // 2 - 2) as i:
                for k in range(2):
                    add_expert(2 * i + 1 + k, 1)
                    add_expert(2 * i + 2 + k, 0)
                    split_w1(2 * i + 4 + k, k)
            for e in range(NE - 2, NE):
                add_expert(e - 1, 1)
                add_expert(e, 0)
            add_expert(NE - 1, 1)


_INS = ['x', 'ctx_768', 'L0_xattn_Wv', 'L0_xattn_bv', 'L0_xattn_Wt', 'L0_xattn_bt', 'L0_ffn_w_gate', 'L0_ffn_w_up',
        'L0_ffn_w_down', 'L1_xattn_Wq', 'L1_xattn_Wk', 'L1_xattn_Wv', 'L1_xattn_Wout', 'L1_xattn_bout',
        'L1_ffn_gate_w', 'L1_ffn_gate_b', 'L1_ffn_w1', 'L1_ffn_b1', 'L1_ffn_w2', 'L1_ffn_b2']
_OUTS = [((8, 128, 128), 'float32')]


def kernel(**inputs):
    import numpy as _np
    import concourse.bacc as _bacc
    from concourse import mybir as _mybir
    from concourse.bass_utils import run_bass_kernel_spmd as _run

    nc = _bacc.Bacc("TRN2", target_bir_lowering=False, num_devices=1)
    arrays, args = {}, []
    for name in _INS:
        a = _np.ascontiguousarray(inputs[name])
        arrays[f"in_{name}_dram"] = a
        args.append(nc.dram_tensor(f"in_{name}_dram", a.shape, _mybir.dt.from_np(a.dtype), kind="ExternalInput").ap())
    for i, (shape, dtype) in enumerate(_OUTS):
        dt = _mybir.dt.from_np(_np.dtype(dtype))
        args.append(nc.dram_tensor(f"out_{i}_dram", shape, dt, kind="ExternalOutput").ap())
    xattn_ffn_two_layers(nc, *args)
    r = _run(nc, [arrays], core_ids=[0])
    got = tuple(r.results[0][f"out_{i}_dram"] for i in range(len(_OUTS)))
    return got[0]
```

```python
import concourse.bass as bass
from concourse import mybir
from contextlib import ExitStack


def xattn_ffn_two_layers(nc, x, ctx_768, L0_xattn_Wv, L0_xattn_bv, L0_xattn_Wt, L0_xattn_bt, L0_ffn_w_gate,
                         L0_ffn_w_up, L0_ffn_w_down, L1_xattn_Wq, L1_xattn_Wk, L1_xattn_Wv, L1_xattn_Wout,
                         L1_xattn_bout, L1_ffn_gate_w, L1_ffn_gate_b, L1_ffn_w1, L1_ffn_b1, L1_ffn_w2,
                         L1_ffn_b2, out):
    fp32, fp32r, u32 = mybir.dt.float32, mybir.dt.float32r, mybir.dt.uint32
    ALU, ACT, AX = mybir.AluOpType, mybir.ActivationFunctionType, mybir.AxisListType

    P = 128
    NB, S, D = x.shape
    C = ctx_768.shape[2]
    T = NB * S
    HALF = T // 2
    CH = NB // 2
    HD = L0_xattn_Wv.shape[0]
    FC0 = L0_ffn_w_gate.shape[0] // P
    BLK = 32
    NBLK = D // BLK
    NH = L1_xattn_Wq.shape[1] // P
    DH = P
    NE, _, F1 = L1_ffn_w1.shape
    FC1 = F1 // P
    assert S == P and D == P and T == 1024 and NH % 2 == 0 and NE % 2 == 0

    LN_EPS = 1e-5
    COS_EPS = 1e-8
    RNORM_MAX = 1e30
    QMAX = 32767.0
    SCALE_MIN = 1e-12
    WMAX = 7.0
    MAGIC = 1.5 * 2.0 ** 23
    MAGIC16 = MAGIC * 2.0 ** -16
    SIG_TOP = 65535.0 / 65536.0
    SM_SCALE = 1.5 * DH ** -0.5
    E1 = 2.718281828459045

    es = ExitStack()
    with es:
        def sb(name, shape, dt=fp32):
            return es.enter_context(nc.sbuf_tensor(name, shape, dt))

        def sem(name):
            return es.enter_context(nc.semaphore(name))

        ident = sb("ident", [P, P])
        ones = sb("ones", [P, P])
        magic = sb("magic", [P, 1])
        minus_magic = sb("minus_magic", [P, 1])
        minus_magic16 = sb("minus_magic16", [P, 1])
        minus_half = sb("minus_half", [P, NB])
        base_e = sb("base_e", [P, NB])
        xs = sb("xs", [P, NB, D])
        xn = sb("xn", [P, NB, D])
        xnT = sb("xnT", [P, T])
        xnT_hi = sb("xnT_hi", [P, T], fp32r)
        xnT_lo = sb("xnT_lo", [P, T], fp32r)
        bstat = sb("bstat", [P, NB, 6])
        mv = sb("mv", [P, NB, 2])
        var_eps = sb("var_eps", [P, NB])
        rstd = sb("rstd", [P, NB])
        ctx = sb("ctx", [P, NB, C])
        CW = C + 1
        ctx_hi = sb("ctx_hi", [P, NB, CW], fp32r)
        ctx_lo = sb("ctx_lo", [P, NB, CW], fp32r)
        ctxT = sb("ctxT", [C, T])
        ctxT_hi = sb("ctxT_hi", [C + 1, T], fp32r)
        ctxT_lo = sb("ctxT_lo", [C, T], fp32r)
        wv0 = sb("wv0", [HD, D])
        wt0 = sb("wt0", [HD, C])
        bv0 = sb("bv0", [HD, 1])
        bt0 = sb("bt0", [HD, 1])
        wT0 = sb("wT0", [P, 2, HD])
        nsq = sb("nsq", [P, 2, NB])
        rn = sb("rn", [P, 2, NB])
        NWB = 3 * FC0 * NBLK
        wf = sb("wf", [P, 3, FC0 * NBLK, BLK])
        wf_s = sb("wf_s", [P, NWB])
        wf_rs = sb("wf_rs", [P, NWB])
        wfT = sb("wfT", [P, 3 * FC0, P])
        amax = sb("amax", [P, 8, 4])
        qs = sb("qs", [P, 8, 8])
        bout = sb("bout", [1, D])
        A_hi = sb("A_hi", [D, NH + 1, C], fp32r)
        A_lo = sb("A_lo", [D, NH + 1, C], fp32r)
        BW = D + 1
        Bh = sb("Bh", [C + 1, NH, BW])
        Acur_hi = sb("Acur_hi", [D, 2, C], fp32r)
        Acur_lo = sb("Acur_lo", [D, 2, C], fp32r)
        qT_hi = sb("qT_hi", [C + 1, 2, T], fp32r)
        qT_lo = sb("qT_lo", [C, 2, T], fp32r)
        tmax = sb("tmax", [P, NB])
        minus_max = sb("minus_max", [P, CH])
        max_diag = sb("max_diag", [P, HALF], fp32r)
        last_row = sb("last_row", [P, C + 1], fp32r)
        rsum = sb("rsum", [P, 2, CH])
        O = sb("O", [C + 1, 2, HALF])
        P_hi = sb("P_hi", [P, NB, HALF], fp32r)
        P_lo = sb("P_lo", [P, NB, HALF], fp32r)
        R = sb("R", [P, 9 * T])
        gw = sb("gw", [D, NE])
        gb = sb("gb", [P, NE])
        b1n = sb("b1n", [NE * FC1, P])
        b1T = sb("b1T", [P, NE * FC1])
        b1cur = sb("b1cur", [P, 2, FC1])
        w1 = sb("w1", [D, NE, F1])
        w2 = sb("w2", [P, NE, FC1, D])
        w1_hi = sb("w1_hi", [D, 2, F1], fp32r)
        w1_lo = sb("w1_lo", [D, 2, F1], fp32r)
        w2_hi = sb("w2_hi", [P, 2, FC1 * D], fp32r)
        w2_lo = sb("w2_lo", [P, 2, FC1 * D], fp32r)
        b2 = sb("b2", [NE, D])
        top = sb("top", [P, NB, 8])
        topi = sb("topi", [P, NB, 8], u32)
        topf = sb("topf", [P, NB, 8])
        iota_i = sb("iota_i", [P, NE], mybir.dt.int32)
        iota_f = sb("iota_f", [P, NE])
        dtop = sb("dtop", [P, NB])
        etop = sb("etop", [P, NB])
        g01 = sb("g01", [P, 2, NB])
        gates = sb("gates", [P, NB, NE])

        E = R[:, 0:NB * HALF].rearrange("p (n t) -> p n t", n=NB)
        gate_rows = R[:, 4 * T:6 * T].rearrange("p (a t) -> p a t", a=2)
        moeT = R[:, 6 * T:7 * T]
        term = R[:, 7 * T:8 * T]
        gate_a, gate_b, logit = (R[:, 8 * T + i * NB * NE:8 * T + (i + 1) * NB * NE].rearrange("p (b e) -> p b e", b=NB)
                                 for i in range(3))
        wq = w1[:, 0:2, :].rearrange("p a f -> p (a f)")
        wout = w1[:, 2:4, :].rearrange("p a f -> p (a f)").rearrange("p (h d) -> p h d", h=NH)
        wk, wv = R[0:C, 0:NH * DH], R[0:C, NH * DH:2 * NH * DH]
        vT, vsq, tT, tsq = (R[0:HD, (2 + i) * T:(3 + i) * T] for i in range(4))
        cosr = R[:, 6 * T:7 * T].rearrange("p (b d) -> p b d", b=NB)
        A32 = R[:, 7 * T:7 * T + NH * C].rearrange("p (h c) -> p h c", h=NH)
        hT = R[:, 8 * T:8 * T + 2 * (D + 2 * C)].rearrange("p (a c) -> p a c", a=2)
        g_raw, u_raw, sig = (R[:, i * FC0 * T:(i + 1) * FC0 * T].rearrange("p (c t) -> p c t", c=FC0)
                             for i in range(3))
        gatesT = ctxT[0:NE, :]
        gates_dram = nc.dram_tensor("gates_dram", [NE, T], fp32).ap()
        ps = es.enter_context(nc.psum_tensor("ps", [P, 8, HALF], fp32))

        def chunks(bank, n=CH):
            return ps[:, bank, 0:n * P].rearrange("p (b d) -> p b d", b=n)

        ld = {n: sem("ld_" + n) for n in ("x0", "x1", "ctx", "w0", "wf", "watt", "wout", "small", "w1", "w2")}
        const_step, const_ready = sem("const_step"), sem("const_ready")
        dve_done, act_done, pool_done = sem("dve_done"), sem("act_done"), sem("pool_done")
        var_ready, rstd_ready, xn_ready = sem("var_ready"), sem("rstd_ready"), sem("xn_ready")
        xT_ps, xT_ready, xT_hi_ready, xT_lo_ready = sem("xT_ps"), sem("xT_ready"), sem("xT_hi_ready"), sem("xT_lo_ready")
        ctxT_ps, ctxT_ready, ctxT_lo_ready = sem("ctxT_ps"), sem("ctxT_ready"), sem("ctxT_lo_ready")
        wT0_ps, wT0_ready = sem("wT0_ps"), sem("wT0_ready")
        t_ps, t_ready, v_ps, v_ready = sem("t_ps"), sem("t_ready"), sem("v_ps"), sem("v_ready")
        nsq_ps, nsq_ready, rn_pow, rn_ready = sem("nsq_ps"), sem("nsq_ready"), sem("rn_pow"), sem("rn_ready")
        rt_ps, dots_ps, cos_used = sem("rt_ps"), sem("dots_ps"), sem("cos_used")
        hT_ps, hT_ready, AB_ps, AB_ready, A_lo_ready = (sem("hT_ps"), sem("hT_ready"), sem("AB_ps"), sem("AB_ready"),
                                                        sem("A_lo_ready"))
        wq_ready, wfT_ps, wfT_ready = sem("wq_ready"), sem("wfT_ps"), sem("wfT_ready")
        am_ready, amT_ps, gmax_read = sem("am_ready"), sem("amT_ps"), sem("gmax_read")
        raw_ps, raw_ready, xq_ready = sem("raw_ps"), sem("raw_ready"), sem("xq_ready")
        ng_ready, sig_ready, no_ready, down_ps, x_added = (sem("ng_ready"), sem("sig_ready"), sem("no_ready"),
                                                           sem("down_ps"), sem("x_added"))
        Acur_ready, q_ps, q_hi_ready, q_lo_ready = sem("Acur_ready"), sem("q_ps"), sem("q_hi_ready"), sem("q_lo_ready")
        max_ps, max_read, z_ready, z_ps, mrow_ready = (sem("max_ps"), sem("max_read"), sem("z_ready"), sem("z_ps"),
                                                       sem("mrow_ready"))
        st_ps, exp_ready, pv_ps, o_ready = sem("st_ps"), sem("exp_ready"), sem("pv_ps"), sem("o_ready")
        y_ps, rs_ready, y_added = sem("y_ps"), sem("rs_ready"), sem("y_added")
        bout_ps, bout_added = sem("bout_ps"), sem("bout_added")
        b1T_ps, b1T_ready, logit_ps, logit_read = sem("b1T_ps"), sem("b1T_ready"), sem("logit_ps"), sem("logit_read")
        dtop_ready, etop_ready, gates_ready, gT_ps, gT_ready, b2_ps = (
            sem("dtop_ready"), sem("etop_ready"), sem("gates_ready"), sem("gT_ps"), sem("gT_ready"), sem("b2_ps"))
        p_hi_dve, p_lo_dve, p_lo_pool = sem("p_hi_dve"), sem("p_lo_dve"), sem("p_lo_pool")
        ctx_split, join_ready, inv_ready, vq_ready, stats_in = (sem("ctx_split"), sem("join_ready"),
                                                                   sem("inv_ready"), sem("vq_ready"), sem("stats_in"))
        w_split, w1_hi_ready, w1_lo_ready, w2_hi_ready, w2_lo_ready = (
            sem("w_split"), sem("w1_hi_ready"), sem("w1_lo_ready"), sem("w2_hi_ready"), sem("w2_lo_ready"))
        hid_ps, hid_ready, hid_hi_dve, hid_lo_dve, hid_lo_pool = (
            sem("hid_ps"), sem("hid_ready"), sem("hid_hi_dve"), sem("hid_lo_dve"), sem("hid_lo_pool"))
        uq_ready, clip_ready, round_ready, product_ready = (sem("uq_ready"), sem("clip_ready"), sem("round_ready"),
                                                            sem("product_ready"))
        first_lo_pool, first_lo_dve = sem("first_lo_pool"), sem("first_lo_dve")
        gates_stored = sem("gates_stored")
        gate_row = [sem(f"gate_row{i}") for i in range(2)]
        ey_ps, term_ready, moe_init, moe_added = sem("ey_ps"), sem("term_ready"), sem("moe_init"), sem("moe_added")
        moe_ps, out_ready, out_stored = sem("moe_ps"), sem("out_ready"), sem("out_stored")

        block = es.enter_context(nc.Block())

        LAG = 3
        MAX_AT = [1, 1, 2, 1, 2, 1, 0, 0]
        FIRST_MAX_BANKS = (2, 3, 5, 7)
        Z_AT = 6
        O_AT = 3
        Y_AT = 5
        LAST_Y_AT = 4
        assert sum(MAX_AT) == 2 * CH and len(MAX_AT) == NB and LAG <= O_AT < Y_AT
        HI_DVE = (0, 2, 4, 6)
        LO_DVE = (3, 7)
        HI_ACT = tuple(t for t in range(NB) if t not in HI_DVE)
        LO_POOL = tuple(t for t in range(NB) if t not in LO_DVE)
        NT = 2 * FC1
        HID_HI_DVE = (0, 2, 4, 6)
        HID_LO_POOL = (1, 5)
        HID_LO_DVE = tuple(s for s in range(NT) if s not in HID_LO_POOL)
        assert NT == NB

        def hid_split(e, s):
            if isinstance(e, int) and e == 0:
                return (first_lo_pool, s + 1) if s < FC1 else (first_lo_dve, s - FC1 + 1)
            if s in HID_LO_POOL:
                return hid_lo_pool, len(HID_LO_POOL) * (e - 1) + HID_LO_POOL.index(s) + 1
            return hid_lo_dve, len(HID_LO_DVE) * (e - 1) + HID_LO_DVE.index(s) + 1

        @block.sync
        def _(sp):
            def load(dst, src, s):
                sp.dma_start(dst, src).then_inc(s, 16)
            load(xs[:, 0:CH, :], x[0:CH].rearrange("b s d -> s b d"), ld["x0"])
            load(wt0[:, :], L0_xattn_Wt, ld["w0"])
            load(wv0[:, :], L0_xattn_Wv, ld["w0"])
            load(bt0[:, :], L0_xattn_bt.rearrange("(h o) -> h o", o=1), ld["w0"])
            load(bv0[:, :], L0_xattn_bv.rearrange("(h o) -> h o", o=1), ld["w0"])
            for i, w in enumerate((L0_ffn_w_gate, L0_ffn_w_up)):
                load(wf[:, i, :, :].rearrange("p (c n) k -> p c (n k)", c=FC0),
                     w.rearrange("(c p) d -> p c d", p=P), ld["wf"])
            load(wf[:, 2, :, :].rearrange("p n k -> p (n k)"), L0_ffn_w_down, ld["wf"])
            load(wout[:, :, :], L1_xattn_Wout.rearrange("(h j) d -> j h d", j=DH), ld["wout"])
            load(bout[:, :], L1_xattn_bout.rearrange("(o d) -> o d", o=1), ld["small"])
            load(gw[:, :], L1_ffn_gate_w, ld["small"])
            load(gb[:, :], L1_ffn_gate_b.rearrange("(o d) -> o d", o=1).to_broadcast([P, NE]), ld["small"])
            load(b1n[:, :], L1_ffn_b1.rearrange("e (c p) -> (e c) p", p=P), ld["small"])
            load(b2[:, :], L1_ffn_b2, ld["small"])

            for e in range(NE):
                load(w2[:, e, :, :], L1_ffn_w2[e].rearrange("(c p) d -> p c d", p=P), ld["w2"])
            sp.wait_ge(AB_ready, NH)
            load(w1[:, :, :], L1_ffn_w1.rearrange("e d f -> d e f"), ld["w1"])
            sp.wait_ge(gT_ready, 1)
            sp.dma_start(gates_dram[:, :], gatesT).then_inc(gates_stored, 16)
            sp.wait_ge(gates_stored, 16)
            for e in range(NE):
                if e >= 2:
                    sp.wait_ge(term_ready, 2 * (e - 1))
                sp.dma_start(gate_rows[:, e % 2, :], gates_dram[e:e + 1, :].to_broadcast([P, T])
                             ).then_inc(gate_row[e % 2], 16)
            for h in range(2):
                sp.wait_ge(out_ready, h + 1)
                sp.dma_start(out[h * CH:(h + 1) * CH].rearrange("b s d -> s b d"), xs[:, h * CH:(h + 1) * CH, :]
                             ).then_inc(out_stored, 16)
            sp.wait_ge(out_stored, 32)

        @block.gpsimd
        def _(pool):
            nc.gpsimd.memset(ident[:, :], 0.0)
            nc.gpsimd.memset(ones[:, :], 1.0)
            nc.gpsimd.memset(magic[:, :], MAGIC)
            nc.gpsimd.memset(minus_magic[:, :], -MAGIC)
            nc.gpsimd.memset(minus_magic16[:, :], -MAGIC16)
            nc.gpsimd.memset(minus_half[:, :], -0.5)
            nc.gpsimd.memset(base_e[:, :], E1)
            nc.gpsimd.memset(ctx_hi[:, :, C:C + 1].bitcast(fp32), 1.0)
            nc.gpsimd.memset(ctx_lo[:, :, C:CW].bitcast(fp32), 0.0)
            nc.gpsimd.memset(last_row[:, 0:C].bitcast(fp32), 0.0)
            nc.gpsimd.memset(last_row[:, C:C + 1].bitcast(fp32), 1.0)
            nc.gpsimd.memset(A_hi[:, NH, :].bitcast(fp32), 0.0)
            nc.gpsimd.memset(A_lo[:, NH, :].bitcast(fp32), 0.0)
            nc.gpsimd.iota(iota_i[:, :], [[1, NE]], base=0, channel_multiplier=0).then_inc(const_step, 1)
            pool.wait_ge(const_step, 1)
            nc.gpsimd.affine_select(out=ident[:, :], in_=ident[:, :], compare_op=ALU.not_equal, fill=1.0, base=0,
                                    pattern=[[-1, P]], channel_multiplier=1).then_inc(const_ready, 1)

            def rstd_pow(k):
                b = slice(0, NB) if k < 2 else slice((k % 2) * CH, (k % 2 + 1) * CH)
                pool.wait_ge(var_ready, k + 1)
                nc.gpsimd.tensor_tensor(out=rstd[:, b], in0=var_eps[:, b], in1=minus_half[:, b],
                                        op=ALU.pow).then_inc(rstd_ready, 1)

            def norm_pow(i):
                pool.wait_ge(nsq_ready, i + 1)
                nc.gpsimd.tensor_tensor(out=rn[:, i, :], in0=nsq[:, i, :], in1=minus_half[:, 0:NB],
                                        op=ALU.pow).then_inc(rn_pow, 1)

            rstd_pow(0)
            norm_pow(0)
            norm_pow(1)
            pool.wait_ge(ld["ctx"], 16)
            nc.gpsimd.tensor_copy(ctx_hi[:, :, 0:C], ctx[:, :, :]).then_inc(ctx_split, 1)
            pool.wait_ge(ctx_split, 1)
            nc.gpsimd.tensor_tensor(out=ctx_lo[:, :, 0:C], in0=ctx[:, :, :], in1=ctx_hi[:, :, 0:C].bitcast(fp32),
                                    op=ALU.subtract).then_inc(ctx_split, 1)
            rstd_pow(1)
            pool.wait_ge(AB_ready, NH)
            nc.gpsimd.tensor_tensor(out=A_lo[:, 0:NH, :], in0=A32, in1=A_hi[:, 0:NH, :].bitcast(fp32),
                                    op=ALU.subtract).then_inc(A_lo_ready, 1)

            def stage_A(h, buf):
                src_hi = A_hi[:, bass.ds(h, 1), :].rearrange("p o c -> p (o c)").bitcast(fp32)
                src_lo = A_lo[:, bass.ds(h, 1), :].rearrange("p o c -> p (o c)").bitcast(fp32)
                nc.gpsimd.tensor_copy(Acur_hi[:, buf, :], src_hi)
                nc.gpsimd.tensor_copy(Acur_lo[:, buf, :], src_lo).then_inc(Acur_ready, 1)
            pool.wait_ge(A_lo_ready, 1)
            stage_A(0, 0)
            stage_A(1, 1)
            def product(k, factor):
                pool.wait_ge(round_ready, k)
                nc.gpsimd.tensor_tensor(out=sig[:, 0, :], in0=sig[:, 0, :], in1=factor[:, 0, :], op=ALU.mult
                                        ).then_inc(product_ready, 1)
            product(1, g_raw)
            pool.wait_ge(b1T_ready, 1)
            pool.wait_ge(ld["w1"], 16)
            pool.wait_ge(ld["w2"], 16 * NE)
            w2_first = w2[:, 0:2, :, :].rearrange("p e c d -> p e (c d)")
            nc.gpsimd.tensor_copy(b1cur[:, :, :].rearrange("p a c -> p (a c)"), b1T[:, 0:2 * FC1])
            nc.gpsimd.tensor_copy(w1_hi[:, :, :], w1[:, 0:2, :])
            nc.gpsimd.tensor_copy(w2_hi[:, :, :], w2_first).then_inc(w_split, 1)
            pool.wait_ge(uq_ready, 1)
            product(2, u_raw)
            pool.wait_ge(w_split, 1)
            nc.gpsimd.tensor_tensor(out=w1_lo[:, :, :], in0=w1[:, 0:2, :], in1=w1_hi[:, :, :].bitcast(fp32),
                                    op=ALU.subtract)
            nc.gpsimd.tensor_tensor(out=w2_lo[:, :, :], in0=w2_first, in1=w2_hi[:, :, :].bitcast(fp32), op=ALU.subtract
                                    ).then_inc(w_split, 1)
            rstd_pow(2)
            rstd_pow(3)

            def exp_lo(u, t):
                n = NB * u + t
                if t in HI_DVE:
                    pool.wait_ge(p_hi_dve, len(HI_DVE) * u + HI_DVE.index(t) + 1)
                else:
                    pool.wait_ge(exp_ready, n + 1)
                nc.gpsimd.tensor_tensor(out=P_lo[:, t, :], in0=E[:, t, :], in1=P_hi[:, t, :].bitcast(fp32),
                                        op=ALU.subtract).then_inc(p_lo_pool, 1)

            def head(h, buf, stage=True):
                for f in range(2):
                    for t in LO_POOL:
                        if not stage and f == 1 and t == NB - 2:
                            rstd_pow(4)
                        if f == 0 and t == LO_POOL[2] and stage:
                            pool.wait_ge(q_ps, 2 * h + 2)
                        exp_lo(2 * h + f, t)
                        if f == 0 and t == LO_POOL[2] and stage:
                            stage_A(h + 2, buf)
            head(0, 0)
            with pool.Fori(0, NH // 2 - 1) as i:
                head(2 * i + 1, 1)
                head(2 * i + 2, 0)
            head(NH - 1, 1, stage=False)

            def first_hidden_lo(s):
                pool.wait_ge(hid_ready, s + 1)
                nc.gpsimd.tensor_tensor(out=P_lo[:, s, :], in0=E[:, s, :], in1=P_hi[:, s, :].bitcast(fp32),
                                        op=ALU.subtract).then_inc(first_lo_pool, 1)
            first_hidden_lo(0)
            first_hidden_lo(1)
            rstd_pow(5)
            first_hidden_lo(2)
            first_hidden_lo(3)
            def hidden_lo(e, s):
                if s in HID_HI_DVE:
                    pool.wait_ge(hid_hi_dve, len(HID_HI_DVE) * (e - 1) + HID_HI_DVE.index(s) + 1)
                else:
                    pool.wait_ge(hid_ready, NT * e + s + 1)
                nc.gpsimd.tensor_tensor(out=P_lo[:, s, :], in0=E[:, s, :], in1=P_hi[:, s, :].bitcast(fp32),
                                        op=ALU.subtract).then_inc(hid_lo_pool, 1)

            def w1_low(e, buf):
                pool.wait_ge(w1_hi_ready, e - 1)
                nc.gpsimd.tensor_tensor(out=w1_lo[:, buf, :], in0=w1[:, bass.ds(e, 1), :].rearrange("p o f -> p (o f)"),
                                        in1=w1_hi[:, buf, :].bitcast(fp32), op=ALU.subtract).then_inc(w1_lo_ready, 1)

            def w2_low(e, buf):
                pool.wait_ge(w2_hi_ready, e - 1)
                nc.gpsimd.tensor_tensor(out=w2_lo[:, buf, :],
                                        in0=w2[:, bass.ds(e, 1), :, :].rearrange("p o c d -> p (o c d)"),
                                        in1=w2_hi[:, buf, :].bitcast(fp32), op=ALU.subtract).then_inc(w2_lo_ready, 1)

            def add_term(e, hf, first=False):
                pool.wait_ge(term_ready, 2 * e + hf + 1)
                if first:
                    pool.wait_ge(moe_init, hf + 1)
                else:
                    pool.wait_ge(moe_added, 2 * e + hf - 1)
                c = slice(hf * HALF, (hf + 1) * HALF)
                nc.gpsimd.tensor_tensor(out=moeT[:, c], in0=term[:, c], in1=moeT[:, c], op=ALU.add
                                        ).then_inc(moe_added, 1)

            def expert(e, buf, last=False):
                if not last:
                    w1_low(e + 1, 1 - buf)
                for s in range(NT):
                    if s in HID_LO_POOL:
                        hidden_lo(e, s)
                    if s == 0:
                        add_term(e - 1, 0)
                    if s == FC1:
                        add_term(e - 1, 1)
                        if not last:
                            w2_low(e + 1, 1 - buf)
            pool.wait_ge(dtop_ready, 1)
            nc.gpsimd.tensor_tensor(out=etop[:, :], in0=base_e[:, :], in1=dtop[:, :], op=ALU.pow
                                    ).then_inc(etop_ready, 1)
            hidden_lo(1, HID_LO_POOL[0])
            w1_low(2, 0)
            hidden_lo(1, HID_LO_POOL[1])
            add_term(0, 0, first=True)
            add_term(0, 1, first=True)
            w2_low(2, 0)
            with pool.Fori(0, NE // 2 - 2) as i:
                expert(2 * i + 2, 0)
                expert(2 * i + 3, 1)
            expert(NE - 2, 0)
            expert(NE - 1, 1, last=True)
            add_term(NE - 1, 0)

        @block.tensor
        def _(pe):
            mm, tr = nc.tensor.matmul, nc.tensor.transpose

            def transpose_half(k, h, bank):
                for j in range(CH):
                    pe.wait_ge(xn_ready, NB * k + CH * h + j + 1)
                    i = tr(ps[:, bank, j * P:(j + 1) * P], xn[:, CH * h + j, :], ident[:, :])
                i.then_inc(xT_ps, 1)

            def keep_clock_up(bank, n):
                for _ in range(n):
                    mm(ps[:, bank, 0:P], ones[:, :], ones[:, :], start=True, stop=True)

            pe.wait_ge(const_ready, 1)
            keep_clock_up(7, 9)
            pe.wait_ge(ld["ctx"], 16)
            for b in range(NB):
                i = tr(ps[0:C, b // CH, (b % CH) * P:(b % CH + 1) * P], ctx[:, b, :], ident[:, :])
                if b % CH == CH - 1:
                    i.then_inc(ctxT_ps, 1)
            keep_clock_up(7, 6)
            pe.wait_ge(ld["w0"], 64)
            tr(ps[0:C, 2, 0:HD], wt0[:, :], ident[0:HD, 0:HD])
            tr(ps[0:D, 2, HD:2 * HD], wv0[:, :], ident[0:HD, 0:HD]).then_inc(wT0_ps, 1)
            pe.wait_ge(wT0_ready, 1)
            for h in range(2):
                pe.wait_ge(ctxT_ready, h + 1)
                mm(ps[0:HD, 3 + h, :], wT0[0:C, 0, :], ctxT[:, h * HALF:(h + 1) * HALF], start=True, stop=True
                   ).then_inc(t_ps, 1)
            for h in range(2):
                transpose_half(0, h, 5 + h)

            def squared_norms(i, sq, bank):
                for b in range(NB):
                    j = mm(ps[:, bank, b:b + 1], sq[:, b * P:(b + 1) * P], ones[0:HD, 0:1],
                           start=True, stop=True)
                j.then_inc(nsq_ps, 1)
            keep_clock_up(7, 3)
            pe.wait_ge(t_ready, 2)
            for h in range(2):
                pe.wait_ge(xT_ready, h + 1)
                mm(ps[0:HD, 3 + h, :], wT0[:, 1, :], xnT[:, h * HALF:(h + 1) * HALF], start=True, stop=True
                   ).then_inc(v_ps, 1)
            squared_norms(0, tsq, 2)
            pe.wait_ge(v_ready, 2)
            squared_norms(1, vsq, 7)
            pe.wait_ge(rn_ready, 1)
            pe.wait_ge(ctxT_lo_ready, 2)
            for b in range(NB):
                i = mm(ps[:, b // CH, (b % CH) * P:(b % CH + 1) * P], rn[:, 0, b:b + 1].to_broadcast([P, P]),
                       ident[:, :], start=True, stop=True)
                if b % CH == CH - 1:
                    i.then_inc(rt_ps, 1)
            for b in range(NB):
                i = mm(ps[:, 5 + b // CH, (b % CH) * P:(b % CH + 1) * P], vT[:, b * P:(b + 1) * P],
                       tT[:, b * P:(b + 1) * P], start=True, stop=True)
                if b % CH == CH - 1:
                    i.then_inc(dots_ps, 1)

            pe.wait_ge(ld["watt"], 48)
            pe.wait_ge(ld["wout"], 16)

            def head_transposes(h):
                if h >= 2:
                    pe.wait_ge(hT_ready, h - 1)
                bank = 3 + h % 2
                cols = slice(h * DH, (h + 1) * DH)
                tr(ps[:, bank, 0:D], wq[:, cols], ident[:, :])
                tr(ps[:, bank, D:D + C], wk[:, cols], ident[0:C, 0:C])
                tr(ps[:, bank, D + C:D + 2 * C], wv[:, cols], ident[0:C, 0:C]).then_inc(hT_ps, 1)

            def head_products(h):
                pe.wait_ge(hT_ready, h + 1)
                if h < 2:
                    pe.wait_ge(nsq_ready, h + 1)
                else:
                    pe.wait_ge(AB_ready, h - 1)
                bank, w = (2, 7)[h % 2], hT[:, h % 2, :]
                mm(ps[:, bank, 0:C], w[:, 0:D], w[:, D:D + C], start=True, stop=True)
                mm(ps[0:C, bank, P:P + D], w[:, D + C:D + 2 * C], wout[:, h, :], start=True, stop=True
                   ).then_inc(AB_ps, 1)
            head_transposes(0)
            for h in range(NH):
                if h + 1 < NH:
                    head_transposes(h + 1)
                head_products(h)

            pe.wait_ge(wq_ready, 1)
            pe.wait_ge(AB_ready, NH)
            for j in range(3 * FC0):
                w, c = j // FC0, j % FC0
                i = tr(ps[:, (3, 4, 2)[w], c * P:(c + 1) * P],
                       wf[:, w, c * NBLK:(c + 1) * NBLK, :].rearrange("p n k -> p (n k)"), ident[:, :])
                if c == FC0 - 1:
                    i.then_inc(wfT_ps, 1)
            pe.wait_ge(ld["small"], 80)
            pe.wait_ge(x_added, 1)
            tr(ps[:, 0, 0:NE * FC1], b1n[:, :], ident[0:NE * FC1, 0:NE * FC1]).then_inc(b1T_ps, 1)

            def spread_max(k):
                pe.wait_ge(am_ready, k + 1)
                mm(ps[:, 7, 0:P], amax[:, k, 3:4].to_broadcast([P, P]), ident[:, :], start=True, stop=True
                   ).then_inc(amT_ps, 1)
            spread_max(0)
            pe.wait_ge(wfT_ready, 3)
            keep_clock_up(2, 6)
            for b in range(NB):
                if b % CH == 0:
                    pe.wait_ge(xq_ready, b // CH + 1)
                i = tr(ps[:, 5 + b // CH, (b % CH) * P:(b % CH + 1) * P], xn[:, b, :], ident[:, :])
                if b % CH == CH - 1:
                    i.then_inc(xT_ps, 1)
            for j in range(4 * FC0):
                w, c, h = j // (2 * FC0), j // 2 % FC0, j % 2
                if j == 0:
                    pe.wait_ge(b1T_ready, 1)
                if j < 2:
                    pe.wait_ge(xT_ready, 2 + h + 1)
                if j >= 5:
                    pe.wait_ge(raw_ready, j - 4)
                mm(ps[:, j % 5, :], wfT[:, w * FC0 + c, :], xnT[:, h * HALF:(h + 1) * HALF], start=True, stop=True
                   ).then_inc(raw_ps, 1)
                if j == 8:
                    spread_max(1)
            spread_max(2)
            spread_max(3)
            pe.wait_ge(raw_ready, 4 * FC0)
            keep_clock_up(4, 16)
            spread_max(4)
            keep_clock_up(4, 8)
            for b in range(NB):
                if b % CH == 0:
                    pe.wait_ge(no_ready, b // CH + 1)
                for c in range(FC0):
                    i = mm(ps[:, 5 + b // CH, (b % CH) * P:(b % CH + 1) * P], sig[:, c, b * P:(b + 1) * P],
                           wfT[:, 2 * FC0 + c, :], start=(c == 0), stop=(c == FC0 - 1))
                if b % CH == CH - 1:
                    i.then_inc(down_ps, 1)

            pe.wait_ge(raw_ready, 4 * FC0)
            mm(ps[:, 4, 0:D], ones[0:1, :], bout[:, :], start=True, stop=True).then_inc(bout_ps, 1)

            def project(head, f, hb):
                if f == 0:
                    pe.wait_ge(Acur_ready, head + 1)
                cols = slice(f * HALF, (f + 1) * HALF)
                o = ps[0:C, 6, :]
                mm(o, Acur_hi[:, hb, :], xnT_hi[:, cols], start=True, stop=False)
                mm(o, Acur_hi[:, hb, :], xnT_lo[:, cols], start=False, stop=False)
                mm(o, Acur_lo[:, hb, :], xnT_hi[:, cols], start=False, stop=True).then_inc(q_ps, 1)

            def max_tile(u, f, hb, n, first=False):
                qc, kh = n // 2, n % 2
                if n == 0:
                    pe.wait_ge(q_hi_ready, u + 1)
                if first and n >= len(FIRST_MAX_BANKS):
                    pe.wait_ge(max_read, n - len(FIRST_MAX_BANKS) + 1)
                if not first:
                    pe.wait_ge(max_read, 2 * CH * u + n - 1)
                q0 = f * HALF + qc * P
                mm(ps[:, FIRST_MAX_BANKS[n % 4] if first else 2 + n % 2, :], qT_hi[0:C, hb, q0:q0 + P], ctxT_hi[0:C, kh * HALF:(kh + 1) * HALF],
                   start=True, stop=True).then_inc(max_ps, 1)

            def max_row(u):
                pe.wait_ge(z_ready, u + 1)
                mm(ps[0:C + 1, 7, :], last_row[:, :], max_diag[:, :], start=True, stop=True).then_inc(z_ps, 1)

            def score_tile(u, f, hb, t, first=False):
                if t == 0:
                    pe.wait_ge(mrow_ready, u + 1)
                    pe.wait_ge(q_lo_ready, u + 1)
                if not (first and t < 2):
                    pe.wait_ge(exp_ready, NB * u + t - 1)
                k, q, o = slice(t * P, (t + 1) * P), slice(f * HALF, (f + 1) * HALF), ps[:, t % 2, :]
                mm(o, ctxT_hi[:, k], qT_hi[:, hb, q], start=True, stop=False)
                mm(o, ctxT_hi[0:C, k], qT_lo[:, hb, q], start=False, stop=False)
                mm(o, ctxT_lo[:, k], qT_hi[0:C, hb, q], start=False, stop=True).then_inc(st_ps, 1)

            def output_chunk(u, f, t):
                if t in LO_DVE:
                    pe.wait_ge(p_lo_dve, len(LO_DVE) * u + LO_DVE.index(t) + 1)
                else:
                    pe.wait_ge(p_lo_pool, len(LO_POOL) * u + LO_POOL.index(t) + 1)
                o = ps[0:CW, 4 + f, :]
                mm(o, ctx_hi[:, t, :], P_hi[:, t, :], start=(t == 0), stop=False)
                mm(o, ctx_lo[:, t, :], P_hi[:, t, :], start=False, stop=False)
                mm(o, ctx_hi[:, t, :], P_lo[:, t, :], start=False, stop=(t == NB - 1)).then_inc(pv_ps, 1)

            def y_place(f, j):
                return ps[:, 4 + f, j * BW:(j + 1) * BW] if j < CH - 1 else ps[:, 6, 0:BW]

            def project_out(u, head, f):
                pe.wait_ge(o_ready, u + 1)
                for j in range(CH):
                    i = mm(y_place(f, j), O[:, f, j * P:(j + 1) * P], Bh[:, bass.ds(head, 1), :].rearrange("p o d -> p (o d)"),
                           start=True, stop=True)
                i.then_inc(y_ps, 1)

            def unit(u, head, f, hb, first=False, second=False, n_next=2):
                n_max = 0
                for t in range(NB):
                    score_tile(u, f, hb, t, first)
                    if t == 0 and n_next == 2:
                        pe.wait_ge(q_lo_ready, u + 2)
                        if not (first or second):
                            pe.wait_ge(y_added, u - 1)
                        project(head + 1, f, 1 - hb)
                    if t == LAG and first:
                        pe.wait_ge(bout_added, 1)
                    if t == LAG and not (first or second):
                        pe.wait_ge(y_added, u - 1)
                    for k in range(2):
                        if n_next >= 1 and k < MAX_AT[t]:
                            max_tile(u + 1, 1 - f, hb if f == 0 else 1 - hb, n_max)
                            n_max += 1
                        if k == 0 and t >= LAG:
                            output_chunk(u, f, t - LAG)
                        elif k == 0 and not first:
                            output_chunk(u - 1, 1 - f, t - LAG + NB)
                    if n_next >= 1 and t == Z_AT:
                        max_row(u + 1)
                    if t == (Y_AT if n_next else LAST_Y_AT) and not first:
                        if n_next == 2:
                            pe.wait_ge(q_lo_ready, u + 3)
                        project_out(u - 1, head if f == 1 else head - 1, 1 - f)

            transpose_half(2, 0, 0)
            keep_clock_up(7, 4)
            pe.wait_ge(ctx_split, 2)
            pe.wait_ge(xT_lo_ready, 1)
            pe.wait_ge(x_added, 3)
            project(0, 0, 0)
            transpose_half(2, 1, 1)
            for n in range(2 * CH):
                max_tile(0, 0, 0, n, first=True)
            pe.wait_ge(xT_lo_ready, 2)
            pe.wait_ge(q_lo_ready, 1)
            project(0, 1, 0)
            keep_clock_up(0, 9)
            max_row(0)
            unit(0, 0, 0, 0, first=True)
            unit(1, 0, 1, 0, second=True)
            with pe.Fori(0, NH // 2 - 1) as i:
                for k in range(4):
                    unit(4 * i + 2 + k, 2 * i + 1 + k // 2, k % 2, (k // 2 + 1) % 2)
            unit(2 * NH - 2, NH - 1, 0, 1, n_next=1)
            unit(2 * NH - 1, NH - 1, 1, 1, n_next=0)
            for t in range(NB - LAG, NB):
                if t == NB - 1:
                    transpose_half(3, 0, 7)
                output_chunk(2 * NH - 1, 1, t)

            def router():
                pe.wait_ge(xT_ready, 6)
                pe.wait_ge(xT_lo_ready, 3)
                for b in range(NB):
                    i = mm(ps[:, 7, b * NE:(b + 1) * NE], xnT[:, b * P:(b + 1) * P], gw[:, :], start=True, stop=True)
                i.then_inc(logit_ps, 1)

            def transpose_gates():
                pe.wait_ge(gates_ready, 1)
                for b in range(NB):
                    i = tr(ps[0:NE, 6 + b // CH, (b % CH) * P:(b % CH + 1) * P], gates[:, b, :], ident[:, :])
                i.then_inc(gT_ps, 1)

            def gate_bias():
                pe.wait_ge(gT_ready, 1)
                for h in range(2):
                    mm(ps[:, 6 + h, :], b2[:, :], gatesT[:, h * HALF:(h + 1) * HALF], start=True, stop=True
                       ).then_inc(b2_ps, 1)

            def hidden_tile(e, buf, s, first=False, second=False):
                hf, c = s // FC1, s % FC1
                if s == 0:
                    if first:
                        pe.wait_ge(w_split, 2)
                    elif not second:
                        pe.wait_ge(w1_lo_ready, e - 1)
                if not (first and s < 4):
                    pe.wait_ge(hid_ready, 2 * FC1 * e + s - 3)
                f, t = slice(c * P, (c + 1) * P), slice(hf * HALF, (hf + 1) * HALF)
                o = ps[:, s % 4, :]
                mm(o, w1_hi[:, buf, f], xnT_hi[:, t], start=True, stop=False)
                mm(o, w1_hi[:, buf, f], xnT_lo[:, t], start=False, stop=False)
                mm(o, w1_lo[:, buf, f], xnT_hi[:, t], start=False, stop=True).then_inc(hid_ps, 1)

            def output_tile(e, buf, s, first=False, second=False):
                hf, c = s // FC1, s % FC1
                pe.wait_ge(*hid_split(e, s))
                if s == 0 and not (first or second):
                    pe.wait_ge(w2_lo_ready, e - 1)
                if c == 0 and not (first or second):
                    pe.wait_ge(term_ready, 2 * (e - 2) + hf + 1)
                if c == 0 and second:
                    pe.wait_ge(moe_init, hf + 1)
                o, w = ps[:, 4 + 2 * buf + hf, :], slice(c * D, (c + 1) * D)
                mm(o, w2_hi[:, buf, w], P_hi[:, s, :], start=(c == 0), stop=False)
                mm(o, w2_lo[:, buf, w], P_hi[:, s, :], start=False, stop=False)
                mm(o, w2_hi[:, buf, w], P_lo[:, s, :], start=False, stop=(c == FC1 - 1)).then_inc(ey_ps, 1)

            def outputs(e, buf):
                for s in range(FC1):
                    hidden_tile(e, buf, s + FC1)
                    output_tile(e, buf, s)
                for s in range(FC1):
                    hidden_tile(e + 1, 1 - buf, s)
                    output_tile(e, buf, s + FC1)
            pe.wait_ge(xT_lo_ready, 3)
            pe.wait_ge(exp_ready, 2 * NH * NB)
            pe.wait_ge(max_read, 2 * NH * 2 * CH)
            hidden_tile(0, 0, 0, first=True)
            project_out(2 * NH - 1, NH - 1, 1)
            for s in range(1, FC1):
                hidden_tile(0, 0, s, first=True)
            output_tile(0, 0, 0, first=True)
            output_tile(0, 0, 1, first=True)
            transpose_half(3, 1, 6)
            output_tile(0, 0, 2, first=True)
            output_tile(0, 0, 3, first=True)
            router()
            pe.wait_ge(xT_lo_ready, 4)
            for s in range(FC1, NT):
                hidden_tile(0, 0, s, first=True)
            for s in range(FC1):
                hidden_tile(1, 1, s, second=True)
                output_tile(0, 0, s + FC1, first=True)
            transpose_gates()
            hidden_tile(1, 1, FC1, second=True)
            hidden_tile(1, 1, FC1 + 1, second=True)
            gate_bias()
            for s in range(FC1 + 2, NT):
                hidden_tile(1, 1, s, second=True)
                output_tile(1, 1, s - FC1 - 2, second=True)
            output_tile(1, 1, FC1 - 2, second=True)
            output_tile(1, 1, FC1 - 1, second=True)
            for s in range(FC1):
                hidden_tile(2, 0, s)
                output_tile(1, 1, s + FC1, second=True)
            with pe.Fori(0, NE // 2 - 2) as i:
                outputs(2 * i + 2, 0)
                outputs(2 * i + 3, 1)
            outputs(NE - 2, 0)
            for s in range(FC1):
                hidden_tile(NE - 1, 1, s + FC1)
                output_tile(NE - 1, 1, s)
            for s in range(FC1, NT):
                output_tile(NE - 1, 1, s)
            pe.wait_ge(hid_ready, NT * NE)
            for h in range(2):
                pe.wait_ge(moe_added, 2 * (NE - 1) + h + 1)
                for j in range(CH):
                    i = tr(ps[:, h, j * P:(j + 1) * P], moeT[:, (h * CH + j) * P:(h * CH + j + 1) * P], ident[:, :])
                i.then_inc(moe_ps, 1)

        @block.scalar
        def _(act):
            af, count = nc.scalar.activation, [0]

            def link(ins):
                count[0] += 1
                ins.then_inc(act_done, 1)
                act.wait_ge(act_done, count[0])

            act.dma_start(xs[:, CH:NB, :], x[CH:NB].rearrange("b s d -> s b d")).then_inc(ld["x1"], 16)
            act.dma_start(ctx[:, :, :], ctx_768.rearrange("b s c -> s b c")).then_inc(ld["ctx"], 16)
            act.dma_start(wq[:, :], L1_xattn_Wq).then_inc(ld["watt"], 16)
            act.dma_start(wk, L1_xattn_Wk).then_inc(ld["watt"], 16)
            act.dma_start(wv, L1_xattn_Wv).then_inc(ld["watt"], 16)

            def cols(h):
                return slice(h * HALF, (h + 1) * HALF)
            act.wait_ge(const_ready, 1)
            for h in range(2):
                act.wait_ge(ctxT_ps, h + 1)
                af(ctxT[:, cols(h)], ps[0:C, h, :], ACT.Copy)
                af(ctxT_hi[0:C, cols(h)], ps[0:C, h, :], ACT.Copy).then_inc(ctxT_ready, 1)
            act.wait_ge(wT0_ps, 1)
            af(wT0[0:C, 0, :], ps[0:C, 2, 0:HD], ACT.Copy)
            af(wT0[:, 1, :], ps[:, 2, HD:2 * HD], ACT.Copy).then_inc(wT0_ready, 1)

            def with_bias(src_ps, bias, dst, dst_sq, ready):
                for h in range(2):
                    act.wait_ge(src_ps, h + 1)
                    af(dst[:, cols(h)], ps[0:HD, 3 + h, :], ACT.Identity, bias=bias[:, 0:1])
                    af(dst_sq[:, cols(h)], ps[0:HD, 3 + h, :], ACT.Square, bias=bias[:, 0:1]).then_inc(ready, 1)

            def evacuate_xT(k, bank, plain=True):
                for h in range(2):
                    act.wait_ge(xT_ps, 2 * k + h + 1)
                    af(xnT[:, cols(h)], ps[:, bank + h, :], ACT.Copy).then_inc(xT_ready, 1)
            with_bias(t_ps, bt0, tT, tsq, t_ready)
            evacuate_xT(0, 5)
            with_bias(v_ps, bv0, vT, vsq, v_ready)

            def keep_products(h):
                act.wait_ge(AB_ps, h + 1)
                bank = (2, 7)[h % 2]
                af(A32[:, h, :], ps[:, bank, 0:C], ACT.Copy)
                af(A_hi[:, h, :], ps[:, bank, 0:C], ACT.Copy)
                af(Bh[0:C, h, 0:D], ps[0:C, bank, P:P + D], ACT.Copy).then_inc(AB_ready, 1)
            for h in range(NH):
                act.wait_ge(hT_ps, h + 1)
                if h >= 2:
                    act.wait_ge(AB_ps, h - 1)
                af(hT[:, h % 2, :], ps[:, 3 + h % 2, 0:D + 2 * C], ACT.Copy).then_inc(hT_ready, 1)
                if h >= 1:
                    keep_products(h - 1)
            keep_products(NH - 1)
            for w in range(3):
                act.wait_ge(wfT_ps, w + 1)
                af(wfT[:, w * FC0:(w + 1) * FC0, :], chunks((3, 4, 2)[w], FC0), ACT.Copy).then_inc(wfT_ready, 1)
            act.wait_ge(b1T_ps, 1)
            af(b1T[:, :], ps[:, 0, 0:NE * FC1], ACT.Copy).then_inc(b1T_ready, 1)
            evacuate_xT(1, 5)
            nc.scalar.preload_act_table(ACT.Sigmoid)

            def first_quant_step(k, t):
                af(t, t, ACT.Identity, bias=magic[:, 0:1], scale=qs[:, k, 1:2]).then_inc(vq_ready, 1)
            for j in range(4 * FC0):
                act.wait_ge(raw_ps, j + 1)
                dst = (g_raw, u_raw)[j // (2 * FC0)]
                af(dst[:, j // 2 % FC0, cols(j % 2)], ps[:, j % 5, :], ACT.Copy).then_inc(raw_ready, 1)
                if j == 9:
                    act.wait_ge(inv_ready, 1)
                    for c in range(1, FC0):
                        first_quant_step(1, g_raw[:, c, :])
            act.wait_ge(A_lo_ready, 1)
            for c in range(FC0):
                act.wait_ge(ng_ready, c + 1)
                af(sig[:, c, :], g_raw[:, c, :], ACT.Sigmoid, scale=qs[:, 1, 0:1]).then_inc(sig_ready, 1)
            act.wait_ge(clip_ready, 1)
            af(sig[:, 0, :], sig[:, 0, :], ACT.Identity, bias=minus_magic16[:, 0:1]).then_inc(round_ready, 1)
            act.wait_ge(inv_ready, 2)
            for c in range(FC0):
                first_quant_step(2, u_raw[:, c, :])
            for c in range(FC0):
                act.wait_ge(vq_ready, FC0 + c)
                af(u_raw[:, c, :], u_raw[:, c, :], ACT.Identity, bias=minus_magic[:, 0:1]).then_inc(uq_ready, 1)
            act.wait_ge(inv_ready, 3)
            for c in range(FC0 - 1):
                first_quant_step(3, sig[:, c, :])
                if c == 0:
                    act.wait_ge(vq_ready, 2 * FC0)
                    af(sig[:, 0, :], sig[:, 0, :], ACT.Identity, bias=minus_magic[:, 0:1]).then_inc(round_ready, 1)
            act.wait_ge(inv_ready, 4)
            first_quant_step(4, sig[:, :, cols(1)])

            def split_xT(k, h, bank):
                act.wait_ge(xT_ps, 2 * k + h + 1)
                af(xnT_hi[:, cols(h)], ps[:, bank, :], ACT.Copy).then_inc(xT_hi_ready, 1)
                if k == 3 and h == 1:
                    af(xnT[:, cols(h)], ps[:, bank, :], ACT.Copy).then_inc(xT_ready, 1)
            nc.scalar.preload_act_table(ACT.Exp)
            split_xT(2, 0, 0)

            def queries_hi(u, f, hb):
                act.wait_ge(q_ps, u + 1)
                af(qT_hi[0:C, hb, cols(f)], ps[0:C, 6, :], ACT.Copy).then_inc(q_hi_ready, 1)

            def max_row(u, f, hb):
                act.wait_ge(z_ps, u + 1)
                af(qT_hi[C:C + 1, hb, cols(f)], ps[C:C + 1, 7, :], ACT.Copy).then_inc(mrow_ready, 1)

            def take_output(u, f):
                act.wait_ge(pv_ps, NB * (u + 1))
                af(O[:, f, :], ps[0:CW, 4 + f, :], ACT.Copy).then_inc(o_ready, 1)

            def unit(u, f, hb, first=False, n_next=2):
                for t in range(NB):
                    act.wait_ge(st_ps, NB * u + t + 1)
                    if not first:
                        act.wait_ge(pv_ps, NB * (u - 1) + t + 1)
                    i = af(E[:, t, :], ps[:, t % 2, :], ACT.Exp, scale=SM_SCALE)
                    if t in HI_ACT:
                        i = af(P_hi[:, t, :], ps[:, t % 2, :], ACT.Exp, scale=SM_SCALE)
                    i.then_inc(exp_ready, 1)
                    if t == 1 and n_next == 2:
                        queries_hi(u + 2, f, 1 - hb)
                    if t == O_AT and not first:
                        take_output(u - 1, 1 - f)
                    if t == Z_AT and n_next >= 1:
                        max_row(u + 1, 1 - f, hb if f == 0 else 1 - hb)
            queries_hi(0, 0, 0)
            split_xT(2, 1, 1)
            queries_hi(1, 1, 0)
            max_row(0, 0, 0)
            unit(0, 0, 0, first=True)
            unit(1, 1, 0)
            with act.Fori(0, NH // 2 - 1) as i:
                for k in range(4):
                    unit(4 * i + 2 + k, k % 2, (k // 2 + 1) % 2)
            unit(2 * NH - 2, 0, 1, n_next=1)
            unit(2 * NH - 1, 1, 1, n_next=0)
            nc.scalar.preload_act_table(ACT.Gelu)
            split_xT(3, 0, 7)
            take_output(2 * NH - 1, 1)
            act.wait_ge(xT_lo_ready, 3)
            af(xnT[:, cols(0)], ps[:, 7, :], ACT.Copy).then_inc(xT_ready, 1)

            def hidden(e, buf, s, first=False):
                act.wait_ge(hid_ps, NT * e + s + 1)
                if not first:
                    act.wait_ge(ey_ps, NT * (e - 1) + s + 1)
                bias = b1cur[:, buf, s % FC1:s % FC1 + 1]
                i = af(E[:, s, :], ps[:, s % 4, :], ACT.Gelu, bias=bias)
                if first or s not in HID_HI_DVE:
                    i = af(P_hi[:, s, :], ps[:, s % 4, :], ACT.Gelu, bias=bias)
                i.then_inc(hid_ready, 1)
            for s in range(FC1):
                hidden(0, 0, s, first=True)
            split_xT(3, 1, 6)
            for s in range(FC1, NT):
                hidden(0, 0, s, first=True)
            for s in range(FC1):
                hidden(1, 1, s)
            act.wait_ge(gT_ps, 1)
            for h in range(2):
                j = af(gatesT[:, cols(h)], ps[0:NE, 6 + h, :], ACT.Copy)
            j.then_inc(gT_ready, 1)
            hidden(1, 1, FC1)
            hidden(1, 1, FC1 + 1)
            for h in range(2):
                act.wait_ge(b2_ps, h + 1)
                af(moeT[:, cols(h)], ps[:, 6 + h, :], ACT.Copy).then_inc(moe_init, 1)
            for s in range(FC1 + 2, NT):
                hidden(1, 1, s)
            with act.Fori(0, NE // 2 - 1) as i:
                for buf in range(2):
                    for s in range(NT):
                        hidden(2 * i + 2 + buf, buf, s)

        @block.vector
        def _(dve):
            v, count = nc.vector, [0]

            def link(ins):
                count[0] += 1
                ins.then_inc(dve_done, 1)
                dve.wait_ge(dve_done, count[0])

            def cols(h):
                return slice(h * HALF, (h + 1) * HALF)

            def chunk_stats(h):
                for b in range(h * CH, (h + 1) * CH):
                    i = v.bn_stats(bstat[:, b, :], xs[:, b, :])
                return i

            def layer_norm_stats(h=None):
                b0, b1 = (0, NB) if h is None else (h * CH, (h + 1) * CH)
                for b in range(b0, b1):
                    i = v.bn_aggr(mv[:, b, :], bstat[:, b, :])
                link(i)
                v.tensor_scalar(var_eps[:, b0:b1], mv[:, b0:b1, 1], LN_EPS, None, ALU.add).then_inc(var_ready, 1)

            def half(t, h):
                return t[:, h * CH:(h + 1) * CH, :]

            def layer_norm(k, h=None):
                dve.wait_ge(rstd_ready, k + 1 if h is None else 2 * k + h - 1)
                for b in range(NB) if h is None else range(h * CH, (h + 1) * CH):
                    i = v.tensor_scalar(xn[:, b, :], xs[:, b, :], mv[:, b, 0:1], rstd[:, b:b + 1], ALU.subtract,
                                        ALU.mult)
                    i.then_inc(xn_ready, 1)

            v.memset(ctxT_hi[C:C + 1, :].bitcast(fp32), 1.0)
            v.memset(Bh[0:C, :, D:BW], 0.0)
            v.memset(Bh[C:C + 1, :, 0:D], 0.0)
            v.memset(Bh[C:C + 1, :, D:BW], 1.0)
            for h in range(2):
                dve.wait_ge(ld[f"x{h}"], 16)
                i = chunk_stats(h)
            link(i)
            layer_norm_stats()
            layer_norm(0)
            for h in range(2):
                dve.wait_ge(ctxT_ready, h + 1)
                v.tensor_tensor(ctxT_lo[:, cols(h)], ps[0:C, h, :], ctxT_hi[0:C, cols(h)].bitcast(fp32),
                                ALU.subtract).then_inc(ctxT_lo_ready, 1)

            dve.wait_ge(ld["wf"], 48)
            w3 = wf[:, :, :, :].rearrange("p a n k -> p (a n) k")
            link(v.tensor_reduce(wf_s[:, :], w3, AX.X, ALU.max, apply_absolute_value=True))
            link(v.tensor_scalar(wf_s[:, :], wf_s[:, :], 1.0 / WMAX, SCALE_MIN, ALU.mult, ALU.max))
            link(v.reciprocal(wf_rs[:, :], wf_s[:, :]))

            def per_block(t):
                return t[:, :].rearrange("p (n o) -> p n o", o=1).to_broadcast([P, NWB, BLK])
            link(v.tensor_tensor(w3, w3, per_block(wf_rs), ALU.mult))
            link(v.tensor_scalar(w3, w3, WMAX, -WMAX - 1.0, ALU.min, ALU.max))
            link(v.tensor_scalar(w3, w3, MAGIC, MAGIC, ALU.add, ALU.subtract))
            v.tensor_tensor(w3, w3, per_block(wf_s), ALU.mult).then_inc(wq_ready, 1)

            def norms(i, bank):
                dve.wait_ge(nsq_ps, i + 1)
                v.tensor_copy(nsq[:, i, :], ps[:, bank, 0:NB]).then_inc(nsq_ready, 1)

            def clamp_norms(i):
                dve.wait_ge(rn_pow, i + 1)
                v.tensor_scalar(rn[:, i, :], rn[:, i, :], RNORM_MAX, None, ALU.min).then_inc(rn_ready, 1)
            norms(0, 2)
            norms(1, 7)
            clamp_norms(0)
            clamp_norms(1)
            dve.wait_ge(rn_ready, 2)
            for h in range(2):
                dve.wait_ge(rt_ps, h + 1)
                for j in range(CH):
                    b = h * CH + j
                    i = v.tensor_scalar(cosr[:, b, :], chunks(h)[:, j, :], rn[:, 1, b:b + 1], 1.0 / COS_EPS,
                                        ALU.mult, ALU.min)
            link(i)
            for h in range(2):
                dve.wait_ge(dots_ps, h + 1)
                i = v.tensor_tensor(half(cosr, h), chunks(5 + h), half(cosr, h), ALU.mult)
            i.then_inc(x_added, 1)
            dve.wait_ge(x_added, 1)
            for h in range(2):
                link(v.tensor_tensor(half(xs, h), half(xs, h), half(cosr, h), ALU.add))
                i = chunk_stats(h)
            link(i)

            def global_max(k):
                dve.wait_ge(amT_ps, k + 1)
                link(v.tensor_reduce(qs[:, k, 7:8], ps[:, 7, 0:P], AX.X, ALU.max))

            def quant_scale(k, unit):
                s_q = 1.0 / QMAX if unit is None else qs[:, k, 2:3]
                link(v.tensor_scalar(qs[:, k, 0:1], qs[:, k, 7:8], s_q, SCALE_MIN, ALU.mult, ALU.max))
                if unit is None:
                    return v.reciprocal(qs[:, k, 1:2], qs[:, k, 0:1])
                link(v.reciprocal(qs[:, k, 3:4], qs[:, k, 0:1]))
                return v.tensor_scalar(qs[:, k, 1:2], qs[:, k, 3:4], unit, None, ALU.mult)

            def unit_over_qmax(k, unit):
                return v.tensor_scalar(qs[:, k, 2:3], unit, 1.0 / QMAX, None, ALU.mult)

            def first_quant_step(k, t):
                return v.tensor_scalar(t, t, qs[:, k, 1:2], MAGIC, ALU.mult, ALU.add)

            def second_quant_step(t):
                return v.tensor_scalar(t, t, MAGIC, None, ALU.subtract)

            def part_max(k, c, src):
                return v.tensor_reduce(amax[:, k, c:c + 1], src, AX.X, ALU.max, apply_absolute_value=True)

            def join_max(k):
                v.tensor_reduce(amax[:, k, 3:4], amax[:, k, 0:3], AX.X, ALU.max).then_inc(am_ready, 1)

            layer_norm_stats()
            layer_norm(1)
            dve.wait_ge(xn_ready, 2 * NB)
            v.tensor_reduce(amax[:, 0, 3:4], xn[:, :, :], AX.XY, ALU.max, apply_absolute_value=True
                            ).then_inc(am_ready, 1)
            global_max(0)
            link(quant_scale(0, None))
            for h in range(2):
                link(first_quant_step(0, half(xn, h)))
                second_quant_step(half(xn, h)).then_inc(xq_ready, 1)
            sx = qs[:, 0, 0:1]
            unit_over_qmax(1, sx)
            unit_over_qmax(2, sx)
            for c in range(FC0):
                dve.wait_ge(raw_ready, 2 * (c + 1))
                i = part_max(1, c, g_raw[:, c, :])
            link(i)
            join_max(1)
            global_max(1)
            quant_scale(1, sx).then_inc(inv_ready, 1)
            dve.wait_ge(inv_ready, 1)
            link(first_quant_step(1, g_raw[:, 0, :]))
            second_quant_step(g_raw[:, 0, :]).then_inc(ng_ready, 1)
            for c in range(1, FC0):
                dve.wait_ge(vq_ready, c)
                second_quant_step(g_raw[:, c, :]).then_inc(ng_ready, 1)
            sg = qs[:, 1, 0:1]
            unit_over_qmax(3, sg)
            def clip_sigmoid(c):
                dve.wait_ge(sig_ready, c + 1)
                return v.tensor_scalar(sig[:, c, :], sig[:, c, :], SIG_TOP, MAGIC16, ALU.min, ALU.add)

            def times_sigmoid(c):
                link(clip_sigmoid(c))
                link(v.scalar_tensor_tensor(out=sig[:, c, :], in0=sig[:, c, :], scalar=MAGIC16, in1=g_raw[:, c, :],
                                            op0=ALU.subtract, op1=ALU.mult))
                return part_max(3, c, sig[:, c, :])
            for c in range(FC0):
                dve.wait_ge(raw_ready, 2 * (FC0 + c + 1))
                i = part_max(2, c, u_raw[:, c, :])
                if c == 0:
                    clip_sigmoid(0).then_inc(clip_ready, 1)
            link(i)
            join_max(2)

            times_sigmoid(1)
            global_max(2)
            quant_scale(2, sx).then_inc(inv_ready, 1)
            su = qs[:, 2, 0:1]
            for c in range(2, FC0):
                i = times_sigmoid(c)
            dve.wait_ge(product_ready, 1)
            link(part_max(3, 0, sig[:, 0, :]))
            join_max(3)
            global_max(3)
            quant_scale(3, sg).then_inc(inv_ready, 1)
            dve.wait_ge(inv_ready, 3)
            link(first_quant_step(3, sig[:, FC0 - 1, :]))
            for c in reversed(range(1, FC0)):
                dve.wait_ge(uq_ready, c + 1)
                if c < FC0 - 1:
                    dve.wait_ge(vq_ready, 2 * FC0 + c)
                link(v.scalar_tensor_tensor(out=sig[:, c, :], in0=sig[:, c, :], scalar=MAGIC, in1=u_raw[:, c, :],
                                            op0=ALU.subtract, op1=ALU.mult))
                i = part_max(4, c, sig[:, c, :])
            dve.wait_ge(product_ready, 2)
            link(part_max(4, 0, sig[:, 0, :]))
            join_max(4)
            so_unit = qs[:, 5, 0:1]
            link(v.tensor_scalar(so_unit, qs[:, 3, 0:1], su, None, ALU.mult))
            unit_over_qmax(4, so_unit)
            global_max(4)
            quant_scale(4, so_unit).then_inc(inv_ready, 1)
            dve.wait_ge(inv_ready, 4)
            link(first_quant_step(4, sig[:, :, cols(0)]))
            second_quant_step(sig[:, :, cols(0)]).then_inc(no_ready, 1)
            dve.wait_ge(vq_ready, 3 * FC0 - 1)
            second_quant_step(sig[:, :, cols(1)]).then_inc(no_ready, 1)
            def add_down(h):
                dve.wait_ge(down_ps, h + 1)
                return v.scalar_tensor_tensor(out=half(xs, h), in0=chunks(5 + h), scalar=qs[:, 4, 0:1],
                                              in1=half(xs, h), op0=ALU.mult, op1=ALU.add)

            def split_xT(k, h, bank):
                dve.wait_ge(xT_hi_ready, 2 * (k - 2) + h + 1)
                if k == 3 and h == 1:
                    dve.wait_ge(xT_ready, 6)
                v.tensor_tensor(xnT_lo[:, cols(h)], ps[:, bank, :], xnT_hi[:, cols(h)].bitcast(fp32),
                                ALU.subtract).then_inc(xT_lo_ready, 1)
            link(add_down(0))
            link(chunk_stats(0))
            layer_norm_stats(0)
            add_down(1).then_inc(x_added, 2)
            layer_norm(2, 0)
            dve.wait_ge(x_added, 3)
            link(chunk_stats(1))
            layer_norm_stats(1)
            split_xT(2, 0, 0)
            layer_norm(2, 1)

            def queries_lo(u, f, hb):
                dve.wait_ge(q_hi_ready, u + 1)
                v.tensor_tensor(qT_lo[:, hb, cols(f)], ps[0:C, 6, :], qT_hi[0:C, hb, cols(f)].bitcast(fp32),
                                ALU.subtract).then_inc(q_lo_ready, 1)

            def tile_max(u, n, first=False):
                dve.wait_ge(max_ps, 2 * CH * u + n + 1)
                v.tensor_reduce(tmax[:, n:n + 1], ps[:, FIRST_MAX_BANKS[n % 4] if first else 2 + n % 2, :], AX.X, ALU.max).then_inc(max_read, 1)

            def join_tiles(u, first=False):
                dve.wait_ge(max_read, 2 * CH * (u + 1))
                v.tensor_reduce(minus_max[:, :], tmax[:, :].rearrange("p (q a) -> p q a", a=2), AX.X, ALU.max,
                                negate=True).then_inc(join_ready, 1)
                dve.wait_ge(join_ready, u + 1)
                if not first:
                    dve.wait_ge(z_ps, u)
                v.tensor_tensor(max_diag[:, :].rearrange("p (q k) -> p q k", q=CH),
                                ident[:, :].rearrange("p (o k) -> p o k", o=1).to_broadcast([P, CH, P]),
                                minus_max[:, :].rearrange("p (q o) -> p q o", o=1).to_broadcast([P, CH, P]), ALU.mult
                                ).then_inc(z_ready, 1)

            def split_exp(u, t):
                if t not in HI_DVE and t not in LO_DVE:
                    return
                dve.wait_ge(exp_ready, NB * u + t + 1)
                if t in HI_DVE:
                    v.tensor_copy(P_hi[:, t, :], E[:, t, :]).then_inc(p_hi_dve, 1)
                if t in LO_DVE:
                    v.tensor_tensor(P_lo[:, t, :], E[:, t, :], P_hi[:, t, :].bitcast(fp32),
                                    ALU.subtract).then_inc(p_lo_dve, 1)

            def add_head(u, f):
                dve.wait_ge(y_ps, u + 1)
                y = ps[:, 4 + f, 0:(CH - 1) * BW].rearrange("p (j d) -> p j d", d=BW)
                y_last = ps[:, 6, 0:BW]
                v.reciprocal(rsum[:, f, 0:CH - 1], y[:, :, D])
                v.reciprocal(rsum[:, f, CH - 1:CH], y_last[:, D:BW]).then_inc(rs_ready, 1)
                dve.wait_ge(rs_ready, u + 1)
                for j in range(CH):
                    b = f * CH + j
                    i = v.scalar_tensor_tensor(out=xs[:, b, :], in0=y[:, j, 0:D] if j < CH - 1 else y_last[:, 0:D],
                                               scalar=rsum[:, f, j:j + 1], in1=xs[:, b, :], op0=ALU.mult, op1=ALU.add)
                i.then_inc(y_added, 1)

            def unit(u, f, hb, first=False, n_next=2):
                n_max = 0
                for t in range(NB):
                    for k in range(2):
                        if n_next >= 1 and k < MAX_AT[t]:
                            tile_max(u + 1, n_max)
                            n_max += 1
                            if n_max == 2 * CH:
                                join_tiles(u + 1)
                        if k == 0:
                            split_exp(u, t)
                    if t == 1 and n_next == 2:
                        queries_lo(u + 2, f, 1 - hb)
                    if t == (Y_AT if n_next else LAST_Y_AT) + 1 and not first:
                        add_head(u - 1, 1 - f)
                        if n_next == 0:
                            dve.wait_ge(y_added, u)
                            link(chunk_stats(0))
                            layer_norm_stats(0)
                    if t == NB - 2 and n_next == 0:
                        layer_norm(3, 0)
            queries_lo(0, 0, 0)
            split_xT(2, 1, 1)
            for n in range(2 * CH):
                tile_max(0, n, first=True)
            join_tiles(0, first=True)
            queries_lo(1, 1, 0)
            dve.wait_ge(bout_ps, 1)
            v.tensor_tensor(xs[:, :, :], xs[:, :, :],
                            ps[:, 4, 0:D].rearrange("p (o d) -> p o d", o=1).to_broadcast([P, NB, D]), ALU.add
                            ).then_inc(bout_added, 1)
            unit(0, 0, 0, first=True)
            dve.wait_ge(bout_added, 1)
            unit(1, 1, 0)
            with dve.Fori(0, NH // 2 - 1) as i:
                for k in range(4):
                    unit(4 * i + 2 + k, k % 2, (k // 2 + 1) % 2)
            unit(2 * NH - 2, 0, 1, n_next=1)
            unit(2 * NH - 1, 1, 1, n_next=0)
            split_xT(3, 0, 7)
            add_head(2 * NH - 1, 1)
            dve.wait_ge(y_added, 2 * NH)
            link(chunk_stats(1))
            layer_norm_stats(1)

            def split_hidden(e, s):
                dve.wait_ge(hid_ready, NT * e + s + 1)
                if s in HID_HI_DVE:
                    v.tensor_copy(P_hi[:, s, :], E[:, s, :]).then_inc(hid_hi_dve, 1)
                    dve.wait_ge(hid_hi_dve, len(HID_HI_DVE) * (e - 1) + HID_HI_DVE.index(s) + 1)
                if s in HID_LO_DVE:
                    v.tensor_tensor(P_lo[:, s, :], E[:, s, :], P_hi[:, s, :].bitcast(fp32), ALU.subtract
                                    ).then_inc(hid_lo_dve, 1)

            def first_split_hidden(s):
                dve.wait_ge(hid_ready, s + 1)
                v.tensor_tensor(P_lo[:, s, :], E[:, s, :], P_hi[:, s, :].bitcast(fp32), ALU.subtract
                                ).then_inc(first_lo_dve, 1)
            layer_norm(3, 1)
            split_xT(3, 1, 6)
            dve.wait_ge(logit_ps, 1)
            link(v.tensor_tensor(logit[:, :, :], ps[:, 7, 0:NB * NE].rearrange("p (b e) -> p b e", e=NE),
                                 gb[:, :].rearrange("p (o e) -> p o e", o=1).to_broadcast([P, NB, NE]), ALU.add))
            for b in range(NB):
                i = v.max(top[:, b, :], logit[:, b, :])
            link(i)
            for b in range(NB):
                i = v.max_index(topi[:, b, :], top[:, b, :], logit[:, b, :])
            v.tensor_tensor(dtop[:, :], top[:, :, 1], top[:, :, 0], ALU.subtract).then_inc(dtop_ready, 1)
            link(v.tensor_copy(iota_f[:, :], iota_i[:, :]))
            link(v.tensor_copy(topf[:, :, :], topi[:, :, :]))
            for s in range(FC1, FC1 + 2):
                first_split_hidden(s)
            dve.wait_ge(etop_ready, 1)
            link(v.tensor_scalar(g01[:, 1, :], etop[:, :], 1.0, None, ALU.add))
            link(v.reciprocal(g01[:, 0, :], g01[:, 1, :]))
            link(v.tensor_tensor(g01[:, 1, :], etop[:, :], g01[:, 0, :], ALU.mult))

            def along_e(a):
                return a.rearrange("p (b o) -> p b o", o=1).to_broadcast([P, NB, NE])
            iota_b = iota_f[:, :].rearrange("p (o e) -> p o e", o=1).to_broadcast([P, NB, NE])
            for j, g in ((0, gate_a), (1, gate_b)):
                link(v.tensor_tensor(g[:, :, :], iota_b, topf[:, :, j:j + 1].to_broadcast([P, NB, NE]), ALU.is_equal))
                link(v.tensor_tensor(g[:, :, :], g[:, :, :], along_e(g01[:, j, :]), ALU.mult))
            v.tensor_tensor(gates[:, :, :], gate_a[:, :, :], gate_b[:, :, :], ALU.add).then_inc(gates_ready, 1)

            for s in range(FC1 + 2, NT):
                first_split_hidden(s)

            def weigh(e, buf, hf, k, first=False):
                dve.wait_ge(ey_ps, NT * e + FC1 * (hf + 1))
                if hf == 0:
                    dve.wait_ge(gate_row[buf], 16 * k)
                if not first:
                    dve.wait_ge(moe_added, 2 * (e - 1) + hf + 1)
                v.tensor_tensor(term[:, cols(hf)], ps[:, 4 + 2 * buf + hf, :], gate_rows[:, buf, cols(hf)], ALU.mult
                                ).then_inc(term_ready, 1)

            def w1_high(e, buf):
                dve.wait_ge(hid_ready, NT * (e - 1))
                v.tensor_copy(b1cur[:, buf, :], b1T[:, bass.ds(FC1 * e, FC1)])
                v.tensor_copy(w1_hi[:, buf, :], w1[:, bass.ds(e, 1), :].rearrange("p o f -> p (o f)")
                              ).then_inc(w1_hi_ready, 1)

            def w2_high(e, buf):
                dve.wait_ge(ey_ps, NT * (e - 1))
                v.tensor_copy(w2_hi[:, buf, :], w2[:, bass.ds(e, 1), :, :].rearrange("p o c d -> p (o c d)")
                              ).then_inc(w2_hi_ready, 1)

            def expert(e, buf, k, last=False):
                if not last:
                    w1_high(e + 1, 1 - buf)
                for s in range(NT):
                    split_hidden(e, s)
                    if s == 0:
                        weigh(e - 1, 1 - buf, 0, k + buf)
                    if s == FC1:
                        weigh(e - 1, 1 - buf, 1, None)
                        if not last:
                            w2_high(e + 1, 1 - buf)
            w1_high(2, 0)
            for s in range(FC1 + 1):
                split_hidden(1, s)
            for s in range(FC1 + 1, NT):
                split_hidden(1, s)
            weigh(0, 0, 0, 1, first=True)
            weigh(0, 0, 1, None, first=True)
            w2_high(2, 0)
            with dve.Fori(0, NE // 2 - 2) as i:
                expert(2 * i + 2, 0, i + 1)
                expert(2 * i + 3, 1, i + 1)
            expert(NE - 2, 0, NE // 2 - 1)
            expert(NE - 1, 1, NE // 2 - 1, last=True)
            weigh(NE - 1, 1, 0, NE // 2)
            weigh(NE - 1, 1, 1, None)
            dve.wait_ge(term_ready, 2 * NE)
            dve.wait_ge(moe_added, 2 * NE - 1)
            v.tensor_tensor(moeT[:, cols(1)], term[:, cols(1)], moeT[:, cols(1)], ALU.add).then_inc(moe_added, 1)
            for h in range(2):
                dve.wait_ge(moe_ps, h + 1)
                v.tensor_tensor(half(xs, h), chunks(h), half(xs, h), ALU.add).then_inc(out_ready, 1)


_INS = ['x', 'ctx_768', 'L0_xattn_Wv', 'L0_xattn_bv', 'L0_xattn_Wt', 'L0_xattn_bt', 'L0_ffn_w_gate', 'L0_ffn_w_up',
        'L0_ffn_w_down', 'L1_xattn_Wq', 'L1_xattn_Wk', 'L1_xattn_Wv', 'L1_xattn_Wout', 'L1_xattn_bout',
        'L1_ffn_gate_w', 'L1_ffn_gate_b', 'L1_ffn_w1', 'L1_ffn_b1', 'L1_ffn_w2', 'L1_ffn_b2']
_OUTS = [((8, 128, 128), 'float32')]


def kernel(**inputs):
    import numpy as _np
    import concourse.bacc as _bacc
    from concourse import mybir as _mybir
    from concourse.bass_utils import run_bass_kernel_spmd as _run

    nc = _bacc.Bacc("TRN2", target_bir_lowering=False, num_devices=1)
    arrays, args = {}, []
    for name in _INS:
        a = _np.ascontiguousarray(inputs[name])
        arrays[f"in_{name}_dram"] = a
        args.append(nc.dram_tensor(f"in_{name}_dram", a.shape, _mybir.dt.from_np(a.dtype), kind="ExternalInput").ap())
    for i, (shape, dtype) in enumerate(_OUTS):
        dt = _mybir.dt.from_np(_np.dtype(dtype))
        args.append(nc.dram_tensor(f"out_{i}_dram", shape, dt, kind="ExternalOutput").ap())
    xattn_ffn_two_layers(nc, *args)
    r = _run(nc, [arrays], core_ids=[0])
    got = tuple(r.results[0][f"out_{i}_dram"] for i in range(len(_OUTS)))
    return got[0]
```
